# Optimizing a Trainium2 kernel written in Bass

```python
import numpy as np
import jax
import jax.numpy as jnp

def _softmax(x, axis=-1):
    return jax.nn.softmax(x, axis=axis)

def _gelu(x):
    return jax.nn.gelu(x, approximate=True)

def _silu(x):
    return jax.nn.silu(x)

def _sigmoid(x):
    return jax.nn.sigmoid(x)

def _layernorm(x, axis=-1, eps=1e-05):
    m = jnp.mean(x, axis=axis, keepdims=True)
    v = jnp.var(x, axis=axis, keepdims=True)
    return (x - m) / jnp.sqrt(v + eps)

def _scatter_add(tgt, idx, src, axis=0):
    return tgt.at[idx].add(src)

def _segment_sum(src, seg, n):
    return jax.ops.segment_sum(src, seg, n)
kernel_name = 'mk_metaformer_d1_conv_nchw512_r4_1ee51f'

def setup_inputs(seed: int=0):
    np.random.seed(seed)
    _w = jnp.asarray

    def _rec_inputs():
        import jax
        import jax.numpy as jnp
        _gk = jax.random.key(seed)
        x = -0.000125 + 0.9999 * jax.random.normal(jax.random.fold_in(_gk, 1), (16, 128, 16, 16), jnp.float32)
        return x
    x = _rec_inputs()

    def _L0_conv_setup():
        import jax, jax.numpy as jnp
        import numpy as np
        from jax import lax
        DIM = 128
        MED = 2 * DIM
        NF = 4
        SIZE = 16
        FS = SIZE // 2 + 1
        HR = int(0.5 * DIM)
        HS = int(0.5 * DIM)
        B = 16

        def _conv1x1(x, w, b):
            return jnp.einsum('bchw,oc->bohw', x, w[:, :, 0, 0]) + b[None, :, None, None]

        def _conv3x3(x, w, b):
            return lax.conv_general_dilated(x, w, (1, 1), 'SAME') + b[None, :, None, None]
        key = jax.random.key(seed)
        ks = jax.random.split(key, 12)
        n = lambda k, shape, s=0.02: jax.random.normal(k, shape, jnp.float32) * s
        return dict(x=jax.random.normal(ks[0], (B, DIM, SIZE, SIZE), jnp.float32), w_pw1=n(ks[1], (MED, DIM)), w_pw2=n(ks[2], (DIM, MED)), star_scale=jnp.ones((1,), jnp.float32), star_bias=jnp.zeros((1,), jnp.float32), rw_fc1_w=n(ks[3], (HR, DIM, 1, 1)), rw_fc1_b=jnp.zeros((HR,), jnp.float32), rw_conv_w=n(ks[4], (HR, HR, 1, 1)), rw_conv_b=jnp.zeros((HR,), jnp.float32), rw_fc2_w=n(ks[5], (NF * MED, HR, 1, 1)), rw_fc2_b=jnp.zeros((NF * MED,), jnp.float32), sp_fc1_w=n(ks[6], (HS, DIM, 3, 3)), sp_fc1_b=jnp.zeros((HS,), jnp.float32), sp_fc2_w=n(ks[7], (NF * MED, HS, 3, 3)), sp_fc2_b=jnp.zeros((NF * MED,), jnp.float32), complex_weights=n(ks[8], (SIZE, FS, NF, 2), 0.02), spatial_weights=n(ks[9], (SIZE, SIZE, NF), 0.03))
    _L0_conv_all = _L0_conv_setup()
    _L0_conv_in = {k: v for k, v in _L0_conv_all.items() if k in ('w_pw1', 'w_pw2', 'star_scale', 'star_bias', 'rw_fc1_w', 'rw_fc1_b', 'rw_conv_w', 'rw_conv_b', 'rw_fc2_w', 'rw_fc2_b', 'sp_fc1_w', 'sp_fc1_b', 'sp_fc2_w', 'sp_fc2_b', 'complex_weights', 'spatial_weights')}
    del _L0_conv_all

    def _L0_ffn_setup():
        import jax, jax.numpy as jnp
        import numpy as np
        NUM_EXPERTS = 8
        TOP_K = 2
        key = jax.random.key(seed)
        ks = jax.random.split(key, 5)
        B, T, D, H, E = (8, 1024, 128, 384, NUM_EXPERTS)
        scale = 0.02
        x = jax.random.normal(ks[0], (B, T, D), dtype=jnp.float32)
        gate_w = jax.random.normal(ks[1], (E, D), dtype=jnp.float32) * scale
        w1 = jax.random.normal(ks[2], (E, H, D), dtype=jnp.float32) * scale
        w3 = jax.random.normal(ks[3], (E, H, D), dtype=jnp.float32) * scale
        w2 = jax.random.normal(ks[4], (E, D, H), dtype=jnp.float32) * scale
        return {'x': x, 'gate_w': gate_w, 'w1': w1, 'w3': w3, 'w2': w2}
    _L0_ffn_all = _L0_ffn_setup()
    _L0_ffn_in = {k: v for k, v in _L0_ffn_all.items() if k in ('gate_w', 'w1', 'w3', 'w2')}
    del _L0_ffn_all
    return {'x': x, 'L0_conv_w_pw1': _L0_conv_in['w_pw1'], 'L0_conv_w_pw2': _L0_conv_in['w_pw2'], 'L0_conv_star_scale': _L0_conv_in['star_scale'], 'L0_conv_star_bias': _L0_conv_in['star_bias'], 'L0_conv_rw_fc1_w': _L0_conv_in['rw_fc1_w'], 'L0_conv_rw_fc1_b': _L0_conv_in['rw_fc1_b'], 'L0_conv_rw_conv_w': _L0_conv_in['rw_conv_w'], 'L0_conv_rw_conv_b': _L0_conv_in['rw_conv_b'], 'L0_conv_rw_fc2_w': _L0_conv_in['rw_fc2_w'], 'L0_conv_rw_fc2_b': _L0_conv_in['rw_fc2_b'], 'L0_conv_sp_fc1_w': _L0_conv_in['sp_fc1_w'], 'L0_conv_sp_fc1_b': _L0_conv_in['sp_fc1_b'], 'L0_conv_sp_fc2_w': _L0_conv_in['sp_fc2_w'], 'L0_conv_sp_fc2_b': _L0_conv_in['sp_fc2_b'], 'L0_conv_complex_weights': _L0_conv_in['complex_weights'], 'L0_conv_spatial_weights': _L0_conv_in['spatial_weights'], 'L0_ffn_gate_w': _L0_ffn_in['gate_w'], 'L0_ffn_w1': _L0_ffn_in['w1'], 'L0_ffn_w3': _L0_ffn_in['w3'], 'L0_ffn_w2': _L0_ffn_in['w2']}

def reference(x, L0_conv_w_pw1, L0_conv_w_pw2, L0_conv_star_scale, L0_conv_star_bias, L0_conv_rw_fc1_w, L0_conv_rw_fc1_b, L0_conv_rw_conv_w, L0_conv_rw_conv_b, L0_conv_rw_fc2_w, L0_conv_rw_fc2_b, L0_conv_sp_fc1_w, L0_conv_sp_fc1_b, L0_conv_sp_fc2_w, L0_conv_sp_fc2_b, L0_conv_complex_weights, L0_conv_spatial_weights, L0_ffn_gate_w, L0_ffn_w1, L0_ffn_w3, L0_ffn_w2):
    import jax
    import jax.numpy as jnp

    def _L0_conv_ref(x, w_pw1, w_pw2, star_scale, star_bias, rw_fc1_w, rw_fc1_b, rw_conv_w, rw_conv_b, rw_fc2_w, rw_fc2_b, sp_fc1_w, sp_fc1_b, sp_fc2_w, sp_fc2_b, complex_weights, spatial_weights):
        import jax, jax.numpy as jnp
        import numpy as np
        from jax import lax
        DIM = 128
        MED = 2 * DIM
        NF = 4
        SIZE = 16
        FS = SIZE // 2 + 1
        HR = int(0.5 * DIM)
        HS = int(0.5 * DIM)
        B = 16

        def _conv1x1(x, w, b):
            return jnp.einsum('bchw,oc->bohw', x, w[:, :, 0, 0]) + b[None, :, None, None]

        def _conv3x3(x, w, b):
            return lax.conv_general_dilated(x, w, (1, 1), 'SAME') + b[None, :, None, None]
        Bn, _, H, W = x.shape
        r = jax.nn.relu(_conv1x1(x, rw_fc1_w, rw_fc1_b))
        r = jax.nn.relu(_conv1x1(r, rw_conv_w, rw_conv_b))
        r = _conv1x1(r, rw_fc2_w, rw_fc2_b)
        routeing = jax.nn.softmax(r.mean(axis=(2, 3)).reshape(Bn, NF, MED), axis=1)
        s = jax.nn.relu(_conv3x3(x, sp_fc1_w, sp_fc1_b))
        s = _conv3x3(s, sp_fc2_w, sp_fc2_b)
        spatial_routeing = jax.nn.softmax(s.mean(axis=(2, 3)).reshape(Bn, NF, MED), axis=1)
        xc = jnp.transpose(x, (0, 2, 3, 1))
        xp = jnp.einsum('bhwc,mc->bhwm', xc, w_pw1)
        xp = star_scale * jnp.square(jax.nn.relu(xp)) + star_bias
        xf = jnp.fft.rfft2(xp, axes=(1, 2), norm='ortho')
        cw = lax.complex(complex_weights[..., 0], complex_weights[..., 1])
        weight = jnp.einsum('bfc,hwf->bhwc', routeing.astype(cw.dtype), cw)
        spatial_weight = jnp.einsum('bfc,hwf->bhwc', spatial_routeing, spatial_weights)
        xs = jnp.fft.irfft2(xf * weight, s=(H, W), axes=(1, 2), norm='ortho')
        out = xp * spatial_weight + xs
        out = jnp.einsum('bhwm,dm->bhwd', out, w_pw2)
        return jnp.transpose(out, (0, 3, 1, 2))

    def _L0_ffn_ref(x, gate_w, w1, w3, w2):
        import jax, jax.numpy as jnp
        import numpy as np
        NUM_EXPERTS = 8
        TOP_K = 2
        B, T, D = x.shape
        E = gate_w.shape[0]
        xf = x.reshape(-1, D)
        N = xf.shape[0]
        gate_logits = xf @ gate_w.T
        weights, indices = jax.lax.top_k(gate_logits, TOP_K)
        weights = jax.nn.softmax(weights, axis=-1)
        combine = jnp.zeros((N, E), dtype=xf.dtype).at[jnp.arange(N)[:, None], indices].add(weights)
        out = jnp.zeros_like(xf)
        for e in range(E):
            h = jax.nn.silu(xf @ w1[e].T) * (xf @ w3[e].T)
            y = h @ w2[e].T
            out = out + combine[:, e:e + 1] * y
        return out.reshape(B, T, D)

    def _gn(v, G=32, eps=1e-05):
        B_, C_, H_, W_ = v.shape
        g = v.reshape(B_, G, C_ // G, H_, W_)
        m = jnp.mean(g, axis=(2, 3, 4), keepdims=True)
        s = jnp.var(g, axis=(2, 3, 4), keepdims=True)
        return ((g - m) / jnp.sqrt(s + eps)).reshape(v.shape)

    def _ln_c(v, eps=1e-06):
        m = jnp.mean(v, axis=1, keepdims=True)
        s = jnp.var(v, axis=1, keepdims=True)
        return (v - m) / jnp.sqrt(s + eps)

    def _ln_t(v, eps=1e-05):
        m = jnp.mean(v, axis=-1, keepdims=True)
        s = jnp.var(v, axis=-1, keepdims=True)
        return (v - m) / jnp.sqrt(s + eps)

    def _to_tokens(v):
        B_, C_, H_, W_ = v.shape
        return v.reshape(B_, C_, H_ * W_).transpose(0, 2, 1)

    def _from_tokens(t, like):
        B_, C_, H_, W_ = like.shape
        return t.transpose(0, 2, 1).reshape(B_, C_, H_, W_)
    x = x + _L0_conv_ref(_ln_c(x), L0_conv_w_pw1, L0_conv_w_pw2, L0_conv_star_scale, L0_conv_star_bias, L0_conv_rw_fc1_w, L0_conv_rw_fc1_b, L0_conv_rw_conv_w, L0_conv_rw_conv_b, L0_conv_rw_fc2_w, L0_conv_rw_fc2_b, L0_conv_sp_fc1_w, L0_conv_sp_fc1_b, L0_conv_sp_fc2_w, L0_conv_sp_fc2_b, L0_conv_complex_weights, L0_conv_spatial_weights)
    t = _to_tokens(x)
    t = t + _L0_ffn_ref(_ln_t(t), L0_ffn_gate_w, L0_ffn_w1, L0_ffn_w3, L0_ffn_w2)
    x = _from_tokens(t, x)
    return x

_drawn_inputs = setup_inputs


def setup_inputs(seed=0):
    import zlib

    import numpy as np

    out = dict(_drawn_inputs(seed))
    spreads = {'L0_conv_rw_fc1_b': (0.0, 0.8),
     'L0_conv_rw_conv_b': (0.0, 0.8),
     'L0_conv_rw_fc2_b': (0.0, 0.8),
     'L0_conv_sp_fc1_b': (0.0, 0.8),
     'L0_conv_sp_fc2_b': (0.0, 0.8)}
    factors = {'L0_conv_w_pw1': 8.0,
     'L0_conv_w_pw2': 8.0,
     'L0_conv_rw_fc1_w': 8.0,
     'L0_conv_rw_conv_w': 8.0,
     'L0_conv_rw_fc2_w': 8.0,
     'L0_conv_sp_fc1_w': 8.0,
     'L0_conv_sp_fc2_w': 8.0,
     'L0_conv_complex_weights': 8.0,
     'L0_conv_spatial_weights': 8.0,
     'L0_ffn_gate_w': 8.0,
     'L0_ffn_w1': 7.902,
     'L0_ffn_w3': 7.841,
     'L0_ffn_w2': 7.846}
    for name, (base, spread) in spreads.items():
        noise = np.random.default_rng([zlib.crc32(name.encode()), seed]).standard_normal(out[name].shape)
        drawn = base * np.exp(spread * noise) if base else spread * noise
        out[name] = jnp.asarray(drawn.astype(out[name].dtype))
    for name, factor in factors.items():
        out[name] = (out[name] * factor).astype(out[name].dtype)
    return out
```

```python
from contextlib import ExitStack

import numpy as np

import concourse.bass as bass
from concourse import mybir

ALU = mybir.AluOpType
ACT = mybir.ActivationFunctionType
AX = mybir.AxisListType
F32 = mybir.dt.float32
F32R = mybir.dt.float32r
I32 = mybir.dt.int32
U32 = mybir.dt.uint32
ds = bass.ds

P = 128
DIM = 128
MED = 2 * DIM
NF = 4
SIZE = 16
FS = SIZE // 2 + 1
PIX = SIZE * SIZE
BATCH = 16
PAIRS = BATCH // 2
HALF = 64
TAPS = 9
PAD = SIZE + 2
NTOK = BATCH * PIX
TILES = NTOK // P
E = 8
HID = 384
HC = HID // P
SLOT_TILES = 2 * TILES + E
LN_C_EPS = 1e-6
LN_T_EPS = 1e-5


def fourier_tables():
    h = np.arange(8)[:, None]
    w = np.arange(16)[None, :]
    forward = np.zeros((2, P, P), np.float64)
    inverse = np.zeros((2, P, P), np.float64)
    sel = np.zeros((2, 2, SIZE * FS, 2, P), np.float64)

    def at(ky, kx):
        return (ky % SIZE) * FS + kx

    for par in range(2):
        kys = range(par, SIZE, 2)
        full = [(ky, kx) for ky in kys for kx in range(1, 8)]
        full += [(ky, kx) for ky in kys if 0 < ky < 8 for kx in (0, 8)]
        real = [(ky, kx) for ky in kys if ky in (0, 8) for kx in (0, 8)]
        assert 2 * len(full) + len(real) == P
        for n, (ky, kx) in enumerate(full):
            th = (2 * np.pi / SIZE) * (ky * h + kx * w)
            re, im = n, n + 64
            forward[par, :, re] = np.cos(th).ravel()
            forward[par, :, im] = -np.sin(th).ravel()
            inverse[par, re] = 2 * np.cos(th).ravel() / PIX
            inverse[par, im] = -2 * np.sin(th).ravel() / PIX
            if kx in (0, 8):
                terms = [(at(ky, kx), 0.5, 0.5), (at(-ky, kx), 0.5, -0.5)]
            else:
                terms = [(at(ky, kx), 1.0, 1.0)]
            for b, cr, ci in terms:
                sel[0, 0, b, par, re] += cr
                sel[0, 0, b, par, im] += cr
                sel[1, 1, b, par, re] -= ci
                sel[1, 1, b, par, im] += ci
        for n, (ky, kx) in enumerate(real):
            row = (len(full) + n) if n < 2 else (64 + len(full) + n - 2)
            cs = np.cos((2 * np.pi / SIZE) * (ky * h + kx * w)).ravel()
            forward[par, :, row] = cs
            inverse[par, row] = cs / PIX
            sel[0, 0, at(ky, kx), par, row] = 1.0
    sel = sel.transpose(2, 0, 1, 3, 4).reshape(SIZE * FS, 2, 4, P)
    return (forward.transpose(1, 0, 2).astype(np.float32), inverse.transpose(1, 0, 2).astype(np.float32),
            np.ascontiguousarray(sel.astype(np.float32)))


def wait_done(eng, sem, count):
    if isinstance(count, int) and count <= 0:
        return
    eng.wait_ge(sem, count)


def wait_apart(eng, sem, count):
    if not isinstance(count, int):
        count = eng.to_reg(count)
        eng.wait_ge(sem, 1)
    wait_done(eng, sem, count)


def pair_loop(eng, step):
    step(0, 0)
    step(1, 1)
    with eng.Fori(1, PAIRS // 2 - 1) as n:
        for u in range(2):
            step(n * 2 + u, u)
    step(PAIRS - 2, 0)
    step(PAIRS - 1, 1)


def tile_loop(eng, step, width):
    for b in range(width):
        step(b, b)
    with eng.Fori(1, SLOT_TILES // width - 1) as n:
        for b in range(width):
            step(n * width + b, b)
    for b in range(width):
        step(SLOT_TILES - width + b, b)


def first(i):
    return isinstance(i, int) and i == 0


def last(i, n):
    return isinstance(i, int) and i == n - 1


def flat(ap):
    return ap.rearrange("p a n -> p (a n)")


def metaformer(nc, io):
    with ExitStack() as ctx:
        def sb(name, shape, dt=F32):
            return ctx.enter_context(nc.sbuf_tensor(name, shape, dt))

        tn_dram = nc.dram_tensor("tn_dram", (NTOK, DIM), F32).ap()
        y_dram = nc.dram_tensor("y_dram", (2 * NTOK + SLOT_TILES * P, DIM), F32).ap()

        ident = sb("ident", [P, P])
        fwd = sb("fwd", [P, 2, P])
        inv = sb("inv", [P, 2, P])
        sp1 = sb("sp1", [P, TAPS, HALF])
        rw1 = sb("rw1", [P, HALF])
        rwc = sb("rwc", [P, P])
        sp1_b = sb("sp1_b", [P, 1])
        rw1_b = sb("rw1_b", [P, 1])
        rwc_b = sb("rwc_b", [P, 1])
        route_b = sb("route_b", [P, 2 * NF * 2])
        wp1 = sb("wp1", [P, MED])
        wp2 = sb("wp2", [P, 2, DIM])
        star_s = sb("star_s", [P, 1])
        star_b = sb("star_b", [P, 1])
        gate = sb("gate", [P, P])
        cw_a = sb("cw_a", [P, NF, 2])
        cw_b = sb("cw_b", [SIZE * FS - P, NF, 2])
        coef = sb("coef", [P, 6, P], F32R)
        coef_hl = sb("coef_hl", [NF, 2, 4 * P + PIX], F32R)
        sw_rows = sb("sw_rows", [NF, PIX])
        mhalf = sb("mhalf", [P, 4])
        var_eps = sb("var_eps", [P, 2, 4])
        tri = sb("tri", [P, P])
        ones = sb("ones", [P, P])
        T = sb("T", [P, TILES, DIM])
        mix = sb("mix", [P, 2, TILES])
        idx_gather = sb("idx_gather", [P, SLOT_TILES], U32)
        idx_scatter = sb("idx_scatter", [P, SLOT_TILES], U32)
        tile_expert = sb("tile_expert", [1, SLOT_TILES], I32)
        logits = sb("logits", [P, TILES, E])
        st6 = sb("st6", [P, 2, 4, 6])
        mv = sb("mv", [P, 2, 4, 2])
        rstd = sb("rstd", [P, 2, 4])
        xn = sb("xn", [P, 2, 4, DIM])
        xp = sb("xp", [P, 2, 2, PAD, PAD])
        xc = sb("xc", [P, 2, 512])
        s_all = sb("s_all", [P, PAIRS, SIZE, SIZE])
        r1 = sb("r1", [P, PIX])
        r2 = sb("r2", [P, PIX])
        rsum = sb("rsum", [P, PAIRS])
        rows = sb("rows", [P, 3, PAIRS, SIZE])
        tap_sum = sb("tap_sum", [P, 3, 3, PAIRS])
        tap_k = sb("tap_k", [P, 5, P])
        rw_k = sb("rw_k", [P, P])
        lg = sb("lg", [P, 2, NF, 2, BATCH])
        lmax = sb("lmax", [P, 2, 32])
        lsum = sb("lsum", [P, 2, 32])
        r_hl = sb("r_hl", [P, 2, 2, P], F32R)
        RS = sb("RS", [P, 2, 2, PAIRS, P], F32R)
        q_i32 = sb("q_i32", [P, 2 * TILES], I32)
        q_i32b = sb("q_i32b", [P, 2 * TILES], I32)
        q_e32 = sb("q_e32", [P, E], I32)
        star = sb("star", [P, 2, PAIRS, 512])
        spec = sb("spec", [P, 2, PAIRS, 512])
        shared = sb("shared", [P, 7680])
        buf = sb("buf", [P, 8, 512])

        relu_x, sq_x = buf[:, 0:2, :], buf[:, 2:4, :]
        fold = [[buf[:, 4 + 2 * u + e, :] for e in range(2)] for u in range(2)]
        vt_c = [[buf[:, 2 * u + m, :] for m in range(2)] for u in range(2)]
        tnt = [buf[:, 4, :], buf[:, 5, :]]

        sp2 = shared[:, 0:5 * NF * MED].rearrange("p (t n) -> p t n", t=5)
        rw2 = sb("rw2", [P, NF * MED])
        sel = s_all[:, 0:4].rearrange("p (a b) c d -> p a (b c d)", a=2)
        sel_b = s_all[0:SIZE * FS - P, 4:8].rearrange("p (a b) c d -> p a (b c d)", a=2)

        def area(tensor, first_col):
            at = [first_col]

            def take(n):
                a = tensor[:, at[0]:at[0] + n]
                at[0] += n
                assert at[0] <= tensor.shape[1]
                return a
            return take

        vb = area(shared[:, :], 0)
        sw_c, u_c, prod, cross, y_c, even_c, v_c = ([vb(512), vb(512)] for _ in range(7))
        star_area = star[:].rearrange("p a b n -> p (a b n)")
        spec_area = spec[:].rearrange("p a b n -> p (a b n)")
        st = area(star_area, 0)
        w1s = st(E * HID)
        w3s = st(E * HID)
        oh_s = [st(P) for _ in range(4)]
        oh_j = [st(P) for _ in range(4)]
        q_one, q_tot = st(E * TILES), st(E * TILES)
        q = area(spec_area, 0)
        w2s = q(HC * E * DIM).rearrange("p (c n) -> p c n", c=HC)
        q_rev, q_eq, q_val, q_l2, q_cnt, q_incl, q_slot, q_sel = (q(TILES * E) for _ in range(8))
        q_oh = [q(TILES * E), q(TILES * E)]
        q_m = [q(TILES), q(TILES)]
        q_c, q_diff, q_exp, q_den = (q(TILES) for _ in range(4))
        q_cpad, q_pend, q_base, q_tmp = (q(E) for _ in range(4))
        q_pos, q_low, q_high, q_id1 = (q(2 * TILES) for _ in range(4))
        q_trash, q_v, q_inv = (q(SLOT_TILES) for _ in range(3))
        q_row = q(P)
        q_jtok, q_jcmp = q(E * SLOT_TILES), q(E * SLOT_TILES)
        ff = area(shared[:, :], 0)
        xg, yo = ([ff(P) for _ in range(4)] for _ in range(2))
        xgt = [ff(P), ff(P)]
        silu, hid, hidt = ([ff(HID), ff(HID)] for _ in range(3))
        ya, yb = ([ff(512) for _ in range(4)] for _ in range(2))
        idx_g = [sb(f"idx_g{u}", [P, 4], U32) for u in range(2)]
        idx_s = [sb(f"idx_s{u}", [P, 4], U32) for u in range(2)]

        bank = [ctx.enter_context(nc.psum_tensor(f"bank{n}", [P, 512], F32)) for n in range(8)]
        ps_tr, ps_r, ps_pw, ps_x, ps_conv = bank[0], bank[1], bank[2:4], bank[4:6], bank[6:8]
        ps_w, ps_i, ps_v, ps_y = bank[0:3], bank[3:5], bank[5:7], bank[7]
        ps_tot, ps_rank, ps_idx = bank[0], bank[1], bank[2]
        p_x, p_y, p_h1, p_h3, p_ht = bank[0], bank[1], bank[2:4], bank[4:6], bank[6:8]

        S = {n: ctx.enter_context(nc.semaphore(n)) for n in (
            "consts_in tab_in x_in0 x_in1 x_in2 x_in3 route_in ffn_in w2_in pad_zero coef_zero mhalf_set coef_ps "
            "coef_hi coef_lo coef_in a_stats a_aggr a_eps a_rstd a_norm a_tr a_xc a_xp a_pw a_conv a_rw1 a_relu_s "
            "a_relu_r a_rw2 a_rsum a_rows a_relu a_sq a_star a_fold a_dft a_spec r_cols r_full r_taps r_mm "
            "r_log r_max r_sub r_exp r_sum r_rec r_norm r_tr r_hi r_lo r_rows b_w b_sw b_p b_cross b_u b_y "
            "b_inv b_even b_v b_vt b_vts b_w2 b_t b_stats b_aggr b_eps b_rstd b_norm b_tn0 b_tn1 b_tr b_tnt "
            "b_gate b_logit q_iota q_tri q_dve q_ready q_exp_done q_count q_ranks q_oh_ready q_oh_used q_idx_done "
            "q_tables g_idx s_idx g_x0 g_x1 g_x2 g_x3 f_tr f_xt f_h f_silu f_act f_ht f_hts f_y f_ys y_out0 y_out1 "
            "y_out2 y_out3 c_in0 c_in1 c_in2 c_in3 rs_zero k_zero w_zero r_cat c_sum c_done out_sent").split()}

        def star_at(j, i):
            return flat(star[:, j, ds(i, 1), :])

        def spec_at(lo, hi, e, i):
            return flat(spec[lo:hi, e, ds(i, 1), :])

        def tokens(i):
            return T[:, ds(i * 4, 4), :]

        block = ctx.enter_context(nc.Block())

        @block.sync
        def _(sp):
            x_tiles = io["x"].rearrange("(t p) c -> p t c", p=P)
            for c in range(4):
                sp.dma_start(T[:, 8 * c:8 * c + 8, :], x_tiles[:, 8 * c:8 * c + 8, :]).then_inc(S[f"x_in{c}"], 16)
                if c == 0:
                    for dst, name in ((ident, "ident"), (wp1, "wp1"), (sp1, "sp1"), (rw1, "rw1"), (fwd, "fwd")):
                        sp.dma_start(dst[:], io[name]).then_inc(S["consts_in"], 16)
                    for g in range(2):
                        for dst, name in ((sp1_b, "sp1_b"), (rw1_b, "rw1_b"), (rwc_b, "rwc_b")):
                            sp.dma_start(dst[HALF * g:HALF * g + HALF], io[name]).then_inc(S["consts_in"], 16)
                    sp.wait_ge(S["w_zero"], 3)
                    for g in range(2):
                        sp.dma_start(rwc[HALF * g:HALF * g + HALF, HALF * g:HALF * g + HALF], io["rwc"])\
                            .then_inc(S["consts_in"], 16)
                    for dst, name in ((star_s, "star_s"), (star_b, "star_b")):
                        sp.dma_start(dst[:, :], io[name].partition_broadcast(P)).then_inc(S["consts_in"], 16)
            for dst, name in ((inv, "inv"), (wp2, "wp2"), (route_b, "route_b"),
                              (sw_rows, "sw_rows"), (cw_a, "cw_a"), (cw_b, "cw_b")):
                sp.dma_start(dst[:], io[name]).then_inc(S["tab_in"], 16)
            sp.dma_start(gate[:, 0:E], io["gate"]).then_inc(S["tab_in"], 16)
            sp.dma_start(sel, io["sel_a"]).then_inc(S["tab_in"], 16)
            sp.dma_start(sel_b, io["sel_b"]).then_inc(S["tab_in"], 16)
            sp.dma_start(sp2[0:HALF, 0:5], io["sp2_even"]).then_inc(S["route_in"], 16)
            sp.dma_start(sp2[HALF:P, 0:4], io["sp2_odd"]).then_inc(S["route_in"], 16)
            for g in range(2):
                sp.dma_start(rw2[HALF * g:HALF * g + HALF], io["rw2"]).then_inc(S["route_in"], 16)
            sp.wait_ge(S["coef_zero"], 1)
            sp.wait_ge(S["coef_hi"], 2)
            sp.wait_ge(S["coef_lo"], 2)
            for r in range(4):
                sp.dma_start(coef[4 * r:4 * r + 4, 0:4, :].bitcast(F32), coef_hl[:, r // 2, 0:4 * P].rearrange(
                    "f (c k) -> f c k", c=4).bitcast(F32)).then_inc(S["coef_in"], 16)
                sp.dma_start(coef[16 + 4 * r:20 + 4 * r, 4:6, :].bitcast(F32), coef_hl[:, r // 2, 4 * P:4 * P + PIX].rearrange(
                    "f (c k) -> f c k", c=2).bitcast(F32)).then_inc(S["coef_in"], 16)
            sp.wait_ge(S["r_hi"], 1)
            sp.wait_ge(S["r_lo"], 1)
            sp.wait_ge(S["rs_zero"], 1)
            for kind in range(2):
                for r in range(4):
                    row = 16 * (1 - kind) + 4 * r
                    sp.dma_start(RS[row:row + 4].rearrange("f c g b m -> f (c g b) m").bitcast(F32),
                                 r_hl[:, r % 2, kind, :].bitcast(F32))\
                        .then_inc(S["r_rows"], 16)

            def store_tn(i, u):
                sp.wait_ge(S["b_norm"], i + 1)
                sp.dma_start(tn_dram[ds(i * (4 * P), 4 * P), :].rearrange("(q p) d -> p q d", p=P),
                             xn[:, u, :, :]).then_inc(S[f"b_tn{u}"], 16)
            pair_loop(sp, store_tn)
            sp.wait_ge(S["b_u"], 2 * PAIRS)
            sp.dma_start(w1s, io["w1"]).then_inc(S["ffn_in"], 16)
            sp.dma_start(w3s, io["w3"]).then_inc(S["ffn_in"], 16)
            sp.wait_ge(S["b_cross"], 2 * PAIRS)
            sp.dma_start(w2s, io["w2"]).then_inc(S["w2_in"], 16)

            for b in range(4):
                sp.wait_ge(S[f"y_out{b}"], 16 * (SLOT_TILES // 4))
            y_tok = y_dram[0:2 * NTOK, :].rearrange("(k t p) d -> k p t d", k=2, p=P)
            for i in range(PAIRS):
                u = i % 4
                wait_done(sp, S["c_done"], i - 3)
                sp.dma_start(ya[u].rearrange("p (t d) -> p t d", t=4), y_tok[0, :, 4 * i:4 * i + 4, :])\
                    .then_inc(S[f"c_in{u}"], 16)
                sp.dma_start(yb[u].rearrange("p (t d) -> p t d", t=4), y_tok[1, :, 4 * i:4 * i + 4, :])\
                    .then_inc(S[f"c_in{u}"], 16)

        @block.gpsimd
        def _(pool):
            pool.memset(rwc[:, :], 0.0).then_inc(S["w_zero"], 1)
            pool.memset(gate[:, :], 0.0).then_inc(S["w_zero"], 1)
            pool.memset(sp2[:, 4], 0.0).then_inc(S["w_zero"], 1)
            pool.memset(mhalf[:, :], -0.5).then_inc(S["mhalf_set"], 1)
            pool.memset(xp[:].rearrange("p u g a b -> p (u g a b)"), 0.0).then_inc(S["pad_zero"], 1)
            pool.memset(coef[:].rearrange("p c k -> p (c k)").bitcast(F32), 0.0).then_inc(S["coef_zero"], 1)
            pool.memset(ones[:, :], 1.0).then_inc(S["q_tri"], 1)
            pool.memset(tri[:, :], 1.0).then_inc(S["q_tri"], 1)
            pool.wait_ge(S["q_tri"], 2)
            pool.affine_select(out=tri[:, :], in_=tri[:, :], compare_op=ALU.is_gt, fill=0.0, base=0,
                               pattern=[[1, P]], channel_multiplier=-1).then_inc(S["q_tri"], 1)
            pool.memset(RS[:].rearrange("p c g b m -> p (c g b m)").bitcast(F32), 0.0).then_inc(S["rs_zero"], 1)
            pool.memset(tap_k[:].rearrange("p t b -> p (t b)"), 0.0).then_inc(S["k_zero"], 1)
            pool.memset(rw_k[:, :], 0.0).then_inc(S["k_zero"], 1)
            pool.wait_ge(S["mhalf_set"], 1)

            def inv_std(aggr, added, done, eps, i, u):
                wait_apart(pool, S[aggr], i + 1)
                pool.tensor_scalar(var_eps[:, u, :], mv[:, u, :, 1], eps, None, ALU.add).then_inc(S[added], 1)
                wait_apart(pool, S[added], i + 1)
                pool.tensor_tensor(rstd[:, u, :], var_eps[:, u, :], mhalf[:, :], ALU.pow).then_inc(S[done], 1)

            def border(i, u):
                wait_apart(pool, S["a_xc"], i + 1)
                wait_done(pool, S["a_conv"], i - 1)
                pool.tensor_copy(xp[:, u, :, 1:SIZE + 1, 1:SIZE + 1],
                                 xc[:, u, :].rearrange("p (g a b) -> p g a b", g=2, a=SIZE)).then_inc(S["a_xp"], 1)

            def phase_a(i, u):
                if not last(i, PAIRS):
                    inv_std("a_aggr", "a_eps", "a_rstd", LN_C_EPS, i + 1, 1 - u)
                pool.wait_ge(S["a_star"], i * 2 + 2)
                wait_done(pool, S["a_dft"], i * 2 - 2)
                pool.tensor_tensor(fold[u][0], star_at(0, i), star_at(1, i), ALU.add).then_inc(S["a_fold"], 1)
                pool.tensor_tensor(fold[u][1], star_at(0, i), star_at(1, i), ALU.subtract)\
                    .then_inc(S["a_fold"], 1)
                if not last(i, PAIRS):
                    border(i + 1, 1 - u)
            inv_std("a_aggr", "a_eps", "a_rstd", LN_C_EPS, 0, 0)
            pool.wait_ge(S["pad_zero"], 1)
            border(0, 0)
            pair_loop(pool, phase_a)

            def phase_b(i, u):
                for j in range(2):
                    pool.wait_ge(S["b_sw"], i * 2 + j + 1)
                    wait_done(pool, S["b_even"], i * 2 + j - 1)
                    pool.tensor_tensor(u_c[j], star_at(j, i), sw_c[j], ALU.mult).then_inc(S["b_u"], 1)
                if not first(i):
                    inv_std("b_aggr", "b_eps", "b_rstd", LN_T_EPS, i - 1, 1 - u)
                for e in range(2):
                    pool.wait_ge(S["b_cross"], i * 2 + e + 1)
                    wait_done(pool, S["b_inv"], i * 2 + e - 1)
                    pool.tensor_tensor(y_c[e], prod[e], cross[e], ALU.add).then_inc(S["b_y"], 1)
            pair_loop(pool, phase_b)
            inv_std("b_aggr", "b_eps", "b_rstd", LN_T_EPS, PAIRS - 1, 1)

            for ap, pat, base, cm in (
                    (q_rev.rearrange("p (t e) -> p t e", e=E), [[0, TILES], [-1, E]], E, 0),
                    (q_id1.rearrange("p (k t) -> p k t", k=2), [[NTOK, 2], [P, TILES]], 1, 1),
                    (q_row, [[1, P]], 0, 0),
                    (q_trash, [[P, SLOT_TILES]], 2 * NTOK + 1, 1),
                    (q_jtok.rearrange("p (e j) -> p e j", e=E), [[0, E], [P, SLOT_TILES]], 0, 0)):
                pool.iota(ap, pat, base=base, channel_multiplier=cm,
                          allow_small_or_imprecise_dtypes=True).then_inc(S["q_iota"], 1)
            pool.memset(q_one, 1.0).then_inc(S["q_iota"], 1)

            pool.wait_ge(S["q_tables"], 1)
            for u in range(2):
                pool.wait_ge(S[f"b_tn{u}"], 16 * (PAIRS // 2))

            def gather(j, b):
                wait_apart(pool, S["f_tr"], j - 3)
                quad, col, u = b // 4 % 2, b % 4, b % 4
                if col == 0:
                    pool.tensor_copy(idx_g[quad][:, :], idx_gather[:, ds(j, 4)]).then_inc(S["g_idx"], 4)
                    wait_apart(pool, S["g_idx"], j + 4)
                pool.indirect_dma_start(xg[u], None, tn_dram, bass.IndirectOffsetOnAxis(
                    ap=idx_g[quad][:, col:col + 1], axis=0)).then_inc(S[f"g_x{u}"], 16)

            def scatter(j, b):
                wait_apart(pool, S["f_ys"], j + 1)
                quad, col, u = b // 4 % 2, b % 4, b % 4
                if col == 0:
                    pool.tensor_copy(idx_s[quad][:, :], idx_scatter[:, ds(j, 4)]).then_inc(S["s_idx"], 4)
                    wait_apart(pool, S["s_idx"], j + 4)
                pool.indirect_dma_start(y_dram, bass.IndirectOffsetOnAxis(ap=idx_s[quad][:, col:col + 1], axis=0),
                                        yo[u], None).then_inc(S[f"y_out{u}"], 16)

            for b in range(3):
                gather(b, b)

            def step(j, b):
                if not isinstance(j, int) or j + 3 < SLOT_TILES:
                    gather(j + 3, (b + 3) % 8)
                if not isinstance(j, int) or j >= 2:
                    scatter(j - 2, (b - 2) % 8)
            tile_loop(pool, step, 8)
            scatter(SLOT_TILES - 2, 6)
            scatter(SLOT_TILES - 1, 7)

        @block.scalar
        def _(act):
            act.wait_ge(S["coef_ps"], 1)
            act.activation(coef_hl[:, 0, 0:4 * P], ps_conv[1][0:NF, :], ACT.Copy).then_inc(S["coef_hi"], 1)
            act.activation(coef_hl[:, 0, 4 * P:4 * P + PIX], sw_rows[:, :], ACT.Copy).then_inc(S["coef_hi"], 1)
            act.wait_ge(S["consts_in"], 16 * 15)

            def image(i, u):
                act.wait_ge(S["a_tr"], i + 1)
                wait_done(act, S["a_rw1"], i - 1)
                wait_done(act, S["a_xp"], i - 1)
                act.activation(xc[:, u, :], ps_tr[:, :], ACT.Copy).then_inc(S["a_xc"], 1)

            def phase_a(i, u):
                for j in range(2):
                    act.wait_ge(S["a_pw"], i * 2 + j + 1)
                    act.activation(relu_x[:, j, :], ps_pw[j][:, :], ACT.Relu).then_inc(S["a_relu"], 1)
                for j in range(2):
                    act.wait_ge(S["a_relu"], i * 2 + j + 1)
                    wait_done(act, S["a_star"], i * 2 + j - 1)
                    act.activation(sq_x[:, j, :], relu_x[:, j, :], ACT.Square).then_inc(S["a_sq"], 1)
                act.wait_ge(S["a_conv"], i + 1)
                act.activation(s_all[:, ds(i, 1), :, :].rearrange("p o a b -> p (o a b)"), ps_conv[u][:, 0:PIX],
                               ACT.Relu, bias=sp1_b[:, 0:1]).then_inc(S["a_relu_s"], 1)
                act.wait_ge(S["a_rw1"], i + 1)
                act.activation(r1[:, :], ps_r[:, 0:PIX], ACT.Relu, bias=rw1_b[:, 0:1]).then_inc(S["a_relu_r"], 1)
                if not last(i, PAIRS):
                    image(i + 1, 1 - u)
                act.wait_ge(S["a_rw2"], i + 1)
                act.activation(r2[:, :], ps_r[:, 0:PIX], ACT.Relu, bias=rwc_b[:, 0:1],
                               accum_out=rsum[:, ds(i, 1)]).then_inc(S["a_rsum"], 1)
            image(0, 0)
            pair_loop(act, phase_a)

            act.wait_ge(S["r_sub"], 1)
            lg_flat = lg[:].rearrange("p s f c b -> p (s f c b)")
            act.activation(lg_flat, lg_flat, ACT.Exp).then_inc(S["r_exp"], 1)
            act.wait_ge(S["r_tr"], 1)
            act.activation(r_hl[:, 0, :, :].rearrange("p s m -> p (s m)"), ps_tr[:, 0:2 * P], ACT.Copy)\
                .then_inc(S["r_hi"], 1)

            def spatial(i):
                for j in range(2):
                    act.wait_ge(S["b_w"], i * 6 + j + 1)
                    wait_done(act, S["b_u"], i * 2 + j - 1)
                    act.activation(sw_c[j], ps_w[j][:, :], ACT.Copy).then_inc(S["b_sw"], 1)

            def gate_copy(i, u):
                act.wait_ge(S["b_tr"], i + 1)
                wait_done(act, S["b_gate"], i - 1)
                act.activation(tnt[u], ps_v[0][:, :], ACT.Copy).then_inc(S["b_tnt"], 1)

            def phase_b(i, u):
                if not first(i):
                    gate_copy(i - 1, 1 - u)
                if not last(i, PAIRS):
                    spatial(i + 1)
                for m in range(2):
                    act.wait_ge(S["b_vt"], i * 2 + m + 1)
                    wait_done(act, S["b_w2"], i - 1)
                    act.activation(vt_c[u][m], ps_v[m][:, :], ACT.Copy).then_inc(S["b_vts"], 1)
            spatial(0)
            pair_loop(act, phase_b)
            gate_copy(PAIRS - 1, 1)

            act.wait_ge(S["q_ready"], 1)
            act.activation(q_exp, q_diff, ACT.Exp).then_inc(S["q_exp_done"], 1)

            def hidden_copy(j, u):
                act.wait_ge(S["f_ht"], j + 1)
                wait_done(act, S["f_y"], j - 1)
                act.activation(hidt[u], p_ht[u][:, 0:HID], ACT.Copy).then_inc(S["f_hts"], 1)

            def step(j, u):
                act.wait_ge(S["f_h"], j + 1)
                wait_done(act, S["f_act"], j - 1)
                act.activation(silu[u], p_h1[u][:, 0:HID], ACT.Silu).then_inc(S["f_silu"], 1)
                if not first(j):
                    hidden_copy(j - 1, 1 - u)
            tile_loop(act, lambda j, b: step(j, b % 2), 4)
            hidden_copy(SLOT_TILES - 1, 1)

            out_tiles = io["out"].rearrange("(t p) d -> p t d", p=P)
            for i in range(PAIRS):
                act.wait_ge(S["c_done"], i + 1)
                act.dma_start(out_tiles[:, 4 * i:4 * i + 4, :], T[:, 4 * i:4 * i + 4, :]).then_inc(S["out_sent"], 16)
            act.wait_ge(S["out_sent"], 16 * PAIRS)

        @block.tensor
        def _(pe):
            pe.wait_ge(S["tab_in"], 16 * 9)
            n = 0
            for part in range(2):
                for cw, table in ((cw_a, sel), (cw_b, sel_b)):
                    mm = pe.matmul(ps_conv[1][0:NF, :], cw[:, :, part], table[:, part, :], start=(n == 0), stop=(n == 3))
                    n += 1
            mm.then_inc(S["coef_ps"], 1)
            pe.wait_ge(S["consts_in"], 16 * 15)
            pe.wait_ge(S["coef_lo"], 2)

            def transposes(i, u):
                pe.wait_ge(S["a_norm"], i + 1)
                wait_done(pe, S["a_xc"], i)
                for t in range(4):
                    mm = pe.transpose(ps_tr[:, t * P:(t + 1) * P], xn[:, u, t, :], ident[:, :])
                mm.then_inc(S["a_tr"], 1)

            def phase_a(i, u):
                pe.wait_ge(S["a_xc"], i + 1)
                for j in range(2):
                    wait_done(pe, S["a_relu"], i * 2 + j - 1)
                    for g in range(2):
                        mm = pe.matmul(ps_pw[j][:, g * MED:(g + 1) * MED],
                                       xc[:, u, (2 * g + j) * P:(2 * g + j + 1) * P], wp1[:, :], start=True, stop=True)
                    mm.then_inc(S["a_pw"], 1)
                wait_done(pe, S["a_relu_s"], i - 1)
                pe.wait_ge(S["a_xp"], i + 1)
                for t in range(TAPS):
                    for g in range(2):
                        mm = pe.matmul(ps_conv[u][HALF * g:HALF * g + HALF, 0:PIX], sp1[:, t, :],
                                       xp[:, u, g, t // 3:t // 3 + SIZE, t % 3:t % 3 + SIZE],
                                       start=(t == 0), stop=(t == TAPS - 1))
                mm.then_inc(S["a_conv"], 1)
                wait_done(pe, S["a_rsum"], i)
                for g in range(2):
                    mm = pe.matmul(ps_r[HALF * g:HALF * g + HALF, 0:PIX], rw1[:, :],
                                   xc[:, u, g * PIX:(g + 1) * PIX], start=True, stop=True)
                mm.then_inc(S["a_rw1"], 1)
                if not last(i, PAIRS):
                    transposes(i + 1, 1 - u)
                pe.wait_ge(S["a_relu_r"], i + 1)
                pe.matmul(ps_r[:, 0:PIX], rwc[:, :], r1[:, :], start=True, stop=True).then_inc(S["a_rw2"], 1)
                for e in range(2):
                    pe.wait_ge(S["a_fold"], i * 2 + e + 1)
                    wait_done(pe, S["a_spec"], i * 2 + e - 1)
                    pe.matmul(ps_x[e][:, :], fwd[:, e, :], fold[u][e], start=True, stop=True).then_inc(S["a_dft"], 1)
            transposes(0, 0)
            pair_loop(pe, phase_a)

            pe.wait_ge(S["route_in"], 64)
            pe.wait_ge(S["w_zero"], 3)
            pe.wait_ge(S["r_cat"], 6)
            pe.wait_ge(S["a_relu"], 2 * PAIRS)
            pe.wait_ge(S["a_relu_s"], PAIRS)
            for k in range(2 * NF):
                block_k = slice(k % 4 * P, (k % 4 + 1) * P)
                for t in range(5):
                    pe.matmul(ps_conv[k // 4][:, block_k], sp2[:, t, k * P:(k + 1) * P], tap_k[:, t, :],
                              start=(t == 0), stop=(t == 4))
                mm = pe.matmul(ps_pw[k // 4][:, block_k], rw2[:, k * P:(k + 1) * P], rw_k[:, :], start=True, stop=True)
            mm.then_inc(S["r_mm"], 1)
            pe.wait_ge(S["r_norm"], 1)
            for s in range(2):
                mm = pe.transpose(ps_tr[:, s * P:(s + 1) * P], lg[:, s].rearrange("p f c b -> p (f c b)"),
                                  ident[:, :])
            mm.then_inc(S["r_tr"], 1)
            pe.wait_ge(S["coef_in"], 16 * 8)
            pe.wait_ge(S["r_rows"], 16 * 8)
            pe.wait_ge(S["a_spec"], 2 * PAIRS)

            ring = (4, 5, 0, 2, 1, 3)

            def filters(i, part):
                free = ((("b_cross", i * 2 - 1),), (("b_p", i * 2),), (("b_cross", i * 2),),
                        (("b_sw", i * 2 + 1),), (("b_sw", i * 2 + 2),), (("b_p", i * 2 + 1),))
                for n in range(3 * part, 3 * part + 3):
                    for name, count in free[n]:
                        wait_done(pe, S[name], count)
                    pe.matmul(ps_w[n % 3][:, :], coef[:, ring[n], :],
                              RS[:, :, :, ds(i, 1), :].rearrange("r c g b m -> r g c (b m)"), start=True, stop=True)\
                        .then_inc(S["b_w"], 1)

            def project(i, u):
                pe.wait_ge(S["b_vts"], i * 2 + 2)
                wait_done(pe, S["b_logit"], i)
                for t in range(4):
                    for m in range(2):
                        mm = pe.matmul(ps_y[:, t * P:(t + 1) * P], vt_c[u][m][:, t * P:(t + 1) * P], wp2[:, m, :],
                                       start=(m == 0), stop=(m == 1))
                mm.then_inc(S["b_w2"], 1)

            def gating(i, u):
                pe.wait_ge(S["b_norm"], i + 1)
                for t in range(4):
                    mm = pe.transpose(ps_v[0][:, t * P:(t + 1) * P], xn[:, u, t, :], ident[:, :])
                mm.then_inc(S["b_tr"], 1)
                pe.wait_ge(S["b_tnt"], i + 1)
                for t in range(4):
                    mm = pe.matmul(ps_y[:, t * P:(t + 1) * P], tnt[u][:, t * P:(t + 1) * P], gate[:, :],
                                   start=True, stop=True)
                mm.then_inc(S["b_gate"], 1)

            def phase_b(i, u):
                if not first(i):
                    project(i - 1, 1 - u)
                for e in range(2):
                    pe.wait_ge(S["b_y"], i * 2 + e + 1)
                    wait_done(pe, S["b_even"] if e == 0 else S["b_v"], i * 2)
                    pe.matmul(ps_i[e][:, :], inv[:, e, :], y_c[e], start=True, stop=True).then_inc(S["b_inv"], 1)
                if not first(i):
                    gating(i - 1, 1 - u)
                if not last(i, PAIRS):
                    filters(i + 1, 0)
                pe.wait_ge(S["b_v"], i * 2 + 2)
                for m in range(2):
                    wait_done(pe, S["b_vts"], i * 2 + m - 1)
                    for g in range(2):
                        for j in range(2):
                            mm = pe.transpose(ps_v[m][:, (2 * g + j) * P:(2 * g + j + 1) * P],
                                              v_c[j][:, g * MED + m * P:g * MED + (m + 1) * P], ident[:, :])
                    mm.then_inc(S["b_vt"], 1)
                if not last(i, PAIRS):
                    filters(i + 1, 1)
            filters(0, 0)
            filters(0, 1)
            pair_loop(pe, phase_b)
            project(PAIRS - 1, 1)
            gating(PAIRS - 1, 1)

            pe.wait_ge(S["q_tri"], 3)
            pe.wait_ge(S["q_ready"], 2)
            counts = q_cnt.rearrange("p (t e) -> p e t", e=E)
            pe.matmul(ps_tot[:, 0:E * TILES], ones[:, :], counts, start=True, stop=True).then_inc(S["q_count"], 1)
            pe.matmul(ps_rank[:, 0:E * TILES], tri[:, :], counts, start=True, stop=True).then_inc(S["q_count"], 1)

            def place(n, b):
                pe.wait_ge(S["q_oh_ready"], n + 1)
                pe.matmul(ps_idx[:, 0:P], oh_s[b], oh_j[b], start=first(n), stop=last(n, 2 * TILES))\
                    .then_inc(S["q_oh_used"], 1)
            for b in range(4):
                place(b, b)
            with pe.Fori(1, TILES // 2 - 1) as n:
                for b in range(4):
                    place(n * 4 + b, b)
            for b in range(4):
                place(2 * TILES - 4 + b, b)

            pe.wait_ge(S["ffn_in"], 32)
            pe.wait_ge(S["w2_in"], 16)
            pe.wait_ge(S["q_tables"], 1)

            def transpose_x(j, b):
                pe.wait_ge(S[f"g_x{b}"], j * 4 + 16 - 4 * b)
                wait_done(pe, S["f_xt"], j)
                pe.transpose(p_x[:, 0:P], xg[b], ident[:, :]).then_inc(S["f_tr"], 1)

            def turn(j, u):
                pe.wait_ge(S["f_act"], j + 1)
                wait_done(pe, S["f_hts"], j - 1)
                for c in range(HC):
                    mm = pe.transpose(p_ht[u][:, c * P:(c + 1) * P], hid[u][:, c * P:(c + 1) * P], ident[:, :])
                mm.then_inc(S["f_ht"], 1)

            def down(j, u):
                e = pe.value_load(tile_expert[0:1, ds(j, 1)], min_val=0, max_val=E - 1)
                pe.wait_ge(S["f_hts"], j + 1)
                wait_done(pe, S["f_ys"], j)
                for c in range(HC):
                    mm = pe.matmul(p_y[:, 0:DIM], hidt[u][:, c * P:(c + 1) * P], w2s[:, c, ds(e * DIM, DIM)],
                                   start=(c == 0), stop=(c == HC - 1))
                mm.then_inc(S["f_y"], 1)

            def step(j, b):
                u = b % 2
                if not last(j, SLOT_TILES):
                    transpose_x(j + 1, (b + 1) % 4)
                e = pe.value_load(tile_expert[0:1, ds(j, 1)], min_val=0, max_val=E - 1)
                pe.wait_ge(S["f_xt"], j + 1)
                wait_done(pe, S["f_act"], j - 1)
                pe.matmul(p_h1[u][:, 0:HID], xgt[u], w1s[:, ds(e * HID, HID)], start=True, stop=True)
                pe.matmul(p_h3[u][:, 0:HID], xgt[u], w3s[:, ds(e * HID, HID)], start=True, stop=True)\
                    .then_inc(S["f_h"], 1)
                if not first(j):
                    turn(j - 1, 1 - u)
                if not isinstance(j, int) or j >= 2:
                    down(j - 2, u)
            transpose_x(0, 0)
            tile_loop(pe, step, 4)
            turn(SLOT_TILES - 1, 1)
            down(SLOT_TILES - 2, 0)
            down(SLOT_TILES - 1, 1)

        @block.vector
        def _(dve):
            dve.wait_ge(S["coef_hi"], 2)
            dve.tensor_tensor(coef_hl[:, 1, 0:4 * P], ps_conv[1][0:NF, :], coef_hl[:, 0, 0:4 * P].bitcast(F32),
                              ALU.subtract).then_inc(S["coef_lo"], 1)
            dve.tensor_tensor(coef_hl[:, 1, 4 * P:4 * P + PIX], sw_rows[:, :],
                              coef_hl[:, 0, 4 * P:4 * P + PIX].bitcast(F32), ALU.subtract).then_inc(S["coef_lo"], 1)

            def stats(ph, i, u):
                for t in range(4):
                    op = dve.bn_stats(st6[:, u, t, :], flat(T[:, ds(i * 4 + t, 1), :]))
                op.then_inc(S[ph + "_stats"], 1)
                wait_apart(dve, S[ph + "_stats"], i + 1)
                for t in range(4):
                    op = dve.bn_aggr(mv[:, u, t, :], st6[:, u, t, :])
                op.then_inc(S[ph + "_aggr"], 1)

            def normalise(ph, i, u):
                dve.wait_ge(S[ph + "_rstd"], i + 1)
                for t in range(4):
                    op = dve.tensor_scalar(xn[:, u, t, :], flat(T[:, ds(i * 4 + t, 1), :]), mv[:, u, t, 0:1],
                                           rstd[:, u, t:t + 1], ALU.subtract, ALU.mult)
                op.then_inc(S[ph + "_norm"], 1)

            def phase_a(i, u):
                if isinstance(i, int) and i == 1:
                    for c in range(1, 4):
                        dve.wait_ge(S[f"x_in{c}"], 16)
                if not last(i, PAIRS):
                    stats("a", i + 1, 1 - u)
                for j in range(2):
                    dve.wait_ge(S["a_sq"], i * 2 + j + 1)
                    dve.tensor_scalar(star_at(j, i), sq_x[:, j, :], star_s[:, 0:1], star_b[:, 0:1], ALU.mult, ALU.add)\
                        .then_inc(S["a_star"], 1)
                if not last(i, PAIRS):
                    wait_done(dve, S["a_tr"], i)
                    normalise("a", i + 1, 1 - u)
                dve.wait_ge(S["a_relu_s"], i + 1)
                dve.tensor_reduce(rows[:, 1, ds(i, 1), :].rearrange("p o a -> p (o a)"),
                                  s_all[:, ds(i, 1), :, :].rearrange("p o a b -> p (o a) b"), AX.X, ALU.add)\
                    .then_inc(S["a_rows"], 1)
                for e in range(2):
                    dve.wait_ge(S["a_dft"], i * 2 + e + 1)
                    dve.tensor_copy(spec_at(0, P, e, i), ps_x[e][:, :]).then_inc(S["a_spec"], 1)
            dve.wait_ge(S["x_in0"], 16)
            dve.wait_ge(S["consts_in"], 16 * 15)
            stats("a", 0, 0)
            normalise("a", 0, 0)
            pair_loop(dve, phase_a)

            dve.wait_ge(S["a_rows"], PAIRS)
            dve.tensor_tensor(rows[:, 0], rows[:, 1], s_all[:, :, :, SIZE - 1], ALU.subtract).then_inc(S["r_cols"], 1)
            dve.tensor_tensor(rows[:, 2], rows[:, 1], s_all[:, :, :, 0], ALU.subtract).then_inc(S["r_cols"], 1)
            dve.wait_ge(S["r_cols"], 2)
            dve.tensor_reduce(tap_sum[:, 1], rows[:], AX.X, ALU.add).then_inc(S["r_full"], 1)
            dve.wait_ge(S["r_full"], 1)
            dve.tensor_tensor(tap_sum[:, 0], tap_sum[:, 1], rows[:, :, :, SIZE - 1], ALU.subtract)\
                .then_inc(S["r_taps"], 1)
            dve.tensor_tensor(tap_sum[:, 2], tap_sum[:, 1], rows[:, :, :, 0], ALU.subtract).then_inc(S["r_taps"], 1)
            dve.wait_ge(S["r_taps"], 2)
            dve.wait_ge(S["a_rsum"], PAIRS)
            dve.wait_ge(S["k_zero"], 2)
            taps = tap_sum[:].rearrange("p y x b -> p (y x) b")
            for g in range(2):
                half, cols = slice(HALF * g, HALF * g + HALF), slice(PAIRS * g, PAIRS * g + PAIRS)
                dve.tensor_copy(tap_k[0:HALF, 0:5, cols], taps[half, 0:TAPS:2, :]).then_inc(S["r_cat"], 1)
                dve.tensor_copy(tap_k[HALF:P, 0:4, cols], taps[half, 1:TAPS:2, :]).then_inc(S["r_cat"], 1)
                dve.tensor_copy(rw_k[half, cols], rsum[half, :]).then_inc(S["r_cat"], 1)
            dve.wait_ge(S["tab_in"], 16 * 9)
            dve.wait_ge(S["r_mm"], 1)
            for s, banks in ((0, ps_conv), (1, ps_pw)):
                for h in range(2):
                    dve.scalar_tensor_tensor(
                        out=lg[:, s].rearrange("p f c b -> p (f c) b")[:, 4 * h:4 * h + 4],
                        in0=banks[h][:, :].rearrange("p (k n) -> p k n", k=4)[:, :, 0:BATCH], scalar=1.0 / PIX,
                        in1=route_b[:, 8 * s + 4 * h:8 * s + 4 * h + 4].unsqueeze(2).to_broadcast([P, 4, BATCH]),
                        op0=ALU.mult, op1=ALU.add).then_inc(S["r_log"], 1)
            lg_f = lg[:].rearrange("p s f c b -> p s f (c b)")
            dve.wait_ge(S["r_log"], 4)
            dve.tensor_reduce(lmax[:, :, :], lg_f.rearrange("p s f r -> p s r f"), AX.X, ALU.max)\
                .then_inc(S["r_max"], 1)
            dve.wait_ge(S["r_max"], 1)
            dve.tensor_tensor(lg_f, lg_f, lmax[:, :, :].unsqueeze(2).to_broadcast([P, 2, NF, 32]), ALU.subtract)\
                .then_inc(S["r_sub"], 1)
            dve.wait_ge(S["r_exp"], 1)
            dve.tensor_reduce(lsum[:, :, :], lg_f.rearrange("p s f r -> p s r f"), AX.X, ALU.add)\
                .then_inc(S["r_sum"], 1)
            dve.wait_ge(S["r_sum"], 1)
            dve.reciprocal(lmax[:, :, :], lsum[:, :, :]).then_inc(S["r_rec"], 1)
            dve.wait_ge(S["r_rec"], 1)
            dve.tensor_tensor(lg_f, lg_f, lmax[:, :, :].unsqueeze(2).to_broadcast([P, 2, NF, 32]), ALU.mult)\
                .then_inc(S["r_norm"], 1)
            dve.wait_ge(S["r_hi"], 1)
            dve.tensor_tensor(r_hl[:, 1, :, :].rearrange("p s m -> p (s m)"), ps_tr[:, 0:2 * P],
                              r_hl[:, 0, :, :].rearrange("p s m -> p (s m)").bitcast(F32), ALU.subtract)\
                .then_inc(S["r_lo"], 1)

            def filter_products(i):
                for e in range(2):
                    n_p, n_s = (2, 3) if e == 0 else (4, 5)
                    dve.wait_ge(S["b_w"], i * 6 + n_p + 1)
                    wait_done(dve, S["b_y"], i * 2 + e - 1)
                    dve.tensor_tensor(prod[e], spec_at(0, P, e, i), ps_w[n_p % 3][:, :], ALU.mult)\
                        .then_inc(S["b_p"], 1)
                    dve.wait_ge(S["b_w"], i * 6 + n_s + 1)
                    dve.tensor_tensor(cross[e][0:64], spec_at(64, P, e, i), ps_w[n_s % 3][0:64, :], ALU.mult)
                    dve.tensor_tensor(cross[e][64:P], spec_at(0, 64, e, i), ps_w[n_s % 3][64:P, :], ALU.mult)\
                        .then_inc(S["b_cross"], 1)

            def residual(i, u):
                dve.wait_ge(S["b_w2"], i + 1)
                dve.tensor_tensor(tokens(i), tokens(i), ps_y[:, :].rearrange("p (t d) -> p t d", t=4), ALU.add)\
                    .then_inc(S["b_t"], 1)
                wait_apart(dve, S["b_t"], i + 1)
                stats("b", i, u)

            def normalise_tokens(i, u):
                wait_done(dve, S[f"b_tn{u}"], i * 8 - 8 * u)
                wait_done(dve, S["b_tr"], i - 1)
                normalise("b", i, u)

            def logit_copy(i):
                dve.wait_ge(S["b_gate"], i + 1)
                dve.tensor_copy(logits[:, ds(i * 4, 4), :], ps_y[:, :].rearrange("p (t e) -> p t e", t=4)[:, :, 0:E])\
                    .then_inc(S["b_logit"], 1)

            def phase_b(i, u):
                filter_products(i)
                if not first(i):
                    residual(i - 1, 1 - u)
                for j in range(2):
                    dve.wait_ge(S["b_inv"], i * 2 + 1)
                    dve.wait_ge(S["b_u"], i * 2 + j + 1)
                    dve.tensor_tensor(even_c[j], u_c[j], ps_i[0][:, :], ALU.add).then_inc(S["b_even"], 1)
                if not first(i):
                    normalise_tokens(i - 1, 1 - u)
                for j in range(2):
                    dve.wait_ge(S["b_inv"], i * 2 + 2)
                    dve.wait_ge(S["b_even"], i * 2 + j + 1)
                    wait_done(dve, S["b_vt"], i * 2)
                    dve.tensor_tensor(v_c[j], even_c[j], ps_i[1][:, :], ALU.add if j == 0 else ALU.subtract)\
                        .then_inc(S["b_v"], 1)
                if not first(i):
                    logit_copy(i - 1)
            pair_loop(dve, phase_b)
            residual(PAIRS - 1, 1)
            normalise_tokens(PAIRS - 1, 1)
            logit_copy(PAIRS - 1)

            done = [0]

            def then(op):
                done[0] += 1
                op.then_inc(S["q_dve"], 1)
                dve.wait_ge(S["q_dve"], done[0])

            def by_tile(a):
                return a.rearrange("p (t e) -> p t e", e=E)

            def over_experts(a):
                return a.unsqueeze(2).to_broadcast([P, TILES, E])

            dve.wait_ge(S["b_logit"], PAIRS)
            dve.wait_ge(S["q_iota"], 6)
            source = logits[:, :, :]
            for k in range(2):
                then(dve.tensor_reduce(q_m[k], source, AX.X, ALU.max))
                then(dve.tensor_tensor(by_tile(q_eq), source, over_experts(q_m[k]), ALU.is_equal))
                then(dve.tensor_tensor(q_val, q_eq, q_rev, ALU.mult))
                then(dve.tensor_reduce(q_c, by_tile(q_val), AX.X, ALU.max))
                then(dve.tensor_tensor(by_tile(q_oh[k]), by_tile(q_rev), over_experts(q_c), ALU.is_equal))
                if k == 0:
                    then(dve.scalar_tensor_tensor(out=by_tile(q_l2), in0=by_tile(q_oh[0]), scalar=-3.0e38, in1=source,
                                                  op0=ALU.mult, op1=ALU.add))
                    source = by_tile(q_l2)
            dve.tensor_tensor(q_diff, q_m[1], q_m[0], ALU.subtract).then_inc(S["q_ready"], 1)
            dve.tensor_tensor(q_cnt, q_oh[0], q_oh[1], ALU.add).then_inc(S["q_ready"], 1)
            dve.wait_ge(S["q_exp_done"], 1)
            then(dve.tensor_scalar(q_den, q_exp, 1.0, None, ALU.add))
            then(dve.reciprocal(mix[:, 0, :], q_den))
            then(dve.tensor_tensor(mix[:, 1, :], q_exp, mix[:, 0, :], ALU.mult))
            dve.wait_ge(S["q_count"], 2)
            then(dve.tensor_copy(q_tot, ps_tot[:, 0:E * TILES]))
            then(dve.tensor_tensor_scan(q_incl, q_one, q_tot, 0.0, ALU.mult, ALU.add))
            ends = q_incl.rearrange("p (e t) -> p e t", t=TILES)[:, :, TILES - 1]
            then(dve.tensor_copy(q_tmp, ends))
            then(dve.tensor_tensor(q_tmp[:, 1:E], ends[:, 1:E], ends[:, 0:E - 1], ALU.subtract))
            then(dve.tensor_scalar(q_e32[:, :], q_tmp, float(P - 1), None, ALU.add))
            then(dve.tensor_scalar(q_e32[:, :], q_e32[:, :], 7, 7, ALU.logical_shift_right, ALU.logical_shift_left))
            then(dve.tensor_copy(q_cpad, q_e32[:, :]))
            then(dve.tensor_tensor_scan(q_pend, q_one[:, 0:E], q_cpad, 0.0, ALU.mult, ALU.add))
            then(dve.tensor_tensor(q_base, q_pend, q_cpad, ALU.subtract))
            then(dve.tensor_tensor(q_base, q_base, ends, ALU.subtract))
            then(dve.tensor_tensor(q_base, q_base, q_tmp, ALU.add))
            then(dve.tensor_tensor(q_incl, q_incl, q_tot, ALU.subtract))
            then(dve.tensor_tensor(q_incl, q_incl, ps_rank[:, 0:E * TILES], ALU.add))
            then(dve.tensor_tensor(q_slot.rearrange("p (e t) -> p e t", t=TILES),
                                   q_incl.rearrange("p (e t) -> p e t", t=TILES),
                                   q_base.unsqueeze(2).to_broadcast([P, E, TILES]), ALU.add))
            for k in range(2):
                then(dve.tensor_tensor(by_tile(q_sel), by_tile(q_oh[k]), q_slot.rearrange("p (e t) -> p t e", t=TILES),
                                       ALU.mult))
                then(dve.tensor_reduce(q_pos[:, k * TILES:(k + 1) * TILES], by_tile(q_sel), AX.X, ALU.add))
            then(dve.tensor_copy(q_i32[:, :], q_pos))
            then(dve.tensor_scalar(q_i32b[:, :], q_i32[:, :], P - 1, None, ALU.bitwise_and))
            then(dve.tensor_copy(q_low, q_i32b[:, :]))
            then(dve.tensor_scalar(q_i32b[:, :], q_i32[:, :], 7, None, ALU.logical_shift_right))
            then(dve.tensor_copy(q_high, q_i32b[:, :]))

            def one_hot(n, b):
                wait_done(dve, S["q_oh_used"], n - 3)
                dve.tensor_scalar(oh_s[b], q_row, q_low[:, ds(n, 1)], None, ALU.is_equal)
                dve.tensor_scalar(oh_j[b], q_row, q_high[:, ds(n, 1)], q_id1[:, ds(n, 1)], ALU.is_equal, ALU.mult)\
                    .then_inc(S["q_oh_ready"], 1)
            for b in range(4):
                one_hot(b, b)
            with dve.Fori(1, TILES // 2 - 1) as n:
                for b in range(4):
                    one_hot(n * 4 + b, b)
            for b in range(4):
                one_hot(2 * TILES - 4 + b, b)
            then(dve.tensor_tensor(q_jcmp.rearrange("p (e j) -> p e j", e=E), q_jtok.rearrange("p (e j) -> p e j", e=E),
                                   q_pend.unsqueeze(2).to_broadcast([P, E, SLOT_TILES]), ALU.is_ge))
            then(dve.tensor_reduce(q_inv, q_jcmp.rearrange("p (e j) -> p j e", e=E), AX.X, ALU.add))
            then(dve.tensor_scalar(tile_expert[0:1, :], q_inv[0:1, :], float(E - 1), None, ALU.min))
            dve.wait_ge(S["q_oh_used"], 2 * TILES)
            then(dve.tensor_copy(q_v, ps_idx[:, 0:SLOT_TILES]))
            then(dve.tensor_scalar(q_inv, q_v, 0.0, None, ALU.is_equal))
            then(dve.tensor_tensor(q_inv, q_inv, q_trash, ALU.mult))
            then(dve.tensor_tensor(q_v, q_v, q_inv, ALU.add))
            then(dve.tensor_scalar(idx_scatter[:, :], q_v, -1.0, None, ALU.add))
            dve.tensor_scalar(idx_gather[:, :], idx_scatter[:, :], NTOK - 1, None, ALU.bitwise_and)\
                .then_inc(S["q_tables"], 1)

            def x_copy(j, u):
                dve.wait_ge(S["f_tr"], j + 1)
                wait_done(dve, S["f_h"], j - 1)
                dve.tensor_copy(xgt[u], p_x[:, 0:P]).then_inc(S["f_xt"], 1)

            def y_copy(j, b):
                dve.wait_ge(S["f_y"], j + 1)
                wait_done(dve, S[f"y_out{b}"], j * 4 - 4 * b)
                dve.tensor_copy(yo[b], p_y[:, 0:DIM]).then_inc(S["f_ys"], 1)

            def step(j, b):
                u = b % 2
                if not last(j, SLOT_TILES):
                    x_copy(j + 1, 1 - u)
                if not isinstance(j, int) or j >= 3:
                    y_copy(j - 3, (b + 1) % 4)
                dve.wait_ge(S["f_silu"], j + 1)
                wait_done(dve, S["f_ht"], j - 1)
                dve.tensor_tensor(hid[u], silu[u], p_h3[u][:, 0:HID], ALU.mult).then_inc(S["f_act"], 1)
            x_copy(0, 0)
            tile_loop(dve, step, 4)
            for j in range(SLOT_TILES - 3, SLOT_TILES):
                y_copy(j, j % 4)

            for i in range(PAIRS):
                u = i % 4
                dve.wait_ge(S[f"c_in{u}"], 32 * (i // 4 + 1))
                for k, y in enumerate((ya[u], yb[u])):
                    for t in range(4):
                        tile = T[:, 4 * i + t, :]
                        op = dve.scalar_tensor_tensor(out=tile, in0=y[:, t * DIM:(t + 1) * DIM],
                                                      scalar=mix[:, k, 4 * i + t:4 * i + t + 1], in1=tile,
                                                      op0=ALU.mult, op1=ALU.add)
                    if k == 0:
                        op.then_inc(S["c_sum"], 1)
                        dve.wait_ge(S["c_sum"], i + 1)
                op.then_inc(S["c_done"], 1)


def layouts(x, L0_conv_w_pw1, L0_conv_w_pw2, L0_conv_star_scale, L0_conv_star_bias, L0_conv_rw_fc1_w,
            L0_conv_rw_fc1_b, L0_conv_rw_conv_w, L0_conv_rw_conv_b, L0_conv_rw_fc2_w, L0_conv_rw_fc2_b,
            L0_conv_sp_fc1_w, L0_conv_sp_fc1_b, L0_conv_sp_fc2_w, L0_conv_sp_fc2_b, L0_conv_complex_weights,
            L0_conv_spatial_weights, L0_ffn_gate_w, L0_ffn_w1, L0_ffn_w3, L0_ffn_w2):
    c = np.ascontiguousarray
    forward, inverse, sel = fourier_tables()
    cw = L0_conv_complex_weights.reshape(SIZE * FS, NF, 2)
    route_b = np.stack([L0_conv_sp_fc2_b.reshape(NF, 2, P), L0_conv_rw_fc2_b.reshape(NF, 2, P)])
    return {
        "x": c(x.transpose(0, 2, 3, 1).reshape(NTOK, DIM)),
        "ident": np.eye(P, dtype=np.float32),
        "fwd": c(forward), "inv": c(inverse),
        "sel_a": c(sel[:P].reshape(P, 2, 4 * P)), "sel_b": c(sel[P:].reshape(SIZE * FS - P, 2, 4 * P)),
        "sp1": c(L0_conv_sp_fc1_w.transpose(1, 2, 3, 0).reshape(DIM, TAPS, HALF)),
        "rw1": c(L0_conv_rw_fc1_w[:, :, 0, 0].T),
        "rwc": c(L0_conv_rw_conv_w[:, :, 0, 0].T),
        "sp1_b": c(L0_conv_sp_fc1_b[:, None]), "rw1_b": c(L0_conv_rw_fc1_b[:, None]),
        "rwc_b": c(L0_conv_rw_conv_b[:, None]),
        "route_b": c(route_b.transpose(3, 0, 1, 2).reshape(P, 16)),
        "sp2_even": c(L0_conv_sp_fc2_w.transpose(1, 2, 3, 0).reshape(HALF, TAPS, NF * MED)[:, 0::2]),
        "sp2_odd": c(L0_conv_sp_fc2_w.transpose(1, 2, 3, 0).reshape(HALF, TAPS, NF * MED)[:, 1::2]),
        "rw2": c(L0_conv_rw_fc2_w[:, :, 0, 0].T),
        "wp1": c(L0_conv_w_pw1.T),
        "wp2": c(L0_conv_w_pw2.T.reshape(2, P, DIM).transpose(1, 0, 2)),
        "star_s": c(L0_conv_star_scale), "star_b": c(L0_conv_star_bias),
        "gate": c(L0_ffn_gate_w.T),
        "cw_a": c(cw[:P]), "cw_b": c(cw[P:]),
        "sw_rows": c(L0_conv_spatial_weights.reshape(PIX, NF).T),
        "w1": c(L0_ffn_w1.transpose(2, 0, 1).reshape(DIM, E * HID)),
        "w3": c(L0_ffn_w3.transpose(2, 0, 1).reshape(DIM, E * HID)),
        "w2": c(L0_ffn_w2.reshape(E, DIM, HC, P).transpose(3, 2, 0, 1).reshape(P, HC, E * DIM)),
    }


def kernel(**inputs):
    import concourse.bacc as bacc
    from concourse.bass_utils import run_bass_kernel_spmd

    arrays = layouts(**{k: np.asarray(a) for k, a in inputs.items()})
    nc = bacc.Bacc("TRN2", target_bir_lowering=False, num_devices=1)
    io = {k: nc.dram_tensor(f"in_{k}", a.shape, mybir.dt.from_np(a.dtype), kind="ExternalInput").ap()
          for k, a in arrays.items()}
    io["out"] = nc.dram_tensor("out", (NTOK, DIM), F32, kind="ExternalOutput").ap()
    metaformer(nc, io)
    r = run_bass_kernel_spmd(nc, [{f"in_{k}": a for k, a in arrays.items()}], core_ids=[0])
    out = r.results[0]["out"]
    return np.ascontiguousarray(out.reshape(BATCH, SIZE, SIZE, DIM).transpose(0, 3, 1, 2))
```

```python
from contextlib import ExitStack

import numpy as np

import concourse.bass as bass
from concourse import mybir

ALU = mybir.AluOpType
ACT = mybir.ActivationFunctionType
AX = mybir.AxisListType
F32 = mybir.dt.float32
F32R = mybir.dt.float32r
I32 = mybir.dt.int32
U32 = mybir.dt.uint32
ds = bass.ds

P = 128
DIM = 128
MED = 2 * DIM
NF = 4
SIZE = 16
FS = SIZE // 2 + 1
PIX = SIZE * SIZE
BATCH = 16
PAIRS = BATCH // 2
HALF = 64
TAPS = 9
PAD = SIZE + 2
NTOK = BATCH * PIX
TILES = NTOK // P
E = 8
HID = 384
HC = HID // P
SLOT_TILES = 2 * TILES + E
BUFS = 8
AHEAD = 5
LN_C_EPS = 1e-6
LN_T_EPS = 1e-5


def fourier_tables():
    h = np.arange(8)[:, None]
    w = np.arange(16)[None, :]
    forward = np.zeros((2, P, P), np.float64)
    inverse = np.zeros((2, P, P), np.float64)
    sel = np.zeros((2, 2, SIZE * FS, 2, P), np.float64)

    def at(ky, kx):
        return (ky % SIZE) * FS + kx

    for par in range(2):
        kys = range(par, SIZE, 2)
        full = [(ky, kx) for ky in kys for kx in range(1, 8)]
        full += [(ky, kx) for ky in kys if 0 < ky < 8 for kx in (0, 8)]
        real = [(ky, kx) for ky in kys if ky in (0, 8) for kx in (0, 8)]
        assert 2 * len(full) + len(real) == P
        for n, (ky, kx) in enumerate(full):
            th = (2 * np.pi / SIZE) * (ky * h + kx * w)
            re, im = n, n + 64
            forward[par, :, re] = np.cos(th).ravel()
            forward[par, :, im] = -np.sin(th).ravel()
            inverse[par, re] = 2 * np.cos(th).ravel() / PIX
            inverse[par, im] = -2 * np.sin(th).ravel() / PIX
            if kx in (0, 8):
                terms = [(at(ky, kx), 0.5, 0.5), (at(-ky, kx), 0.5, -0.5)]
            else:
                terms = [(at(ky, kx), 1.0, 1.0)]
            for b, cr, ci in terms:
                sel[0, 0, b, par, re] += cr
                sel[0, 0, b, par, im] += cr
                sel[1, 1, b, par, re] -= ci
                sel[1, 1, b, par, im] += ci
        for n, (ky, kx) in enumerate(real):
            row = (len(full) + n) if n < 2 else (64 + len(full) + n - 2)
            cs = np.cos((2 * np.pi / SIZE) * (ky * h + kx * w)).ravel()
            forward[par, :, row] = cs
            inverse[par, row] = cs / PIX
            sel[0, 0, at(ky, kx), par, row] = 1.0
    inverse = np.concatenate([inverse, inverse * np.array([1.0, -1.0])[:, None, None]], axis=2)
    sel = sel.transpose(2, 0, 1, 3, 4).reshape(SIZE * FS, 2, 4, P)
    return (forward.transpose(1, 0, 2).astype(np.float32), inverse.transpose(1, 0, 2).astype(np.float32),
            np.ascontiguousarray(sel.astype(np.float32)))


def wait_done(eng, sem, count):
    if isinstance(count, int) and count <= 0:
        return
    eng.wait_ge(sem, count)


def wait_apart(eng, sem, count):
    if not isinstance(count, int):
        count = eng.to_reg(count)
        eng.wait_ge(sem, 1)
    wait_done(eng, sem, count)


def pair_loop(eng, step):
    step(0, 0)
    step(1, 1)
    with eng.Fori(1, PAIRS // 2 - 1) as n:
        for u in range(2):
            step(n * 2 + u, u)
    step(PAIRS - 2, 0)
    step(PAIRS - 1, 1)


def filter_loop(eng, step):
    for i in range(3):
        step(i, i % 2)
    with eng.Fori(1, PAIRS // 2 - 1) as n:
        for k in range(2):
            step(n * 2 + 1 + k, 1 - k)
    step(PAIRS - 1, 1)


def tile_loop(eng, step):
    for b in range(BUFS):
        step(b, b)
    with eng.Fori(1, SLOT_TILES // BUFS - 1) as n:
        for b in range(BUFS):
            step(n * BUFS + b, b)
    for b in range(BUFS):
        step(SLOT_TILES - BUFS + b, b)


def first(i):
    return isinstance(i, int) and i == 0


def last(i, n):
    return isinstance(i, int) and i == n - 1


def flat(ap):
    return ap.rearrange("p a n -> p (a n)")


def metaformer(nc, io):
    with ExitStack() as ctx:
        def sb(name, shape, dt=F32):
            return ctx.enter_context(nc.sbuf_tensor(name, shape, dt))

        tn_dram = nc.dram_tensor("tn_dram", (NTOK, DIM), F32).ap()
        y_dram = nc.dram_tensor("y_dram", (2 * NTOK + SLOT_TILES * P, DIM), F32).ap()

        ident = sb("ident", [P, P])
        fwd = sb("fwd", [P, 2, P])
        inv = sb("inv", [P, 2, PIX])
        sp1 = sb("sp1", [P, TAPS, HALF])
        rw1 = sb("rw1", [P, HALF])
        rwc = sb("rwc", [P, P])
        sp1_b = sb("sp1_b", [P, 1])
        rw1_b = sb("rw1_b", [P, 1])
        rwc_b = sb("rwc_b", [P, 1])
        route_b = sb("route_b", [P, 2 * NF * 2])
        wp1 = sb("wp1", [P, MED])
        wp2 = sb("wp2", [P, 2, DIM])
        star_s = sb("star_s", [P, 1])
        star_b = sb("star_b", [P, 1])
        gate = sb("gate", [P, P])
        cw_a = sb("cw_a", [P, NF, 2])
        cw_b = sb("cw_b", [SIZE * FS - P, NF, 2])
        coef = sb("coef", [P, 6, P], F32R)
        coef_hl = sb("coef_hl", [NF, 2, 4 * P + PIX], F32R)
        sw_rows = sb("sw_rows", [NF, PIX])
        mhalf = sb("mhalf", [P, 4])
        var_eps = sb("var_eps", [P, 2, 4])
        tri = sb("tri", [P, P])
        ones = sb("ones", [P, P])
        T = sb("T", [P, TILES, DIM])
        mix = sb("mix", [P, 2, TILES])
        idx_gather = sb("idx_gather", [P, SLOT_TILES], U32)
        idx_scatter = sb("idx_scatter", [P, SLOT_TILES], U32)
        tile_experts = sb("tile_experts", [1, SLOT_TILES // BUFS], I32)
        logits = sb("logits", [P, TILES, E])
        st6 = sb("st6", [P, 2, 4, 6])
        mv = sb("mv", [P, 2, 4, 2])
        rstd = sb("rstd", [P, 2, 4])
        xn = sb("xn", [P, 2, 4, DIM])
        xp = sb("xp", [P, 2, 2, PAD, PAD])
        xc = sb("xc", [P, 2, 512])
        s_all = sb("s_all", [P, PAIRS, SIZE, SIZE])
        r1 = sb("r1", [P, PIX])
        r2 = sb("r2", [P, PIX])
        rsum = sb("rsum", [P, PAIRS])
        rows = sb("rows", [P, 3, PAIRS, SIZE])
        tap_sum = sb("tap_sum", [P, 3, 3, PAIRS])
        tap_k = sb("tap_k", [P, 5, P])
        rw_k = sb("rw_k", [P, P])
        lg = sb("lg", [P, 2, NF, 2, BATCH])
        lmax = sb("lmax", [P, 2, 32])
        lsum = sb("lsum", [P, 2, 32])
        r_hl = sb("r_hl", [P, 2, 2, P], F32R)
        RS = sb("RS", [P, 2, 2, PAIRS, P], F32R)
        q_i32 = sb("q_i32", [P, 2 * TILES], I32)
        q_i32b = sb("q_i32b", [P, 2 * TILES], I32)
        q_e32 = sb("q_e32", [P, E], I32)
        spec = sb("spec", [P, 2, PAIRS, 512])
        shared = sb("shared", [P, 7680])
        rw2 = sb("rw2", [P, NF * MED])
        idx_g = [sb(f"idx_g{u}", [P, 4], U32) for u in range(2)]
        idx_s = [sb(f"idx_s{u}", [P, 4], U32) for u in range(2)]
        with nc.sbuf_tensor("star", [P, 2, PAIRS, 512], F32) as star, nc.sbuf_tensor("buf", [P, 8, 512], F32) as buf:
            pass
        w_lo = sb("w_lo", [P, 8192], F32R)
        w3_hi = sb("w3_hi", [P, E * HID], F32R)
        xgt_hl = sb("xgt_hl", [P, 2, 2, P], F32R)

        relu_x, sq_x = buf[:, 0:2, :], buf[:, 2:4, :]
        fold = [[buf[:, 4 + 2 * u + e, :] for e in range(2)] for u in range(2)]
        vt_c = [[buf[:, 2 * u + m, :] for m in range(2)] for u in range(2)]
        tnt = [buf[:, 4, :], buf[:, 5, :]]

        sp2 = shared[:, 0:5 * NF * MED].rearrange("p (t n) -> p t n", t=5)
        sel = s_all[:, 0:4].rearrange("p (a b) c d -> p a (b c d)", a=2)
        sel_b = s_all[0:SIZE * FS - P, 4:8].rearrange("p (a b) c d -> p a (b c d)", a=2)

        def area(tensor, first_col):
            at = [first_col]

            def take(n):
                a = tensor[:, at[0]:at[0] + n]
                at[0] += n
                assert at[0] <= tensor.shape[1]
                return a
            return take

        vb = area(shared[:, :], 0)
        sw_c, prod, cross = ([vb(512), vb(512)] for _ in range(3))
        u_c, y_c = ([[vb(512), vb(512)] for _ in range(2)] for _ in range(2))
        star_area = star[:].rearrange("p a b n -> p (a b n)")
        spec_area = spec[:].rearrange("p a b n -> p (a b n)")
        st = area(star_area, 0)
        w1s = st(E * HID)
        w3s = st(E * HID)
        oh_s = [st(P) for _ in range(4)]
        oh_j = [st(P) for _ in range(4)]
        q_one, q_tot = st(E * TILES), st(E * TILES)
        q = area(spec_area, 0)
        w2s = q(HC * E * DIM).rearrange("p (c n) -> p c n", c=HC)
        q_rev, q_eq, q_val, q_l2, q_cnt, q_incl, q_slot, q_sel = (q(TILES * E) for _ in range(8))
        q_oh = [q(TILES * E), q(TILES * E)]
        q_m = [q(TILES), q(TILES)]
        q_c, q_diff, q_exp, q_den = (q(TILES) for _ in range(4))
        q_cpad, q_pend, q_base, q_tmp = (q(E) for _ in range(4))
        q_pos, q_low, q_high, q_id1 = (q(2 * TILES) for _ in range(4))
        q_trash, q_v, q_inv, q_digit, q_power = (q(SLOT_TILES) for _ in range(5))
        q_row = q(P)
        q_jtok, q_jcmp = q(E * SLOT_TILES), q(E * SLOT_TILES)
        ff = area(shared[:, :], 0)
        xg, yo = ([ff(P) for _ in range(BUFS)] for _ in range(2))
        xgt = [[xgt_hl[:, u, h] for h in range(2)] for u in range(2)]
        silu, hid, hidt = ([ff(HID), ff(HID)] for _ in range(3))
        w1_hl = (RS[:].rearrange("p c g b m -> p (c g b m)")[:, 0:E * HID], w_lo[:, 0:E * HID])
        w3_hl = (w3_hi[:, :], w_lo[:, E * HID:2 * E * HID])
        cc = area(star_area, 0)
        ya, yb = ([cc(512) for _ in range(4)] for _ in range(2))

        bank = [ctx.enter_context(nc.psum_tensor(f"bank{n}", [P, 512], F32)) for n in range(8)]
        ps_tr, ps_r, ps_pw, ps_x, ps_conv = bank[0], bank[1], bank[2:4], bank[4:6], bank[6:8]
        ps_w, ps_v, ps_y = bank[0:3], (bank[3:5], bank[5:7]), bank[7]
        ps_tot, ps_rank, ps_idx = bank[0], bank[1], bank[2]
        p_x, p_y, p_h1, p_h3, p_ht = bank[0], bank[1], bank[2:4], bank[4:6], bank[6:8]

        S = {n: ctx.enter_context(nc.semaphore(n)) for n in (
            "consts_in tab_in x_in0 x_in1 x_in2 x_in3 route_in w1_in w3_in w2_in w_hi w_lo pad_zero coef_zero mhalf_set coef_ps "
            "coef_hi coef_lo coef_in a_stats a_aggr a_eps a_rstd a_norm a_tr a_xc a_xp a_pw a_conv a_rw1 a_relu_s "
            "a_relu_r a_rw2 a_rsum a_rows a_relu a_sq a_star a_fold a_dft a_spec r_cols r_full r_taps r_mm "
            "r_log r_max r_sub r_exp r_sum r_rec r_norm r_tr r_hi r_lo r_rows b_w b_sw b_p b_cross b_u b_y "
            "b_vt b_vts b_w2 b_t b_stats b_aggr b_eps b_rstd b_norm b_tn0 b_tn1 b_tr b_tnt "
            "b_gate b_logit q_iota q_tri q_dve q_ready q_exp_done q_count q_ranks q_oh_ready q_oh_used q_idx_done "
            "q_tables g_idx s_idx f_tr f_xh f_xt f_h f_silu f_act f_ht f_hts f_y f_ys "
            "c_in0 c_in1 c_in2 c_in3 rs_zero k_zero w_zero r_cat c_sum c_done out_sent").split()}
        S.update({f"{n}{b}": ctx.enter_context(nc.semaphore(f"{n}{b}")) for n in ("g_x", "y_out") for b in range(BUFS)})

        def star_at(j, i):
            return flat(star[:, j, ds(i, 1), :])

        def spec_at(lo, hi, e, i):
            return flat(spec[lo:hi, e, ds(i, 1), :])

        def tokens(i):
            return T[:, ds(i * 4, 4), :]

        block = ctx.enter_context(nc.Block())

        @block.sync
        def _(sp):
            x_tiles = io["x"].rearrange("(t p) c -> p t c", p=P)
            for c in range(4):
                sp.dma_start(T[:, 8 * c:8 * c + 8, :], x_tiles[:, 8 * c:8 * c + 8, :]).then_inc(S[f"x_in{c}"], 16)
                if c == 0:
                    for dst, name in ((ident, "ident"), (wp1, "wp1"), (sp1, "sp1"), (rw1, "rw1"), (fwd, "fwd")):
                        sp.dma_start(dst[:], io[name]).then_inc(S["consts_in"], 16)
                    for g in range(2):
                        for dst, name in ((sp1_b, "sp1_b"), (rw1_b, "rw1_b"), (rwc_b, "rwc_b")):
                            sp.dma_start(dst[HALF * g:HALF * g + HALF], io[name]).then_inc(S["consts_in"], 16)
                    sp.wait_ge(S["w_zero"], 3)
                    for g in range(2):
                        sp.dma_start(rwc[HALF * g:HALF * g + HALF, HALF * g:HALF * g + HALF], io["rwc"])\
                            .then_inc(S["consts_in"], 16)
                    for dst, name in ((star_s, "star_s"), (star_b, "star_b")):
                        sp.dma_start(dst[:, :], io[name].partition_broadcast(P)).then_inc(S["consts_in"], 16)
            for dst, name in ((inv, "inv"), (wp2, "wp2"), (route_b, "route_b"),
                              (sw_rows, "sw_rows"), (cw_a, "cw_a"), (cw_b, "cw_b")):
                sp.dma_start(dst[:], io[name]).then_inc(S["tab_in"], 16)
            sp.dma_start(gate[:, 0:E], io["gate"]).then_inc(S["tab_in"], 16)
            sp.dma_start(sel, io["sel_a"]).then_inc(S["tab_in"], 16)
            sp.dma_start(sel_b, io["sel_b"]).then_inc(S["tab_in"], 16)
            sp.dma_start(sp2[0:HALF, 0:5], io["sp2_even"]).then_inc(S["route_in"], 16)
            sp.dma_start(sp2[HALF:P, 0:4], io["sp2_odd"]).then_inc(S["route_in"], 16)
            for g in range(2):
                sp.dma_start(rw2[HALF * g:HALF * g + HALF], io["rw2"]).then_inc(S["route_in"], 16)
            sp.wait_ge(S["coef_zero"], 1)
            sp.wait_ge(S["coef_hi"], 2)
            sp.wait_ge(S["coef_lo"], 2)
            for r in range(4):
                sp.dma_start(coef[4 * r:4 * r + 4, 0:4, :].bitcast(F32), coef_hl[:, r // 2, 0:4 * P].rearrange(
                    "f (c k) -> f c k", c=4).bitcast(F32)).then_inc(S["coef_in"], 16)
                sp.dma_start(coef[16 + 4 * r:20 + 4 * r, 4:6, :].bitcast(F32), coef_hl[:, r // 2, 4 * P:4 * P + PIX].rearrange(
                    "f (c k) -> f c k", c=2).bitcast(F32)).then_inc(S["coef_in"], 16)
            sp.wait_ge(S["r_hi"], 1)
            sp.wait_ge(S["r_lo"], 1)
            sp.wait_ge(S["rs_zero"], 1)
            for kind in range(2):
                for r in range(4):
                    row = 16 * (1 - kind) + 4 * r
                    sp.dma_start(RS[row:row + 4].rearrange("f c g b m -> f (c g b) m").bitcast(F32),
                                 r_hl[:, r % 2, kind, :].bitcast(F32))\
                        .then_inc(S["r_rows"], 16)

            def store_tn(i, u):
                sp.wait_ge(S["b_norm"], i + 1)
                sp.dma_start(tn_dram[ds(i * (4 * P), 4 * P), :].rearrange("(q p) d -> p q d", p=P),
                             xn[:, u, :, :]).then_inc(S[f"b_tn{u}"], 16)
            pair_loop(sp, store_tn)
            sp.wait_ge(S["b_u"], 2 * PAIRS)
            sp.dma_start(w1s, io["w1"]).then_inc(S["w1_in"], 16)
            sp.dma_start(w3s, io["w3"]).then_inc(S["w3_in"], 16)
            sp.wait_ge(S["b_cross"], 2 * PAIRS)
            sp.dma_start(w2s, io["w2"]).then_inc(S["w2_in"], 16)

            for b in range(BUFS):
                sp.wait_ge(S[f"y_out{b}"], 16 * (SLOT_TILES // BUFS))
            y_tok = y_dram[0:2 * NTOK, :].rearrange("(k t p) d -> k p t d", k=2, p=P)
            for i in range(PAIRS):
                u = i % 4
                wait_done(sp, S["c_done"], i - 3)
                sp.dma_start(ya[u].rearrange("p (t d) -> p t d", t=4), y_tok[0, :, 4 * i:4 * i + 4, :])\
                    .then_inc(S[f"c_in{u}"], 16)
                sp.dma_start(yb[u].rearrange("p (t d) -> p t d", t=4), y_tok[1, :, 4 * i:4 * i + 4, :])\
                    .then_inc(S[f"c_in{u}"], 16)

        @block.gpsimd
        def _(pool):
            pool.memset(rwc[:, :], 0.0).then_inc(S["w_zero"], 1)
            pool.memset(gate[:, :], 0.0).then_inc(S["w_zero"], 1)
            pool.memset(sp2[:, 4], 0.0).then_inc(S["w_zero"], 1)
            pool.memset(mhalf[:, :], -0.5).then_inc(S["mhalf_set"], 1)
            pool.memset(xp[:].rearrange("p u g a b -> p (u g a b)"), 0.0).then_inc(S["pad_zero"], 1)
            pool.memset(coef[:].rearrange("p c k -> p (c k)").bitcast(F32), 0.0).then_inc(S["coef_zero"], 1)
            pool.memset(ones[:, :], 1.0).then_inc(S["q_tri"], 1)
            pool.memset(tri[:, :], 1.0).then_inc(S["q_tri"], 1)
            pool.wait_ge(S["q_tri"], 2)
            pool.affine_select(out=tri[:, :], in_=tri[:, :], compare_op=ALU.is_gt, fill=0.0, base=0,
                               pattern=[[1, P]], channel_multiplier=-1).then_inc(S["q_tri"], 1)
            pool.memset(RS[:].rearrange("p c g b m -> p (c g b m)").bitcast(F32), 0.0).then_inc(S["rs_zero"], 1)
            pool.memset(tap_k[:].rearrange("p t b -> p (t b)"), 0.0).then_inc(S["k_zero"], 1)
            pool.memset(rw_k[:, :], 0.0).then_inc(S["k_zero"], 1)
            pool.wait_ge(S["mhalf_set"], 1)

            def inv_std(aggr, added, done, eps, i, u):
                wait_apart(pool, S[aggr], i + 1)
                pool.tensor_scalar(var_eps[:, u, :], mv[:, u, :, 1], eps, None, ALU.add).then_inc(S[added], 1)
                wait_apart(pool, S[added], i + 1)
                pool.tensor_tensor(rstd[:, u, :], var_eps[:, u, :], mhalf[:, :], ALU.pow).then_inc(S[done], 1)

            def border(i, u):
                wait_apart(pool, S["a_xc"], i + 1)
                wait_done(pool, S["a_conv"], i - 1)
                pool.tensor_copy(xp[:, u, :, 1:SIZE + 1, 1:SIZE + 1],
                                 xc[:, u, :].rearrange("p (g a b) -> p g a b", g=2, a=SIZE)).then_inc(S["a_xp"], 1)

            def phase_a(i, u):
                if not last(i, PAIRS):
                    inv_std("a_aggr", "a_eps", "a_rstd", LN_C_EPS, i + 1, 1 - u)
                pool.wait_ge(S["a_star"], i * 2 + 2)
                wait_done(pool, S["a_dft"], i * 2 - 2)
                pool.tensor_tensor(fold[u][0], star_at(0, i), star_at(1, i), ALU.add).then_inc(S["a_fold"], 1)
                pool.tensor_tensor(fold[u][1], star_at(0, i), star_at(1, i), ALU.subtract)\
                    .then_inc(S["a_fold"], 1)
                if not last(i, PAIRS):
                    border(i + 1, 1 - u)
            inv_std("a_aggr", "a_eps", "a_rstd", LN_C_EPS, 0, 0)
            pool.wait_ge(S["pad_zero"], 1)
            border(0, 0)
            pair_loop(pool, phase_a)

            def spatial(i, u):
                for j in range(2):
                    pool.wait_ge(S["b_sw"], i * 2 + j + 1)
                    wait_done(pool, S["b_vt"], i * 2 - 2)
                    pool.tensor_tensor(u_c[u][j], star_at(j, i), sw_c[j], ALU.mult).then_inc(S["b_u"], 1)

            def spectral(i, u):
                for e in range(2):
                    pool.wait_ge(S["b_cross"], i * 2 + e + 1)
                    wait_done(pool, S["b_vt"], i * 2 - 2)
                    pool.tensor_tensor(y_c[u][e], prod[e], cross[e], ALU.add).then_inc(S["b_y"], 1)

            def phase_b(i, u):
                if not last(i, PAIRS):
                    spatial(i + 1, 1 - u)
                if not first(i):
                    inv_std("b_aggr", "b_eps", "b_rstd", LN_T_EPS, i - 1, 1 - u)
                if not last(i, PAIRS):
                    spectral(i + 1, 1 - u)
            spatial(0, 0)
            spectral(0, 0)
            filter_loop(pool, phase_b)
            inv_std("b_aggr", "b_eps", "b_rstd", LN_T_EPS, PAIRS - 1, 1)

            for ap, pat, base, cm in (
                    (q_rev.rearrange("p (t e) -> p t e", e=E), [[0, TILES], [-1, E]], E, 0),
                    (q_id1.rearrange("p (k t) -> p k t", k=2), [[NTOK, 2], [P, TILES]], 1, 1),
                    (q_row, [[1, P]], 0, 0),
                    (q_trash, [[P, SLOT_TILES]], 2 * NTOK + 1, 1),
                    (q_jtok.rearrange("p (e j) -> p e j", e=E), [[0, E], [P, SLOT_TILES]], 0, 0)):
                pool.iota(ap, pat, base=base, channel_multiplier=cm,
                          allow_small_or_imprecise_dtypes=True).then_inc(S["q_iota"], 1)
            pool.memset(q_one, 1.0).then_inc(S["q_iota"], 1)
            for b in range(BUFS):
                pool.memset(q_power[:, b::BUFS], float(E ** b)).then_inc(S["q_iota"], 1)

            for n, (w, hl) in enumerate(((w1s, w1_hl), (w3s, w3_hl))):
                pool.wait_ge(S["w_hi"], n + 1)
                pool.tensor_tensor(hl[1], w, hl[0].bitcast(F32), ALU.subtract).then_inc(S["w_lo"], 1)

            pool.wait_ge(S["q_tables"], 1)
            for u in range(2):
                pool.wait_ge(S[f"b_tn{u}"], 16 * (PAIRS // 2))

            def gather(j, b):
                quad, col = b // 4, b % 4
                wait_apart(pool, S["f_tr"], j - BUFS + 1 if col else j - 4)
                if col == 0:
                    pool.tensor_copy(idx_g[quad][:, :], idx_gather[:, ds(j, 4)]).then_inc(S["g_idx"], 4)
                    wait_apart(pool, S["g_idx"], j + 4)
                pool.indirect_dma_start(xg[b], None, tn_dram, bass.IndirectOffsetOnAxis(
                    ap=idx_g[quad][:, col:col + 1], axis=0)).then_inc(S[f"g_x{b}"], 16)

            def scatter(j, b):
                wait_apart(pool, S["f_ys"], j + 1)
                quad, col = b // 4, b % 4
                if col == 0:
                    pool.tensor_copy(idx_s[quad][:, :], idx_scatter[:, ds(j, 4)]).then_inc(S["s_idx"], 4)
                    wait_apart(pool, S["s_idx"], j + 4)
                pool.indirect_dma_start(y_dram, bass.IndirectOffsetOnAxis(ap=idx_s[quad][:, col:col + 1], axis=0),
                                        yo[b], None).then_inc(S[f"y_out{b}"], 16)

            for b in range(AHEAD):
                gather(b, b)

            def step(j, b):
                if not isinstance(j, int) or j + AHEAD < SLOT_TILES:
                    gather(j + AHEAD, (b + AHEAD) % BUFS)
                if not isinstance(j, int) or j >= 2:
                    scatter(j - 2, (b - 2) % BUFS)
            tile_loop(pool, step)
            scatter(SLOT_TILES - 2, BUFS - 2)
            scatter(SLOT_TILES - 1, BUFS - 1)

        @block.scalar
        def _(act):
            act.wait_ge(S["coef_ps"], 1)
            act.activation(coef_hl[:, 0, 0:4 * P], ps_conv[1][0:NF, :], ACT.Copy).then_inc(S["coef_hi"], 1)
            act.activation(coef_hl[:, 0, 4 * P:4 * P + PIX], sw_rows[:, :], ACT.Copy).then_inc(S["coef_hi"], 1)
            act.wait_ge(S["consts_in"], 16 * 15)

            def image(i, u):
                act.wait_ge(S["a_tr"], i + 1)
                wait_done(act, S["a_rw1"], i - 1)
                wait_done(act, S["a_xp"], i - 1)
                act.activation(xc[:, u, :], ps_tr[:, :], ACT.Copy).then_inc(S["a_xc"], 1)

            def phase_a(i, u):
                for j in range(2):
                    act.wait_ge(S["a_pw"], i * 2 + j + 1)
                    act.activation(relu_x[:, j, :], ps_pw[j][:, :], ACT.Relu).then_inc(S["a_relu"], 1)
                for j in range(2):
                    act.wait_ge(S["a_relu"], i * 2 + j + 1)
                    wait_done(act, S["a_star"], i * 2 + j - 1)
                    act.activation(sq_x[:, j, :], relu_x[:, j, :], ACT.Square).then_inc(S["a_sq"], 1)
                act.wait_ge(S["a_conv"], i + 1)
                act.activation(s_all[:, ds(i, 1), :, :].rearrange("p o a b -> p (o a b)"), ps_conv[u][:, 0:PIX],
                               ACT.Relu, bias=sp1_b[:, 0:1]).then_inc(S["a_relu_s"], 1)
                act.wait_ge(S["a_rw1"], i + 1)
                act.activation(r1[:, :], ps_r[:, 0:PIX], ACT.Relu, bias=rw1_b[:, 0:1]).then_inc(S["a_relu_r"], 1)
                if not last(i, PAIRS):
                    image(i + 1, 1 - u)
                act.wait_ge(S["a_rw2"], i + 1)
                act.activation(r2[:, :], ps_r[:, 0:PIX], ACT.Relu, bias=rwc_b[:, 0:1],
                               accum_out=rsum[:, ds(i, 1)]).then_inc(S["a_rsum"], 1)
            image(0, 0)
            pair_loop(act, phase_a)

            act.wait_ge(S["r_sub"], 1)
            lg_flat = lg[:].rearrange("p s f c b -> p (s f c b)")
            act.activation(lg_flat, lg_flat, ACT.Exp).then_inc(S["r_exp"], 1)
            act.wait_ge(S["r_tr"], 1)
            act.activation(r_hl[:, 0, :, :].rearrange("p s m -> p (s m)"), ps_tr[:, 0:2 * P], ACT.Copy)\
                .then_inc(S["r_hi"], 1)

            def spatial(i):
                for j in range(2):
                    act.wait_ge(S["b_w"], i * 6 + j + 1)
                    wait_done(act, S["b_u"], i * 2 + j - 1)
                    act.activation(sw_c[j], ps_w[j][:, :], ACT.Copy).then_inc(S["b_sw"], 1)

            def branch_copy(i, u, m):
                act.wait_ge(S["b_vt"], i * 2 + m + 1)
                wait_done(act, S["b_w2"], i - 1)
                act.activation(vt_c[u][m], ps_v[u][m][:, :], ACT.Copy).then_inc(S["b_vts"], 1)

            def gate_copy(i, u):
                act.wait_ge(S["b_tr"], i + 1)
                wait_done(act, S["b_gate"], i - 1)
                act.activation(tnt[u], ps_v[1 - u][0][:, :], ACT.Copy).then_inc(S["b_tnt"], 1)

            def phase_b(i, u):
                if not last(i, PAIRS):
                    spatial(i + 1)
                branch_copy(i, u, 0)
                if not isinstance(i, int) or i >= 2:
                    gate_copy(i - 2, u)
                branch_copy(i, u, 1)
            spatial(0)
            filter_loop(act, phase_b)
            for i in range(PAIRS - 2, PAIRS):
                gate_copy(i, i % 2)

            act.wait_ge(S["q_ready"], 1)
            act.activation(q_exp, q_diff, ACT.Exp).then_inc(S["q_exp_done"], 1)

            for n, (w_in, w, hl) in enumerate((("w1_in", w1s, w1_hl), ("w3_in", w3s, w3_hl))):
                act.wait_ge(S[w_in], 16)
                if n == 0:
                    act.wait_ge(S["b_w"], 6 * PAIRS)
                else:
                    act.wait_ge(S["b_gate"], PAIRS)
                act.activation(hl[0], w, ACT.Copy).then_inc(S["w_hi"], 1)

            def x_high(j, u):
                act.wait_ge(S["f_tr"], j + 1)
                wait_done(act, S["f_h"], j - 1)
                act.activation(xgt[u][0], p_x[:, 0:P], ACT.Copy).then_inc(S["f_xh"], 1)

            def hidden_copy(j, u):
                act.wait_ge(S["f_ht"], j + 1)
                wait_done(act, S["f_y"], j - 1)
                act.activation(hidt[u], p_ht[u][:, 0:HID], ACT.Copy).then_inc(S["f_hts"], 1)

            def step(j, u):
                if not last(j, SLOT_TILES):
                    x_high(j + 1, 1 - u)
                act.wait_ge(S["f_h"], j + 1)
                wait_done(act, S["f_act"], j - 1)
                act.activation(silu[u], p_h1[u][:, 0:HID], ACT.Silu).then_inc(S["f_silu"], 1)
                if not first(j):
                    hidden_copy(j - 1, 1 - u)
            x_high(0, 0)
            tile_loop(act, lambda j, b: step(j, b % 2))
            hidden_copy(SLOT_TILES - 1, 1)

            out_tiles = io["out"].rearrange("(t p) d -> p t d", p=P)
            for i in range(PAIRS):
                act.wait_ge(S["c_done"], i + 1)
                act.dma_start(out_tiles[:, 4 * i:4 * i + 4, :], T[:, 4 * i:4 * i + 4, :]).then_inc(S["out_sent"], 16)
            act.wait_ge(S["out_sent"], 16 * PAIRS)

        @block.tensor
        def _(pe):
            pe.wait_ge(S["tab_in"], 16 * 9)
            n = 0
            for part in range(2):
                for cw, table in ((cw_a, sel), (cw_b, sel_b)):
                    mm = pe.matmul(ps_conv[1][0:NF, :], cw[:, :, part], table[:, part, :], start=(n == 0), stop=(n == 3))
                    n += 1
            mm.then_inc(S["coef_ps"], 1)
            pe.wait_ge(S["consts_in"], 16 * 15)
            pe.wait_ge(S["coef_lo"], 2)

            def transposes(i, u):
                pe.wait_ge(S["a_norm"], i + 1)
                wait_done(pe, S["a_xc"], i)
                for t in range(4):
                    mm = pe.transpose(ps_tr[:, t * P:(t + 1) * P], xn[:, u, t, :], ident[:, :])
                mm.then_inc(S["a_tr"], 1)

            def phase_a(i, u):
                pe.wait_ge(S["a_xc"], i + 1)
                for j in range(2):
                    wait_done(pe, S["a_relu"], i * 2 + j - 1)
                    for g in range(2):
                        mm = pe.matmul(ps_pw[j][:, g * MED:(g + 1) * MED],
                                       xc[:, u, (2 * g + j) * P:(2 * g + j + 1) * P], wp1[:, :], start=True, stop=True)
                    mm.then_inc(S["a_pw"], 1)
                wait_done(pe, S["a_relu_s"], i - 1)
                pe.wait_ge(S["a_xp"], i + 1)
                for t in range(TAPS):
                    for g in range(2):
                        mm = pe.matmul(ps_conv[u][HALF * g:HALF * g + HALF, 0:PIX], sp1[:, t, :],
                                       xp[:, u, g, t // 3:t // 3 + SIZE, t % 3:t % 3 + SIZE],
                                       start=(t == 0), stop=(t == TAPS - 1))
                mm.then_inc(S["a_conv"], 1)
                wait_done(pe, S["a_rsum"], i)
                for g in range(2):
                    mm = pe.matmul(ps_r[HALF * g:HALF * g + HALF, 0:PIX], rw1[:, :],
                                   xc[:, u, g * PIX:(g + 1) * PIX], start=True, stop=True)
                mm.then_inc(S["a_rw1"], 1)
                if not last(i, PAIRS):
                    transposes(i + 1, 1 - u)
                pe.wait_ge(S["a_relu_r"], i + 1)
                pe.matmul(ps_r[:, 0:PIX], rwc[:, :], r1[:, :], start=True, stop=True).then_inc(S["a_rw2"], 1)
                for e in range(2):
                    pe.wait_ge(S["a_fold"], i * 2 + e + 1)
                    wait_done(pe, S["a_spec"], i * 2 + e - 1)
                    pe.matmul(ps_x[e][:, :], fwd[:, e, :], fold[u][e], start=True, stop=True).then_inc(S["a_dft"], 1)
            transposes(0, 0)
            pair_loop(pe, phase_a)

            pe.wait_ge(S["route_in"], 64)
            pe.wait_ge(S["w_zero"], 3)
            pe.wait_ge(S["r_cat"], 6)
            pe.wait_ge(S["a_relu"], 2 * PAIRS)
            pe.wait_ge(S["a_relu_s"], PAIRS)
            for k in range(2 * NF):
                block_k = slice(k % 4 * P, (k % 4 + 1) * P)
                for t in range(5):
                    pe.matmul(ps_conv[k // 4][:, block_k], sp2[:, t, k * P:(k + 1) * P], tap_k[:, t, :],
                              start=(t == 0), stop=(t == 4))
                mm = pe.matmul(ps_pw[k // 4][:, block_k], rw2[:, k * P:(k + 1) * P], rw_k[:, :], start=True, stop=True)
            mm.then_inc(S["r_mm"], 1)
            pe.wait_ge(S["r_norm"], 1)
            for s in range(2):
                mm = pe.transpose(ps_tr[:, s * P:(s + 1) * P], lg[:, s].rearrange("p f c b -> p (f c b)"),
                                  ident[:, :])
            mm.then_inc(S["r_tr"], 1)
            pe.wait_ge(S["coef_in"], 16 * 8)
            pe.wait_ge(S["r_rows"], 16 * 8)
            pe.wait_ge(S["a_spec"], 2 * PAIRS)

            ring = (4, 5, 0, 2, 1, 3)

            def filters(i, order):
                free = ((("b_cross", i * 2 - 1),), (("b_p", i * 2),), (("b_cross", i * 2),),
                        (("b_sw", i * 2 + 1),), (("b_sw", i * 2 + 2),), (("b_p", i * 2 + 1),))
                for n in order:
                    for name, count in free[n]:
                        wait_done(pe, S[name], count)
                    pe.matmul(ps_w[n % 3][:, :], coef[:, ring[n], :],
                              RS[:, :, :, ds(i, 1), :].rearrange("r c g b m -> r g c (b m)"), start=True, stop=True)\
                        .then_inc(S["b_w"], 1)

            def branch(i, u, m):
                pe.wait_ge(S["b_u"], i * 2 + 2)
                if not isinstance(i, int) or i >= 3:
                    if m == 0:
                        pe.wait_ge(S["b_tnt"], i - 2)
                    else:
                        pe.wait_ge(S["b_logit"], i - 2)
                wait_done(pe, S["b_vts"], i * 2 - 3 + m)
                for g in range(2):
                    for j in range(2):
                        pe.matmul(ps_v[u][m][:, (2 * g + j) * P:(2 * g + j + 1) * P],
                                  u_c[u][j][:, g * MED + m * P:g * MED + (m + 1) * P], ident[:, :],
                                  start=(g == 0 and j == 0), stop=False)
                pe.wait_ge(S["b_y"], i * 2 + 2)
                for e in range(2):
                    for g in range(2):
                        mm = pe.matmul(ps_v[u][m][:, g * PIX:(g + 1) * PIX],
                                       y_c[u][e][:, g * MED + m * P:g * MED + (m + 1) * P], inv[:, e, :],
                                       start=False, stop=(e == 1 and g == 1))
                mm.then_inc(S["b_vt"], 1)

            def project(i, u):
                pe.wait_ge(S["b_vts"], i * 2 + 2)
                wait_done(pe, S["b_t"], i)
                for t in range(4):
                    for m in range(2):
                        mm = pe.matmul(ps_y[:, t * P:(t + 1) * P], vt_c[u][m][:, t * P:(t + 1) * P], wp2[:, m, :],
                                       start=(m == 0), stop=(m == 1))
                mm.then_inc(S["b_w2"], 1)

            def turn_tokens(i, u):
                pe.wait_ge(S["b_norm"], i + 1)
                wait_done(pe, S["b_vts"], min(2 * PAIRS, i * 2 + 4) if isinstance(i, int) else i * 2 + 4)
                for t in range(4):
                    mm = pe.transpose(ps_v[1 - u][0][:, t * P:(t + 1) * P], xn[:, u, t, :], ident[:, :])
                mm.then_inc(S["b_tr"], 1)

            def gating(i, u):
                pe.wait_ge(S["b_tnt"], i + 1)
                for t in range(4):
                    mm = pe.matmul(ps_v[1 - u][1][:, t * P:(t + 1) * P], tnt[u][:, t * P:(t + 1) * P], gate[:, :],
                                   start=True, stop=True)
                mm.then_inc(S["b_gate"], 1)

            def phase_b(i, u):
                lagging = not isinstance(i, int) or i >= 2
                if not last(i, PAIRS):
                    filters(i + 1, (0, 1, 2))
                if not first(i):
                    project(i - 1, 1 - u)
                if not last(i, PAIRS):
                    filters(i + 1, (3, 4))
                branch(i, u, 0)
                if lagging:
                    turn_tokens(i - 2, u)
                if not last(i, PAIRS):
                    filters(i + 1, (5,))
                branch(i, u, 1)
                if lagging:
                    gating(i - 2, u)
            filters(0, range(6))
            filter_loop(pe, phase_b)
            project(PAIRS - 1, 1)
            for i in range(PAIRS - 2, PAIRS):
                turn_tokens(i, i % 2)
                gating(i, i % 2)

            pe.wait_ge(S["q_tri"], 3)
            pe.wait_ge(S["q_ready"], 2)
            counts = q_cnt.rearrange("p (t e) -> p e t", e=E)
            pe.matmul(ps_tot[:, 0:E * TILES], ones[:, :], counts, start=True, stop=True).then_inc(S["q_count"], 1)
            pe.matmul(ps_rank[:, 0:E * TILES], tri[:, :], counts, start=True, stop=True).then_inc(S["q_count"], 1)

            def place(n, b):
                pe.wait_ge(S["q_oh_ready"], n + 1)
                pe.matmul(ps_idx[:, 0:P], oh_s[b], oh_j[b], start=first(n), stop=last(n, 2 * TILES))\
                    .then_inc(S["q_oh_used"], 1)
            for b in range(4):
                place(b, b)
            with pe.Fori(1, TILES // 2 - 1) as n:
                for b in range(4):
                    place(n * 4 + b, b)
            for b in range(4):
                place(2 * TILES - 4 + b, b)

            pe.wait_ge(S["w_hi"], 2)
            pe.wait_ge(S["w_lo"], 2)
            pe.wait_ge(S["w2_in"], 16)
            pe.wait_ge(S["q_tables"], 1)

            def transpose_x(j, b):
                pe.wait_ge(S[f"g_x{b}"], (j - b) * (16 // BUFS) + 16)
                wait_done(pe, S["f_xt"], j)
                pe.transpose(p_x[:, 0:P], xg[b], ident[:, :]).then_inc(S["f_tr"], 1)

            def turn(j, u):
                pe.wait_ge(S["f_act"], j + 1)
                wait_done(pe, S["f_hts"], j - 1)
                for c in range(HC):
                    mm = pe.transpose(p_ht[u][:, c * P:(c + 1) * P], hid[u][:, c * P:(c + 1) * P], ident[:, :])
                mm.then_inc(S["f_ht"], 1)

            def experts_of(n):
                word = pe.value_load(tile_experts[0:1, ds(n, 1)], min_val=0, max_val=E ** BUFS - 1)
                return [(word // E ** k) % E for k in range(BUFS)]

            def down(j, u, e):
                pe.wait_ge(S["f_hts"], j + 1)
                wait_done(pe, S["f_ys"], j)
                for c in range(HC):
                    mm = pe.matmul(p_y[:, 0:DIM], hidt[u][:, c * P:(c + 1) * P], w2s[:, c, ds(e * DIM, DIM)],
                                   start=(c == 0), stop=(c == HC - 1))
                mm.then_inc(S["f_y"], 1)

            def step(j, b):
                u = b % 2
                if not last(j, SLOT_TILES):
                    transpose_x(j + 1, (b + 1) % BUFS)
                if b == 0:
                    n = j // BUFS
                    before[:] = experts_of(n - 1)[-2:] if not first(j) else []
                    held[:] = experts_of(n)
                cols = ds(held[b] * HID, HID)
                pe.wait_ge(S["f_xt"], j + 1)
                wait_done(pe, S["f_act"], j - 1)
                for n, (xs, ws) in enumerate(((0, 0), (0, 1), (1, 0))):
                    for psum, w_hl in ((p_h1[u], w1_hl), (p_h3[u], w3_hl)):
                        mm = pe.matmul(psum[:, 0:HID], xgt[u][xs], w_hl[ws][:, cols], start=(n == 0), stop=(n == 2))
                mm.then_inc(S["f_h"], 1)
                if not first(j):
                    turn(j - 1, 1 - u)
                if not isinstance(j, int) or j >= 2:
                    down(j - 2, u, held[b - 2] if b >= 2 else before[b])
            held, before = [], []
            transpose_x(0, 0)
            tile_loop(pe, step)
            turn(SLOT_TILES - 1, 1)
            down(SLOT_TILES - 2, 0, held[-2])
            down(SLOT_TILES - 1, 1, held[-1])

        @block.vector
        def _(dve):
            dve.wait_ge(S["coef_hi"], 2)
            dve.tensor_tensor(coef_hl[:, 1, 0:4 * P], ps_conv[1][0:NF, :], coef_hl[:, 0, 0:4 * P].bitcast(F32),
                              ALU.subtract).then_inc(S["coef_lo"], 1)
            dve.tensor_tensor(coef_hl[:, 1, 4 * P:4 * P + PIX], sw_rows[:, :],
                              coef_hl[:, 0, 4 * P:4 * P + PIX].bitcast(F32), ALU.subtract).then_inc(S["coef_lo"], 1)

            def stats(ph, i, u):
                for t in range(4):
                    op = dve.bn_stats(st6[:, u, t, :], flat(T[:, ds(i * 4 + t, 1), :]))
                op.then_inc(S[ph + "_stats"], 1)
                wait_apart(dve, S[ph + "_stats"], i + 1)
                for t in range(4):
                    op = dve.bn_aggr(mv[:, u, t, :], st6[:, u, t, :])
                op.then_inc(S[ph + "_aggr"], 1)

            def normalise(ph, i, u):
                dve.wait_ge(S[ph + "_rstd"], i + 1)
                for t in range(4):
                    op = dve.tensor_scalar(xn[:, u, t, :], flat(T[:, ds(i * 4 + t, 1), :]), mv[:, u, t, 0:1],
                                           rstd[:, u, t:t + 1], ALU.subtract, ALU.mult)
                op.then_inc(S[ph + "_norm"], 1)

            def phase_a(i, u):
                if isinstance(i, int) and i == 1:
                    for c in range(1, 4):
                        dve.wait_ge(S[f"x_in{c}"], 16)
                if not last(i, PAIRS):
                    stats("a", i + 1, 1 - u)
                for j in range(2):
                    dve.wait_ge(S["a_sq"], i * 2 + j + 1)
                    dve.tensor_scalar(star_at(j, i), sq_x[:, j, :], star_s[:, 0:1], star_b[:, 0:1], ALU.mult, ALU.add)\
                        .then_inc(S["a_star"], 1)
                if not last(i, PAIRS):
                    wait_done(dve, S["a_tr"], i)
                    normalise("a", i + 1, 1 - u)
                dve.wait_ge(S["a_relu_s"], i + 1)
                dve.tensor_reduce(rows[:, 1, ds(i, 1), :].rearrange("p o a -> p (o a)"),
                                  s_all[:, ds(i, 1), :, :].rearrange("p o a b -> p (o a) b"), AX.X, ALU.add)\
                    .then_inc(S["a_rows"], 1)
                for e in range(2):
                    dve.wait_ge(S["a_dft"], i * 2 + e + 1)
                    dve.tensor_copy(spec_at(0, P, e, i), ps_x[e][:, :]).then_inc(S["a_spec"], 1)
            dve.wait_ge(S["x_in0"], 16)
            dve.wait_ge(S["consts_in"], 16 * 15)
            stats("a", 0, 0)
            normalise("a", 0, 0)
            pair_loop(dve, phase_a)

            dve.wait_ge(S["a_rows"], PAIRS)
            dve.tensor_tensor(rows[:, 0], rows[:, 1], s_all[:, :, :, SIZE - 1], ALU.subtract).then_inc(S["r_cols"], 1)
            dve.tensor_tensor(rows[:, 2], rows[:, 1], s_all[:, :, :, 0], ALU.subtract).then_inc(S["r_cols"], 1)
            dve.wait_ge(S["r_cols"], 2)
            dve.tensor_reduce(tap_sum[:, 1], rows[:], AX.X, ALU.add).then_inc(S["r_full"], 1)
            dve.wait_ge(S["r_full"], 1)
            dve.tensor_tensor(tap_sum[:, 0], tap_sum[:, 1], rows[:, :, :, SIZE - 1], ALU.subtract)\
                .then_inc(S["r_taps"], 1)
            dve.tensor_tensor(tap_sum[:, 2], tap_sum[:, 1], rows[:, :, :, 0], ALU.subtract).then_inc(S["r_taps"], 1)
            dve.wait_ge(S["r_taps"], 2)
            dve.wait_ge(S["a_rsum"], PAIRS)
            dve.wait_ge(S["k_zero"], 2)
            taps = tap_sum[:].rearrange("p y x b -> p (y x) b")
            for g in range(2):
                half, cols = slice(HALF * g, HALF * g + HALF), slice(PAIRS * g, PAIRS * g + PAIRS)
                dve.tensor_copy(tap_k[0:HALF, 0:5, cols], taps[half, 0:TAPS:2, :]).then_inc(S["r_cat"], 1)
                dve.tensor_copy(tap_k[HALF:P, 0:4, cols], taps[half, 1:TAPS:2, :]).then_inc(S["r_cat"], 1)
                dve.tensor_copy(rw_k[half, cols], rsum[half, :]).then_inc(S["r_cat"], 1)
            dve.wait_ge(S["tab_in"], 16 * 9)
            dve.wait_ge(S["r_mm"], 1)
            for s, banks in ((0, ps_conv), (1, ps_pw)):
                for h in range(2):
                    dve.scalar_tensor_tensor(
                        out=lg[:, s].rearrange("p f c b -> p (f c) b")[:, 4 * h:4 * h + 4],
                        in0=banks[h][:, :].rearrange("p (k n) -> p k n", k=4)[:, :, 0:BATCH], scalar=1.0 / PIX,
                        in1=route_b[:, 8 * s + 4 * h:8 * s + 4 * h + 4].unsqueeze(2).to_broadcast([P, 4, BATCH]),
                        op0=ALU.mult, op1=ALU.add).then_inc(S["r_log"], 1)
            lg_f = lg[:].rearrange("p s f c b -> p s f (c b)")
            dve.wait_ge(S["r_log"], 4)
            dve.tensor_reduce(lmax[:, :, :], lg_f.rearrange("p s f r -> p s r f"), AX.X, ALU.max)\
                .then_inc(S["r_max"], 1)
            dve.wait_ge(S["r_max"], 1)
            dve.tensor_tensor(lg_f, lg_f, lmax[:, :, :].unsqueeze(2).to_broadcast([P, 2, NF, 32]), ALU.subtract)\
                .then_inc(S["r_sub"], 1)
            dve.wait_ge(S["r_exp"], 1)
            dve.tensor_reduce(lsum[:, :, :], lg_f.rearrange("p s f r -> p s r f"), AX.X, ALU.add)\
                .then_inc(S["r_sum"], 1)
            dve.wait_ge(S["r_sum"], 1)
            dve.reciprocal(lmax[:, :, :], lsum[:, :, :]).then_inc(S["r_rec"], 1)
            dve.wait_ge(S["r_rec"], 1)
            dve.tensor_tensor(lg_f, lg_f, lmax[:, :, :].unsqueeze(2).to_broadcast([P, 2, NF, 32]), ALU.mult)\
                .then_inc(S["r_norm"], 1)
            dve.wait_ge(S["r_hi"], 1)
            dve.tensor_tensor(r_hl[:, 1, :, :].rearrange("p s m -> p (s m)"), ps_tr[:, 0:2 * P],
                              r_hl[:, 0, :, :].rearrange("p s m -> p (s m)").bitcast(F32), ALU.subtract)\
                .then_inc(S["r_lo"], 1)

            def filter_products(i, e):
                n_p, n_s = (2, 3) if e == 0 else (4, 5)
                dve.wait_ge(S["b_w"], i * 6 + n_p + 1)
                wait_done(dve, S["b_y"], i * 2 + e - 1)
                dve.tensor_tensor(prod[e], spec_at(0, P, e, i), ps_w[n_p % 3][:, :], ALU.mult)\
                    .then_inc(S["b_p"], 1)
                dve.wait_ge(S["b_w"], i * 6 + n_s + 1)
                dve.tensor_tensor(cross[e][0:64], spec_at(64, P, e, i), ps_w[n_s % 3][0:64, :], ALU.mult)
                dve.tensor_tensor(cross[e][64:P], spec_at(0, 64, e, i), ps_w[n_s % 3][64:P, :], ALU.mult)\
                    .then_inc(S["b_cross"], 1)

            def residual(i, u):
                dve.wait_ge(S["b_w2"], i + 1)
                dve.tensor_tensor(tokens(i), tokens(i), ps_y[:, :].rearrange("p (t d) -> p t d", t=4), ALU.add)\
                    .then_inc(S["b_t"], 1)
                wait_apart(dve, S["b_t"], i + 1)
                stats("b", i, u)

            def normalise_tokens(i, u):
                wait_done(dve, S[f"b_tn{u}"], i * 8 - 8 * u)
                wait_done(dve, S["b_tr"], i - 1)
                normalise("b", i, u)

            def logit_copy(i, u):
                dve.wait_ge(S["b_gate"], i + 1)
                dve.tensor_copy(logits[:, ds(i * 4, 4), :],
                                ps_v[1 - u][1][:, :].rearrange("p (t e) -> p t e", t=4)[:, :, 0:E])\
                    .then_inc(S["b_logit"], 1)

            def phase_b(i, u):
                if not last(i, PAIRS):
                    filter_products(i + 1, 0)
                if not first(i):
                    residual(i - 1, 1 - u)
                if not last(i, PAIRS):
                    filter_products(i + 1, 1)
                if not first(i):
                    normalise_tokens(i - 1, 1 - u)
                if not isinstance(i, int) or i >= 2:
                    logit_copy(i - 2, u)
            filter_products(0, 0)
            filter_products(0, 1)
            filter_loop(dve, phase_b)
            residual(PAIRS - 1, 1)
            normalise_tokens(PAIRS - 1, 1)
            for i in range(PAIRS - 2, PAIRS):
                logit_copy(i, i % 2)

            done = [0]

            def then(op):
                done[0] += 1
                op.then_inc(S["q_dve"], 1)
                dve.wait_ge(S["q_dve"], done[0])

            def by_tile(a):
                return a.rearrange("p (t e) -> p t e", e=E)

            def over_experts(a):
                return a.unsqueeze(2).to_broadcast([P, TILES, E])

            dve.wait_ge(S["b_logit"], PAIRS)
            dve.wait_ge(S["q_iota"], 6 + BUFS)
            source = logits[:, :, :]
            for k in range(2):
                then(dve.tensor_reduce(q_m[k], source, AX.X, ALU.max))
                then(dve.tensor_tensor(by_tile(q_eq), source, over_experts(q_m[k]), ALU.is_equal))
                then(dve.tensor_tensor(q_val, q_eq, q_rev, ALU.mult))
                then(dve.tensor_reduce(q_c, by_tile(q_val), AX.X, ALU.max))
                then(dve.tensor_tensor(by_tile(q_oh[k]), by_tile(q_rev), over_experts(q_c), ALU.is_equal))
                if k == 0:
                    then(dve.scalar_tensor_tensor(out=by_tile(q_l2), in0=by_tile(q_oh[0]), scalar=-3.0e38, in1=source,
                                                  op0=ALU.mult, op1=ALU.add))
                    source = by_tile(q_l2)
            dve.tensor_tensor(q_diff, q_m[1], q_m[0], ALU.subtract).then_inc(S["q_ready"], 1)
            dve.tensor_tensor(q_cnt, q_oh[0], q_oh[1], ALU.add).then_inc(S["q_ready"], 1)
            dve.wait_ge(S["q_exp_done"], 1)
            then(dve.tensor_scalar(q_den, q_exp, 1.0, None, ALU.add))
            then(dve.reciprocal(mix[:, 0, :], q_den))
            then(dve.tensor_tensor(mix[:, 1, :], q_exp, mix[:, 0, :], ALU.mult))
            dve.wait_ge(S["q_count"], 2)
            then(dve.tensor_copy(q_tot, ps_tot[:, 0:E * TILES]))
            then(dve.tensor_tensor_scan(q_incl, q_one, q_tot, 0.0, ALU.mult, ALU.add))
            ends = q_incl.rearrange("p (e t) -> p e t", t=TILES)[:, :, TILES - 1]
            then(dve.tensor_copy(q_tmp, ends))
            then(dve.tensor_tensor(q_tmp[:, 1:E], ends[:, 1:E], ends[:, 0:E - 1], ALU.subtract))
            then(dve.tensor_scalar(q_e32[:, :], q_tmp, float(P - 1), None, ALU.add))
            then(dve.tensor_scalar(q_e32[:, :], q_e32[:, :], 7, 7, ALU.logical_shift_right, ALU.logical_shift_left))
            then(dve.tensor_copy(q_cpad, q_e32[:, :]))
            then(dve.tensor_tensor_scan(q_pend, q_one[:, 0:E], q_cpad, 0.0, ALU.mult, ALU.add))
            then(dve.tensor_tensor(q_base, q_pend, q_cpad, ALU.subtract))
            then(dve.tensor_tensor(q_base, q_base, ends, ALU.subtract))
            then(dve.tensor_tensor(q_base, q_base, q_tmp, ALU.add))
            then(dve.tensor_tensor(q_incl, q_incl, q_tot, ALU.subtract))
            then(dve.tensor_tensor(q_incl, q_incl, ps_rank[:, 0:E * TILES], ALU.add))
            then(dve.tensor_tensor(q_slot.rearrange("p (e t) -> p e t", t=TILES),
                                   q_incl.rearrange("p (e t) -> p e t", t=TILES),
                                   q_base.unsqueeze(2).to_broadcast([P, E, TILES]), ALU.add))
            for k in range(2):
                then(dve.tensor_tensor(by_tile(q_sel), by_tile(q_oh[k]), q_slot.rearrange("p (e t) -> p t e", t=TILES),
                                       ALU.mult))
                then(dve.tensor_reduce(q_pos[:, k * TILES:(k + 1) * TILES], by_tile(q_sel), AX.X, ALU.add))
            then(dve.tensor_copy(q_i32[:, :], q_pos))
            then(dve.tensor_scalar(q_i32b[:, :], q_i32[:, :], P - 1, None, ALU.bitwise_and))
            then(dve.tensor_copy(q_low, q_i32b[:, :]))
            then(dve.tensor_scalar(q_i32b[:, :], q_i32[:, :], 7, None, ALU.logical_shift_right))
            then(dve.tensor_copy(q_high, q_i32b[:, :]))

            def one_hot(n, b):
                wait_done(dve, S["q_oh_used"], n - 3)
                dve.tensor_scalar(oh_s[b], q_row, q_low[:, ds(n, 1)], None, ALU.is_equal)
                dve.tensor_scalar(oh_j[b], q_row, q_high[:, ds(n, 1)], q_id1[:, ds(n, 1)], ALU.is_equal, ALU.mult)\
                    .then_inc(S["q_oh_ready"], 1)
            for b in range(4):
                one_hot(b, b)
            with dve.Fori(1, TILES // 2 - 1) as n:
                for b in range(4):
                    one_hot(n * 4 + b, b)
            for b in range(4):
                one_hot(2 * TILES - 4 + b, b)
            then(dve.tensor_tensor(q_jcmp.rearrange("p (e j) -> p e j", e=E), q_jtok.rearrange("p (e j) -> p e j", e=E),
                                   q_pend.unsqueeze(2).to_broadcast([P, E, SLOT_TILES]), ALU.is_ge))
            then(dve.tensor_reduce(q_inv, q_jcmp.rearrange("p (e j) -> p j e", e=E), AX.X, ALU.add))
            then(dve.scalar_tensor_tensor(out=q_digit[0:1, :], in0=q_inv[0:1, :], scalar=float(E - 1),
                                          in1=q_power[0:1, :], op0=ALU.min, op1=ALU.mult))
            then(dve.tensor_reduce(q_v[0:1, 0:SLOT_TILES // BUFS], q_digit[0:1, :].rearrange("p (n b) -> p n b", b=BUFS),
                                   AX.X, ALU.add))
            then(dve.tensor_copy(tile_experts[0:1, :], q_v[0:1, 0:SLOT_TILES // BUFS]))
            dve.wait_ge(S["q_oh_used"], 2 * TILES)
            then(dve.tensor_copy(q_v, ps_idx[:, 0:SLOT_TILES]))
            then(dve.tensor_scalar(q_inv, q_v, 0.0, None, ALU.is_equal))
            then(dve.tensor_tensor(q_inv, q_inv, q_trash, ALU.mult))
            then(dve.tensor_tensor(q_v, q_v, q_inv, ALU.add))
            then(dve.tensor_scalar(idx_scatter[:, :], q_v, -1.0, None, ALU.add))
            dve.tensor_scalar(idx_gather[:, :], idx_scatter[:, :], NTOK - 1, None, ALU.bitwise_and)\
                .then_inc(S["q_tables"], 1)

            def x_low(j, u):
                dve.wait_ge(S["f_xh"], j + 1)
                wait_done(dve, S["f_h"], j - 1)
                dve.tensor_tensor(xgt[u][1], p_x[:, 0:P], xgt[u][0].bitcast(F32), ALU.subtract).then_inc(S["f_xt"], 1)

            def y_copy(j, b):
                dve.wait_ge(S["f_y"], j + 1)
                wait_done(dve, S[f"y_out{b}"], (j - b) * (16 // BUFS))
                dve.tensor_copy(yo[b], p_y[:, 0:DIM]).then_inc(S["f_ys"], 1)

            def step(j, b):
                u = b % 2
                if not last(j, SLOT_TILES):
                    x_low(j + 1, 1 - u)
                if not isinstance(j, int) or j >= 3:
                    y_copy(j - 3, (b - 3) % BUFS)
                dve.wait_ge(S["f_silu"], j + 1)
                wait_done(dve, S["f_ht"], j - 1)
                dve.tensor_tensor(hid[u], silu[u], p_h3[u][:, 0:HID], ALU.mult).then_inc(S["f_act"], 1)
            x_low(0, 0)
            tile_loop(dve, step)
            for j in range(SLOT_TILES - 3, SLOT_TILES):
                y_copy(j, j % BUFS)

            for i in range(PAIRS):
                u = i % 4
                dve.wait_ge(S[f"c_in{u}"], 32 * (i // 4 + 1))
                for k, y in enumerate((ya[u], yb[u])):
                    for t in range(4):
                        tile = T[:, 4 * i + t, :]
                        op = dve.scalar_tensor_tensor(out=tile, in0=y[:, t * DIM:(t + 1) * DIM],
                                                      scalar=mix[:, k, 4 * i + t:4 * i + t + 1], in1=tile,
                                                      op0=ALU.mult, op1=ALU.add)
                    if k == 0:
                        op.then_inc(S["c_sum"], 1)
                        dve.wait_ge(S["c_sum"], i + 1)
                op.then_inc(S["c_done"], 1)


def layouts(x, L0_conv_w_pw1, L0_conv_w_pw2, L0_conv_star_scale, L0_conv_star_bias, L0_conv_rw_fc1_w,
            L0_conv_rw_fc1_b, L0_conv_rw_conv_w, L0_conv_rw_conv_b, L0_conv_rw_fc2_w, L0_conv_rw_fc2_b,
            L0_conv_sp_fc1_w, L0_conv_sp_fc1_b, L0_conv_sp_fc2_w, L0_conv_sp_fc2_b, L0_conv_complex_weights,
            L0_conv_spatial_weights, L0_ffn_gate_w, L0_ffn_w1, L0_ffn_w3, L0_ffn_w2):
    c = np.ascontiguousarray
    forward, inverse, sel = fourier_tables()
    cw = L0_conv_complex_weights.reshape(SIZE * FS, NF, 2)
    route_b = np.stack([L0_conv_sp_fc2_b.reshape(NF, 2, P), L0_conv_rw_fc2_b.reshape(NF, 2, P)])
    return {
        "x": c(x.transpose(0, 2, 3, 1).reshape(NTOK, DIM)),
        "ident": np.eye(P, dtype=np.float32),
        "fwd": c(forward), "inv": c(inverse),
        "sel_a": c(sel[:P].reshape(P, 2, 4 * P)), "sel_b": c(sel[P:].reshape(SIZE * FS - P, 2, 4 * P)),
        "sp1": c(L0_conv_sp_fc1_w.transpose(1, 2, 3, 0).reshape(DIM, TAPS, HALF)),
        "rw1": c(L0_conv_rw_fc1_w[:, :, 0, 0].T),
        "rwc": c(L0_conv_rw_conv_w[:, :, 0, 0].T),
        "sp1_b": c(L0_conv_sp_fc1_b[:, None]), "rw1_b": c(L0_conv_rw_fc1_b[:, None]),
        "rwc_b": c(L0_conv_rw_conv_b[:, None]),
        "route_b": c(route_b.transpose(3, 0, 1, 2).reshape(P, 16)),
        "sp2_even": c(L0_conv_sp_fc2_w.transpose(1, 2, 3, 0).reshape(HALF, TAPS, NF * MED)[:, 0::2]),
        "sp2_odd": c(L0_conv_sp_fc2_w.transpose(1, 2, 3, 0).reshape(HALF, TAPS, NF * MED)[:, 1::2]),
        "rw2": c(L0_conv_rw_fc2_w[:, :, 0, 0].T),
        "wp1": c(L0_conv_w_pw1.T),
        "wp2": c(L0_conv_w_pw2.T.reshape(2, P, DIM).transpose(1, 0, 2)),
        "star_s": c(L0_conv_star_scale), "star_b": c(L0_conv_star_bias),
        "gate": c(L0_ffn_gate_w.T),
        "cw_a": c(cw[:P]), "cw_b": c(cw[P:]),
        "sw_rows": c(L0_conv_spatial_weights.reshape(PIX, NF).T),
        "w1": c(L0_ffn_w1.transpose(2, 0, 1).reshape(DIM, E * HID)),
        "w3": c(L0_ffn_w3.transpose(2, 0, 1).reshape(DIM, E * HID)),
        "w2": c(L0_ffn_w2.reshape(E, DIM, HC, P).transpose(3, 2, 0, 1).reshape(P, HC, E * DIM)),
    }


def kernel(**inputs):
    import concourse.bacc as bacc
    from concourse.bass_utils import run_bass_kernel_spmd

    arrays = layouts(**{k: np.asarray(a) for k, a in inputs.items()})
    nc = bacc.Bacc("TRN2", target_bir_lowering=False, num_devices=1)
    io = {k: nc.dram_tensor(f"in_{k}", a.shape, mybir.dt.from_np(a.dtype), kind="ExternalInput").ap()
          for k, a in arrays.items()}
    io["out"] = nc.dram_tensor("out", (NTOK, DIM), F32, kind="ExternalOutput").ap()
    metaformer(nc, io)
    r = run_bass_kernel_spmd(nc, [{f"in_{k}": a for k, a in arrays.items()}], core_ids=[0])
    out = r.results[0]["out"]
    return np.ascontiguousarray(out.reshape(BATCH, SIZE, SIZE, DIM).transpose(0, 3, 1, 2))
```

```python
from contextlib import ExitStack

import numpy as np

import concourse.bass as bass
from concourse import mybir

ALU = mybir.AluOpType
ACT = mybir.ActivationFunctionType
AX = mybir.AxisListType
F32 = mybir.dt.float32
F32R = mybir.dt.float32r
I32 = mybir.dt.int32
U32 = mybir.dt.uint32
F16 = mybir.dt.float16
ds = bass.ds

P = 128
DIM = 128
MED = 2 * DIM
NF = 4
SIZE = 16
FS = SIZE // 2 + 1
PIX = SIZE * SIZE
BATCH = 16
PAIRS = BATCH // 2
HALF = 64
TAPS = 9
PAD = SIZE + 2
NTOK = BATCH * PIX
TILES = NTOK // P
E = 8
HID = 384
HC = HID // P
SLOT_TILES = 2 * TILES + E
RUN_TILES = (2 * NTOK + E * (P - 1)) // P
BUFS = 8
AHEAD = 5
X_CHUNKS = (0, 1, 3, 5, PAIRS)
GROUPS = 4
GCOLS = 2 * TILES // GROUPS
EARLY = 4 * (PAIRS - 3)
LN_C_EPS = 1e-6
LN_T_EPS = 1e-5


def fourier_tables():
    h = np.arange(8)[:, None]
    w = np.arange(16)[None, :]
    forward = np.zeros((2, P, P), np.float64)
    inverse = np.zeros((2, P, P), np.float64)
    sel = np.zeros((2, 2, SIZE * FS, 2, P), np.float64)

    def at(ky, kx):
        return (ky % SIZE) * FS + kx

    for par in range(2):
        kys = range(par, SIZE, 2)
        full = [(ky, kx) for ky in kys for kx in range(1, 8)]
        full += [(ky, kx) for ky in kys if 0 < ky < 8 for kx in (0, 8)]
        real = [(ky, kx) for ky in kys if ky in (0, 8) for kx in (0, 8)]
        assert 2 * len(full) + len(real) == P
        for n, (ky, kx) in enumerate(full):
            th = (2 * np.pi / SIZE) * (ky * h + kx * w)
            re, im = n, n + 64
            forward[par, :, re] = np.cos(th).ravel()
            forward[par, :, im] = -np.sin(th).ravel()
            inverse[par, re] = 2 * np.cos(th).ravel() / PIX
            inverse[par, im] = -2 * np.sin(th).ravel() / PIX
            if kx in (0, 8):
                terms = [(at(ky, kx), 0.5, 0.5), (at(-ky, kx), 0.5, -0.5)]
            else:
                terms = [(at(ky, kx), 1.0, 1.0)]
            for b, cr, ci in terms:
                sel[0, 0, b, par, re] += cr
                sel[0, 0, b, par, im] += cr
                sel[1, 1, b, par, re] -= ci
                sel[1, 1, b, par, im] += ci
        for n, (ky, kx) in enumerate(real):
            row = (len(full) + n) if n < 2 else (64 + len(full) + n - 2)
            cs = np.cos((2 * np.pi / SIZE) * (ky * h + kx * w)).ravel()
            forward[par, :, row] = cs
            inverse[par, row] = cs / PIX
            sel[0, 0, at(ky, kx), par, row] = 1.0
    inverse = np.concatenate([inverse, inverse * np.array([1.0, -1.0])[:, None, None]], axis=2)
    sel = sel.transpose(2, 0, 1, 3, 4).reshape(SIZE * FS, 2, 4, P)
    return (forward.transpose(1, 0, 2).astype(np.float32), inverse.transpose(1, 0, 2).astype(np.float32),
            np.ascontiguousarray(sel.astype(np.float32)))


def wait_done(eng, sem, count):
    if isinstance(count, int) and count <= 0:
        return
    eng.wait_ge(sem, count)


def wait_apart(eng, sem, count):
    if not isinstance(count, int):
        count = eng.to_reg(count)
        eng.wait_ge(sem, 1)
    wait_done(eng, sem, count)


def pair_loop(eng, step):
    step(0, 0)
    step(1, 1)
    with eng.Fori(1, PAIRS // 2 - 1) as n:
        for u in range(2):
            step(n * 2 + u, u)
    step(PAIRS - 2, 0)
    step(PAIRS - 1, 1)


def filter_loop(eng, step):
    for i in range(3):
        step(i, i % 2)
    with eng.Fori(1, PAIRS // 2 - 1) as n:
        for k in range(2):
            step(n * 2 + 1 + k, 1 - k)
    step(PAIRS - 1, 1)


def tile_loop(eng, step):
    for b in range(BUFS):
        step(b, b)
    with eng.Fori(1, SLOT_TILES // BUFS - 1) as n:
        for b in range(BUFS):
            step(n * BUFS + b, b)
    for b in range(RUN_TILES - (SLOT_TILES - BUFS)):
        step(SLOT_TILES - BUFS + b, b)


def first(i):
    return isinstance(i, int) and i == 0


def last(i, n):
    return isinstance(i, int) and i == n - 1


def deferred(i):
    return isinstance(i, int) and i >= PAIRS - 2


def flat(ap):
    return ap.rearrange("p a n -> p (a n)")


def metaformer(nc, io):
    with ExitStack() as ctx:
        def sb(name, shape, dt=F32):
            return ctx.enter_context(nc.sbuf_tensor(name, shape, dt))

        tn_dram = nc.dram_tensor("tn_dram", (NTOK, DIM), F32).ap()
        y_dram = nc.dram_tensor("y_dram", (2 * NTOK + SLOT_TILES * P, DIM), F32).ap()

        ident = sb("ident", [P, P])
        fwd = sb("fwd", [P, 2, P])
        inv = sb("inv", [P, 2, PIX])
        sp1 = sb("sp1", [P, TAPS, HALF])
        rw1 = sb("rw1", [P, HALF])
        rwc = sb("rwc", [P, P])
        route1_b = sb("route1_b", [P, 3])
        route_b = sb("route_b", [P, 2 * NF * 2])
        wp1 = sb("wp1", [P, MED])
        wp2 = sb("wp2", [P, 2, DIM])
        star_sb = sb("star_sb", [P, 2])
        star_s, star_b = star_sb[:, 0:1], star_sb[:, 1:2]
        gate = sb("gate", [P, P])
        cw_a = sb("cw_a", [P, NF, 2])
        cw_b = sb("cw_b", [SIZE * FS - P, NF, 2])
        coef = sb("coef", [P, 6, P], F32R)
        coef_hl = sb("coef_hl", [NF, 2, 4 * P + PIX], F32R)
        sw_rows = sb("sw_rows", [NF, PIX])
        mhalf = sb("mhalf", [P, 4])
        var_eps = sb("var_eps", [P, 2, 4])
        tri = sb("tri", [P, P], F16)
        ones = sb("ones", [P, P], F16)
        T = sb("T", [P, TILES, DIM])
        mix = sb("mix", [P, 2, TILES])
        idx_gather = sb("idx_gather", [P, SLOT_TILES], U32)
        idx_scatter = sb("idx_scatter", [P, SLOT_TILES], U32)
        tile_experts = sb("tile_experts", [1, SLOT_TILES // BUFS], I32)
        logits = sb("logits", [P, TILES, E])
        st6 = sb("st6", [P, 2, 4, 6])
        mv = sb("mv", [P, 2, 4, 2])
        rstd = sb("rstd", [P, 2, 4])
        xn = sb("xn", [P, 2, 4, DIM])
        xp = sb("xp", [P, 2, 2, PAD, PAD])
        xc = sb("xc", [P, 2, 512])
        s_all = sb("s_all", [P, PAIRS, SIZE, SIZE])
        r1 = sb("r1", [P, PIX])
        r2 = sb("r2", [P, PIX])
        rsum = sb("rsum", [P, PAIRS])
        rows = sb("rows", [P, 3, PAIRS, SIZE])
        tap_sum = sb("tap_sum", [P, 3, 3, PAIRS])
        tap_k = sb("tap_k", [P, 5, P])
        rw_k = sb("rw_k", [P, P])
        lg = sb("lg", [P, 2, NF, 2, BATCH])
        lmax = sb("lmax", [P, 2, 32])
        lsum = sb("lsum", [P, 2, 32])
        r_hl = sb("r_hl", [P, 2, 2, P], F32R)
        RS = sb("RS", [P, 2, 2, PAIRS, P], F32R)
        q_word = sb("q_word", [1, SLOT_TILES // BUFS], I32)
        q_i32 = sb("q_i32", [P, 2 * TILES], I32)
        q_slot_low = sb("q_slot_low", [P, 2 * TILES], I32)
        q_slot_high = sb("q_slot_high", [P, 2 * TILES], I32)
        q_e32 = sb("q_e32", [P, E], I32)
        spec = sb("spec", [P, 2, PAIRS, 512])
        shared = sb("shared", [P, 7680])
        rw2 = sb("rw2", [P, NF * MED])
        idx_g = [sb(f"idx_g{u}", [P, 4], U32) for u in range(2)]
        idx_s = [sb(f"idx_s{u}", [P, 4], U32) for u in range(2)]
        with nc.sbuf_tensor("star", [P, 2, PAIRS, 512], F32) as star, nc.sbuf_tensor("buf", [P, 8, 512], F32) as buf:
            pass
        w_lo = sb("w_lo", [P, 8192], F32R)
        w3_hi = sb("w3_hi", [P, E * HID], F32R)
        xgt_hl = sb("xgt_hl", [P, 2, 2, P], F32R)

        relu_x, sq_x = buf[:, 0:2, :], buf[:, 2:4, :]
        fold = [[buf[:, 4 + 2 * u + e, :] for e in range(2)] for u in range(2)]
        vt_c = [[buf[:, 2 * u + m, :] for m in range(2)] for u in range(2)]
        tnt = [buf[:, 4, :], buf[:, 5, :]]

        sp2 = shared[:, 0:5 * NF * MED].rearrange("p (t n) -> p t n", t=5)
        sel, sel_b = spec[:, 0, PAIRS - 2:PAIRS, :], spec[0:SIZE * FS - P, 1, PAIRS - 2:PAIRS, :]

        def area(tensor, first_col):
            at = [first_col]

            def take(n):
                a = tensor[:, at[0]:at[0] + n]
                at[0] += n
                assert at[0] <= tensor.shape[1]
                return a
            return take

        vb = area(shared[:, :], 0)
        sw_c, prod, cross = ([vb(512), vb(512)] for _ in range(3))
        u_c, y_c = ([[vb(512), vb(512)] for _ in range(2)] for _ in range(2))
        star_area = star[:].rearrange("p a b n -> p (a b n)")
        spec_area = spec[:].rearrange("p a b n -> p (a b n)")
        st = area(star_area, 0)
        w1s = st(E * HID)
        w3s = st(E * HID)
        q = area(spec_area, 0)
        w2s = q(HC * E * DIM).rearrange("p (c n) -> p c n", c=HC)
        q_eq, q_val, q_l2, q_cnt, q_slot = (q(TILES * E) for _ in range(5))
        q_incl, q_sel, q_oh_both = q(1 + E * TILES), q(2 * TILES * E), q(2 * TILES * E)
        q_oh = [q_oh_both[:, 0:TILES * E], q_oh_both[:, TILES * E:]]
        q_m = [q(TILES), q(TILES)]
        q_c, q_diff, q_exp, q_den = (q(TILES) for _ in range(4))
        q_cpad, q_pend, q_base = (q(E) for _ in range(3))
        q_pos = q(2 * TILES)
        q_v, q_inv, q_digit = (q(SLOT_TILES) for _ in range(3))
        q_wordf = q(SLOT_TILES // BUFS)
        q_ids, q_jcmp = q(GROUPS * SLOT_TILES), q(E * SLOT_TILES)
        tb = area(xp[:].rearrange("p u g a b -> p (u g a b)"), 0)
        q_rev, q_jtok, q_offset = tb(TILES * E), tb(E * SLOT_TILES), tb(GROUPS * SLOT_TILES)
        q_trash, q_power = tb(SLOT_TILES), tb(SLOT_TILES)
        q_one = s_all[:].rearrange("p b h w -> p (b h w)")[:, PAIRS * PIX - E * TILES:]
        half_tables = area(s_all[:].rearrange("p b h w -> p (b h w)").bitcast(F16), 0)
        slot_row = half_tables(P * GCOLS).rearrange("p (s n) -> p s n", n=GCOLS)
        tile_row = half_tables(SLOT_TILES * GCOLS).rearrange("p (j n) -> p j n", n=GCOLS)
        id_row, q_low, q_high = half_tables(GCOLS), half_tables(2 * TILES), half_tables(2 * TILES)
        hb = area(shared[:, :].bitcast(F16), 0)
        oh_s = [hb(P * GCOLS).rearrange("p (s n) -> p s n", n=GCOLS) for _ in range(2)]
        oh_j, oh_id = ([hb(SLOT_TILES * GCOLS).rearrange("p (j n) -> p j n", n=GCOLS) for _ in range(2)]
                       for _ in range(2))
        ff = area(shared[:, :], 0)
        xg, yo = ([ff(P) for _ in range(BUFS)] for _ in range(2))
        xgt = [[xgt_hl[:, u, h] for h in range(2)] for u in range(2)]
        silu, hid, hidt = ([ff(HID), ff(HID)] for _ in range(3))
        w1_hl = (RS[:].rearrange("p c g b m -> p (c g b m)")[:, 0:E * HID], w_lo[:, 0:E * HID])
        w3_hl = (w3_hi[:, :], w_lo[:, E * HID:2 * E * HID])
        cc = area(star_area, 0)
        ya, yb = ([cc(512) for _ in range(PAIRS)] for _ in range(2))

        bank = [ctx.enter_context(nc.psum_tensor(f"bank{n}", [P, 512], F32)) for n in range(8)]
        ps_tr, ps_r, ps_pw, ps_x, ps_conv = bank[0], bank[1], bank[2:4], bank[4:6], bank[6:8]
        ps_w, ps_v, ps_y = bank[0:3], (bank[3:5], bank[5:7]), bank[7]
        ps_tot, ps_rank, ps_idx = bank[0], bank[1], bank[2]
        p_x, p_y, p_h1, p_h3, p_ht = bank[0], bank[1], bank[2:4], bank[4:6], bank[6:8]

        S = {n: ctx.enter_context(nc.semaphore(n)) for n in (
            "ident_in consts_in tab_in x_in0 x_in1 x_in2 x_in3 route_in w1_in w3_in w2_in w_hi w_lo pad_zero coef_zero mhalf_set coef_ps "
            "coef_hi coef_lo coef_in a_stats a_aggr a_eps a_rstd a_norm a_tr a_xc a_xp a_pw a_conv a_rw1 a_relu_s "
            "a_relu_r a_rw2 a_rsum a_rows a_relu a_sq a_star a_fold a_dft a_spec r_cols r_full r_taps r_mm "
            "r_log r_max r_sub r_exp r_sum r_rec r_norm r_tr r_hi r_lo r_rows r_rows_pool b_w b_sw b_p b_cross b_u b_y "
            "b_vt b_vts b_w2 b_t b_stats b_aggr b_eps b_rstd b_norm b_tn0 b_tn1 b_tr b_tnt "
            "b_gate b_logit q_iota q_zero q_tri q_dve q_ready q_exp_done q_count q_oh_tile q_oh_ready q_oh_used "
            "q_tables g_idx s_idx f_tr f_xh f_xt f_h f_silu f_act f_ht f_hts f_y f_ys "
            "rs_zero k_zero w_zero r_cat c_weighed c_sum c_done out_sent").split()}
        S.update({f"{n}{b}": ctx.enter_context(nc.semaphore(f"{n}{b}")) for n in ("g_x", "y_out") for b in range(BUFS)})
        S.update({f"c_in{i}": ctx.enter_context(nc.semaphore(f"c_in{i}")) for i in range(PAIRS)})

        def star_at(j, i):
            return flat(star[:, j, ds(i, 1), :])

        def spec_at(lo, hi, e, i):
            return flat(spec[lo:hi, e, ds(i, 1), :])

        def tokens(i):
            return T[:, ds(i * 4, 4), :]

        def routing_rows(eng, blocks, done):
            eng.wait_ge(S["r_hi"], 1)
            eng.wait_ge(S["r_lo"], 1)
            eng.wait_ge(S["rs_zero"], 1)
            for r in blocks:
                eng.dma_start(RS[4 * r:4 * r + 4].rearrange("f c g b m -> f (c g b) m").bitcast(F32),
                              r_hl[:, r % 2, 1 - r // 4, :].bitcast(F32)).then_inc(S[done], 16)

        CONSTS = 16 * 8
        block = ctx.enter_context(nc.Block())

        @block.sync
        def _(sp):
            x_pairs = io["x"].rearrange("(i p q) c -> p i (q c)", p=P, q=4)
            consts = ((), ((wp1, "wp1"), (sp1, "sp1")), ((fwd, "fwd"),), ())
            for c in range(4):
                for dst, name in consts[c]:
                    sp.dma_start(dst[:], io[name]).then_inc(S["consts_in"], 16)
                i0, i1 = X_CHUNKS[c], X_CHUNKS[c + 1]
                sp.dma_start(T[:, 4 * i0:4 * i1, :].rearrange("p (i q) c -> p i (q c)", q=4), x_pairs[:, i0:i1, :])\
                    .then_inc(S[f"x_in{c}"], 16)
            for dst, name in ((inv, "inv"), (wp2, "wp2"), (route_b, "route_b"),
                              (sw_rows, "sw_rows"), (cw_a, "cw_a"), (cw_b, "cw_b")):
                sp.dma_start(dst[:], io[name]).then_inc(S["tab_in"], 16)
            sp.wait_ge(S["w_zero"], 3)
            sp.dma_start(gate[:, 0:E], io["gate"]).then_inc(S["tab_in"], 16)
            sp.dma_start(sel, io["sel_a"]).then_inc(S["tab_in"], 16)
            sp.dma_start(sel_b, io["sel_b"]).then_inc(S["tab_in"], 16)
            sp.dma_start(sp2[0:HALF, 0:5], io["sp2_even"]).then_inc(S["route_in"], 16)
            sp.dma_start(sp2[HALF:P, 0:4], io["sp2_odd"]).then_inc(S["route_in"], 16)
            for g in range(2):
                sp.dma_start(rw2[HALF * g:HALF * g + HALF], io["rw2"]).then_inc(S["route_in"], 16)
            sp.wait_ge(S["coef_zero"], 1)
            sp.wait_ge(S["coef_hi"], 2)
            sp.wait_ge(S["coef_lo"], 2)
            for r in range(4):
                sp.dma_start(coef[4 * r:4 * r + 4, 0:4, :].bitcast(F32), coef_hl[:, r // 2, 0:4 * P].rearrange(
                    "f (c k) -> f c k", c=4).bitcast(F32)).then_inc(S["coef_in"], 16)
                sp.dma_start(coef[16 + 4 * r:20 + 4 * r, 4:6, :].bitcast(F32), coef_hl[:, r // 2, 4 * P:4 * P + PIX].rearrange(
                    "f (c k) -> f c k", c=2).bitcast(F32)).then_inc(S["coef_in"], 16)
            routing_rows(sp, range(5), "r_rows")

            def store_tn(i, u):
                sp.wait_ge(S["b_norm"], i + 1)
                sp.dma_start(tn_dram[ds(i * (4 * P), 4 * P), :].rearrange("(p q) d -> p q d", p=P),
                             xn[:, u, :, :]).then_inc(S[f"b_tn{u}"], 16)
            pair_loop(sp, store_tn)
            sp.wait_ge(S["b_u"], 2 * PAIRS)
            sp.dma_start(w1s, io["w1"]).then_inc(S["w1_in"], 16)
            sp.dma_start(w3s, io["w3"]).then_inc(S["w3_in"], 16)
            sp.wait_ge(S["b_cross"], 2 * PAIRS)
            sp.dma_start(w2s, io["w2"]).then_inc(S["w2_in"], 16)

            for b in range(BUFS):
                sp.wait_ge(S[f"y_out{b}"], 16 * len(range(b, RUN_TILES, BUFS)))
            y_pairs = y_dram[0:2 * NTOK, :].rearrange("(k i p q) d -> k i p (q d)", k=2, p=P, q=4)
            for i in range(PAIRS):
                for k, y in enumerate((ya[i], yb[i])):
                    sp.dma_start(y, y_pairs[k, i])\
                        .then_inc(S[f"c_in{i}"], 16)

        @block.gpsimd
        def _(pool):
            pool.memset(rwc[:, :], 0.0).then_inc(S["w_zero"], 1)
            pool.memset(gate[:, :], 0.0).then_inc(S["w_zero"], 1)
            pool.memset(sp2[:, 4], 0.0).then_inc(S["w_zero"], 1)
            pool.memset(mhalf[:, :], -0.5).then_inc(S["mhalf_set"], 1)
            pool.memset(xp[:].rearrange("p u g a b -> p (u g a b)"), 0.0).then_inc(S["pad_zero"], 1)
            pool.wait_ge(S["mhalf_set"], 1)

            def inv_std(aggr, added, done, eps, i, u):
                wait_apart(pool, S[aggr], i + 1)
                pool.tensor_scalar(var_eps[:, u, :], mv[:, u, :, 1], eps, None, ALU.add).then_inc(S[added], 1)
                wait_apart(pool, S[added], i + 1)
                pool.tensor_tensor(rstd[:, u, :], var_eps[:, u, :], mhalf[:, :], ALU.pow).then_inc(S[done], 1)

            def fold_rows(i, u):
                pool.wait_ge(S["a_star"], i * 2 + 2)
                wait_done(pool, S["a_dft"], i * 2 - 2)
                pool.tensor_tensor(fold[u][0], star_at(0, i), star_at(1, i), ALU.add).then_inc(S["a_fold"], 1)
                pool.tensor_tensor(fold[u][1], star_at(0, i), star_at(1, i), ALU.subtract)\
                    .then_inc(S["a_fold"], 1)

            def phase_a(i, u):
                if not last(i, PAIRS):
                    inv_std("a_aggr", "a_eps", "a_rstd", LN_C_EPS, i + 1, 1 - u)
                if not deferred(i):
                    fold_rows(i, u)
                if last(i, PAIRS):
                    fold_rows(PAIRS - 2, 0)
            inv_std("a_aggr", "a_eps", "a_rstd", LN_C_EPS, 0, 0)
            pool.memset(coef[:].rearrange("p c k -> p (c k)").bitcast(F32), 0.0).then_inc(S["coef_zero"], 1)
            pool.memset(ones[:, :], 1.0).then_inc(S["q_tri"], 1)
            pool.memset(tri[:, :], -1.0).then_inc(S["q_tri"], 1)
            pool.wait_ge(S["q_tri"], 2)
            pool.affine_select(out=tri[:, :], in_=tri[:, :], compare_op=ALU.is_ge, fill=0.0, base=0,
                               pattern=[[-1, P]], channel_multiplier=1).then_inc(S["q_tri"], 1)
            pool.memset(RS[:].rearrange("p c g b m -> p (c g b m)").bitcast(F32), 0.0).then_inc(S["rs_zero"], 1)
            pool.memset(tap_k[:].rearrange("p t b -> p (t b)"), 0.0).then_inc(S["k_zero"], 1)
            pool.memset(rw_k[:, :], 0.0).then_inc(S["k_zero"], 1)
            pair_loop(pool, phase_a)

            pool.wait_ge(S["a_conv"], PAIRS)
            pool.wait_ge(S["r_taps"], 2)
            for ap, pat, base, cm in (
                    (q_rev.rearrange("p (t e) -> p t e", e=E), [[0, TILES], [-1, E]], E, 0),
                    (id_row.rearrange("p (i q) -> p i q", q=4), [[4 * P, GCOLS // 4], [1, 4]], 1, 4),
                    (slot_row, [[1, P], [0, GCOLS]], 0, 0),
                    (tile_row, [[1, SLOT_TILES], [0, GCOLS]], 0, 0),
                    (q_offset.rearrange("p (g j) -> p g j", g=GROUPS), [[GCOLS * P, GROUPS], [0, SLOT_TILES]], 0, 0),
                    (q_trash, [[P, SLOT_TILES]], 2 * NTOK + 1, 1),
                    (q_jtok.rearrange("p (e j) -> p e j", e=E), [[0, E], [P, SLOT_TILES]], 0, 0)):
                pool.iota(ap, pat, base=base, channel_multiplier=cm,
                          allow_small_or_imprecise_dtypes=True).then_inc(S["q_iota"], 1)
            pool.memset(q_one, 1.0).then_inc(S["q_iota"], 1)
            for b in range(BUFS):
                pool.memset(q_power[:, b::BUFS], float(E ** b)).then_inc(S["q_iota"], 1)

            routing_rows(pool, range(5, 8), "r_rows_pool")
            fold_rows(PAIRS - 1, 1)

            def spatial(i, u):
                for j in range(2):
                    pool.wait_ge(S["b_sw"], i * 2 + j + 1)
                    wait_done(pool, S["b_vt"], i * 2 - 2)
                    pool.tensor_tensor(u_c[u][j], star_at(j, i), sw_c[j], ALU.mult).then_inc(S["b_u"], 1)

            def spectral(i, u):
                for e in range(2):
                    pool.wait_ge(S["b_cross"], i * 2 + e + 1)
                    wait_done(pool, S["b_vt"], i * 2 - 2)
                    pool.tensor_tensor(y_c[u][e], prod[e], cross[e], ALU.add).then_inc(S["b_y"], 1)

            def phase_b(i, u):
                if not last(i, PAIRS):
                    spatial(i + 1, 1 - u)
                if not first(i):
                    inv_std("b_aggr", "b_eps", "b_rstd", LN_T_EPS, i - 1, 1 - u)
                if not last(i, PAIRS):
                    spectral(i + 1, 1 - u)
            spatial(0, 0)
            spectral(0, 0)
            filter_loop(pool, phase_b)
            inv_std("b_aggr", "b_eps", "b_rstd", LN_T_EPS, PAIRS - 1, 1)

            for n, (w, hl) in enumerate(((w1s, w1_hl), (w3s, w3_hl))):
                pool.wait_ge(S["w_hi"], n + 1)
                pool.tensor_tensor(hl[1], w, hl[0].bitcast(F32), ALU.subtract).then_inc(S["w_lo"], 1)

            for u in range(2):
                pool.wait_ge(S[f"b_tn{u}"], 16 * (PAIRS // 2))

            def gather(j, b):
                wait_apart(pool, S["f_tr"], j - BUFS + 1)
                quad, col = b // 4, b % 4
                if col == 0:
                    wait_apart(pool, S["g_idx"], j + 4)
                pool.indirect_dma_start(xg[b], None, tn_dram, bass.IndirectOffsetOnAxis(
                    ap=idx_g[quad][:, col:col + 1], axis=0)).then_inc(S[f"g_x{b}"], 16)

            def scatter(j, b):
                wait_apart(pool, S["f_ys"], j + 1)
                quad, col = b // 4, b % 4
                if col == 0:
                    wait_apart(pool, S["s_idx"], j + 4)
                pool.indirect_dma_start(y_dram, bass.IndirectOffsetOnAxis(ap=idx_s[quad][:, col:col + 1], axis=0),
                                        yo[b], None).then_inc(S[f"y_out{b}"], 16)

            for b in range(AHEAD):
                gather(b, b)

            def step(j, b):
                if not isinstance(j, int) or j + AHEAD < RUN_TILES:
                    gather(j + AHEAD, (b + AHEAD) % BUFS)
                if not isinstance(j, int) or j >= 2:
                    scatter(j - 2, (b - 2) % BUFS)
            tile_loop(pool, step)
            for j in range(RUN_TILES - 2, RUN_TILES):
                scatter(j, j % BUFS)

            for i in range(PAIRS):
                pool.wait_ge(S["c_weighed"], i + 1)
                tiles = T[:, 4 * i:4 * i + 4, :].rearrange("p t d -> p (t d)")
                pool.tensor_tensor(tiles, tiles, ya[i], ALU.add).then_inc(S["c_sum"], 1)

        @block.scalar
        def _(act):
            act.dma_start(ident[:, :], io["ident"]).then_inc(S["ident_in"], 16)
            act.dma_start(rw1[:, :], io["rw1"]).then_inc(S["consts_in"], 16)
            act.dma_start(star_sb[:, :], io["star_sb"].partition_broadcast(P)).then_inc(S["consts_in"], 16)
            act.dma_start(route1_b[:, :], io["route1_b"]).then_inc(S["consts_in"], 16)
            act.wait_ge(S["w_zero"], 3)
            for g in range(2):
                act.dma_start(rwc[HALF * g:HALF * g + HALF, HALF * g:HALF * g + HALF], io["rwc"])\
                    .then_inc(S["consts_in"], 16)

            def image(i, u):
                act.wait_ge(S["a_tr"], i + 1)
                wait_done(act, S["a_rw1"], i - 1)
                act.activation(xc[:, u, :], ps_tr[:, :], ACT.Copy).then_inc(S["a_xc"], 1)
                wait_done(act, S["a_conv"], i - 1)
                act.activation(xp[:, u, :, 1:SIZE + 1, 1:SIZE + 1],
                               ps_tr[:, :].rearrange("p (g a b) -> p g a b", g=2, a=SIZE), ACT.Copy)\
                    .then_inc(S["a_xp"], 1)

            def star_relu(i):
                for j in range(2):
                    act.wait_ge(S["a_pw"], i * 2 + j + 1)
                    wait_done(act, S["a_sq"], i * 2 + j - 1)
                    act.activation(relu_x[:, j, :], ps_pw[j][:, :], ACT.Relu).then_inc(S["a_relu"], 1)

            def star_square(i):
                for j in range(2):
                    act.wait_ge(S["a_relu"], i * 2 + j + 1)
                    wait_done(act, S["a_star"], i * 2 + j - 1)
                    act.activation(sq_x[:, j, :], relu_x[:, j, :], ACT.Square).then_inc(S["a_sq"], 1)

            def phase_a(i, u):
                if not deferred(i):
                    star_relu(i)
                    star_square(i)
                if last(i, PAIRS):
                    star_relu(PAIRS - 2)
                    star_square(PAIRS - 2)
                act.wait_ge(S["a_conv"], i + 1)
                act.activation(s_all[:, ds(i, 1), :, :].rearrange("p o a b -> p (o a b)"), ps_conv[u][:, 0:PIX],
                               ACT.Relu, bias=route1_b[:, 0:1]).then_inc(S["a_relu_s"], 1)
                act.wait_ge(S["a_rw1"], i + 1)
                act.activation(r1[:, :], ps_r[:, 0:PIX], ACT.Relu, bias=route1_b[:, 1:2]).then_inc(S["a_relu_r"], 1)
                if not last(i, PAIRS):
                    image(i + 1, 1 - u)
                act.wait_ge(S["a_rw2"], i + 1)
                act.activation(r2[:, :], ps_r[:, 0:PIX], ACT.Relu, bias=route1_b[:, 2:3],
                               accum_out=rsum[:, ds(i, 1)]).then_inc(S["a_rsum"], 1)
            act.wait_ge(S["pad_zero"], 1)
            image(0, 0)
            act.wait_ge(S["consts_in"], CONSTS)
            pair_loop(act, phase_a)
            act.wait_ge(S["coef_ps"], 1)
            act.activation(coef_hl[:, 0, 0:4 * P], ps_x[0][0:NF, :], ACT.Copy).then_inc(S["coef_hi"], 1)
            act.activation(coef_hl[:, 0, 4 * P:4 * P + PIX], sw_rows[:, :], ACT.Copy).then_inc(S["coef_hi"], 1)

            act.wait_ge(S["r_sub"], 1)
            lg_flat = lg[:].rearrange("p s f c b -> p (s f c b)")
            act.activation(lg_flat, lg_flat, ACT.Exp).then_inc(S["r_exp"], 1)
            star_relu(PAIRS - 1)
            act.wait_ge(S["r_tr"], 1)
            act.activation(r_hl[:, 0, :, :].rearrange("p s m -> p (s m)"), ps_tr[:, 0:2 * P], ACT.Copy)\
                .then_inc(S["r_hi"], 1)
            star_square(PAIRS - 1)

            def spatial(i):
                for j in range(2):
                    act.wait_ge(S["b_w"], i * 6 + j + 1)
                    wait_done(act, S["b_u"], i * 2 + j - 1)
                    act.activation(sw_c[j], ps_w[j][:, :], ACT.Copy).then_inc(S["b_sw"], 1)

            def branch_copy(i, u, m):
                act.wait_ge(S["b_vt"], i * 2 + m + 1)
                wait_done(act, S["b_w2"], i - 1)
                act.activation(vt_c[u][m], ps_v[u][m][:, :], ACT.Copy).then_inc(S["b_vts"], 1)

            def gate_copy(i, u):
                act.wait_ge(S["b_tr"], i + 1)
                wait_done(act, S["b_gate"], i - 1)
                act.activation(tnt[u], ps_v[1 - u][0][:, :], ACT.Copy).then_inc(S["b_tnt"], 1)

            def phase_b(i, u):
                if not last(i, PAIRS):
                    spatial(i + 1)
                branch_copy(i, u, 0)
                if not isinstance(i, int) or 2 <= i < PAIRS - 1:
                    gate_copy(i - 2, u)
                branch_copy(i, u, 1)
            spatial(0)
            filter_loop(act, phase_b)
            for i in range(PAIRS - 3, PAIRS):
                gate_copy(i, i % 2)

            act.wait_ge(S["q_ready"], 1)
            act.activation(q_exp, q_diff, ACT.Exp).then_inc(S["q_exp_done"], 1)

            for n, (w_in, w, hl) in enumerate((("w1_in", w1s, w1_hl), ("w3_in", w3s, w3_hl))):
                act.wait_ge(S[w_in], 16)
                if n == 0:
                    act.wait_ge(S["b_w"], 6 * PAIRS)
                else:
                    act.wait_ge(S["b_gate"], PAIRS)
                act.activation(hl[0], w, ACT.Copy).then_inc(S["w_hi"], 1)

            def x_high(j, u):
                act.wait_ge(S["f_tr"], j + 1)
                wait_done(act, S["f_h"], j - 1)
                act.activation(xgt[u][0], p_x[:, 0:P], ACT.Copy).then_inc(S["f_xh"], 1)

            def hidden_copy(j, u):
                act.wait_ge(S["f_ht"], j + 1)
                wait_done(act, S["f_y"], j - 1)
                act.activation(hidt[u], p_ht[u][:, 0:HID], ACT.Copy).then_inc(S["f_hts"], 1)

            def step(j, u):
                if not last(j, RUN_TILES):
                    x_high(j + 1, 1 - u)
                act.wait_ge(S["f_h"], j + 1)
                wait_done(act, S["f_act"], j - 1)
                act.activation(silu[u], p_h1[u][:, 0:HID], ACT.Silu).then_inc(S["f_silu"], 1)
                if not first(j):
                    hidden_copy(j - 1, 1 - u)
            x_high(0, 0)
            tile_loop(act, lambda j, b: step(j, b % 2))
            hidden_copy(RUN_TILES - 1, (RUN_TILES - 1) % 2)

            def weigh(i):
                act.wait_ge(S[f"c_in{i}"], 32)
                for t in range(4):
                    cols = slice(t * DIM, (t + 1) * DIM)
                    op = act.activation(ya[i][:, cols], ya[i][:, cols], ACT.Copy,
                                        scale=mix[:, 0, 4 * i + t:4 * i + t + 1])
                op.then_inc(S["c_weighed"], 1)

            out_pairs = io["out"].rearrange("(i p q) d -> i p (q d)", p=P, q=4)
            for i in range(2):
                weigh(i)
            for i in range(PAIRS):
                if i + 2 < PAIRS:
                    weigh(i + 2)
                act.wait_ge(S["c_done"], i + 1)
                act.dma_start(out_pairs[i], T[:, 4 * i:4 * i + 4, :].rearrange("p t d -> p (t d)")).then_inc(S["out_sent"], 16)
            act.wait_ge(S["out_sent"], 16 * PAIRS)

        @block.tensor
        def _(pe):
            pe.wait_ge(S["ident_in"], 16)

            def transposes(i, u):
                pe.wait_ge(S["a_norm"], i + 1)
                wait_done(pe, S["a_xp"], i)
                for t in range(4):
                    mm = pe.transpose(ps_tr[:, t * P:(t + 1) * P], xn[:, u, t, :], ident[:, :])
                mm.then_inc(S["a_tr"], 1)

            def star_matmul(i, u):
                pe.wait_ge(S["a_xc"], i + 1)
                for j in range(2):
                    wait_done(pe, S["a_relu"], i * 2 + j - 1)
                    for g in range(2):
                        mm = pe.matmul(ps_pw[j][:, g * MED:(g + 1) * MED],
                                       xc[:, u, (2 * g + j) * P:(2 * g + j + 1) * P], wp1[:, :], start=True, stop=True)
                    mm.then_inc(S["a_pw"], 1)

            def forward(i, u):
                for e in range(2):
                    pe.wait_ge(S["a_fold"], i * 2 + e + 1)
                    wait_done(pe, S["a_spec"], i * 2 + e - 1)
                    pe.matmul(ps_x[e][:, :], fwd[:, e, :], fold[u][e], start=True, stop=True).then_inc(S["a_dft"], 1)

            def phase_a(i, u):
                if not deferred(i):
                    star_matmul(i, u)
                if last(i, PAIRS):
                    star_matmul(PAIRS - 2, 0)
                wait_done(pe, S["a_relu_s"], i - 1)
                pe.wait_ge(S["a_xp"], i + 1)
                for t in range(TAPS):
                    for g in range(2):
                        mm = pe.matmul(ps_conv[u][HALF * g:HALF * g + HALF, 0:PIX], sp1[:, t, :],
                                       xp[:, u, g, t // 3:t // 3 + SIZE, t % 3:t % 3 + SIZE],
                                       start=(t == 0), stop=(t == TAPS - 1))
                mm.then_inc(S["a_conv"], 1)
                wait_done(pe, S["a_rsum"], i)
                for g in range(2):
                    mm = pe.matmul(ps_r[HALF * g:HALF * g + HALF, 0:PIX], rw1[:, :],
                                   xc[:, u, g * PIX:(g + 1) * PIX], start=True, stop=True)
                mm.then_inc(S["a_rw1"], 1)
                if not last(i, PAIRS):
                    transposes(i + 1, 1 - u)
                pe.wait_ge(S["a_relu_r"], i + 1)
                pe.matmul(ps_r[:, 0:PIX], rwc[:, :], r1[:, :], start=True, stop=True).then_inc(S["a_rw2"], 1)
                if not deferred(i):
                    forward(i, u)
            transposes(0, 0)
            pe.wait_ge(S["consts_in"], CONSTS)
            pair_loop(pe, phase_a)
            pe.wait_ge(S["tab_in"], 16 * 9)
            pe.wait_ge(S["a_spec"], 2 * (PAIRS - 2))
            n = 0
            for part in range(2):
                for cw, table in ((cw_a, sel), (cw_b, sel_b)):
                    mm = pe.matmul(ps_x[0][0:NF, :], cw[:, :, part], table[:, part, :], start=(n == 0), stop=(n == 3))
                    n += 1
            mm.then_inc(S["coef_ps"], 1)

            pe.wait_ge(S["route_in"], 64)
            pe.wait_ge(S["w_zero"], 3)
            pe.wait_ge(S["r_cat"], 6)
            pe.wait_ge(S["a_xp"], PAIRS)
            pe.wait_ge(S["a_relu_s"], PAIRS)
            pe.wait_ge(S["a_rsum"], PAIRS)
            for k in range(2 * NF):
                block_k = slice(k % 4 * P, (k % 4 + 1) * P)
                for t in range(5):
                    pe.matmul(ps_conv[k // 4][:, block_k], sp2[:, t, k * P:(k + 1) * P], tap_k[:, t, :],
                              start=(t == 0), stop=(t == 4))
                mm = pe.matmul(bank[k // 4][:, block_k], rw2[:, k * P:(k + 1) * P], rw_k[:, :], start=True, stop=True)
            mm.then_inc(S["r_mm"], 1)
            star_matmul(PAIRS - 1, 1)
            pe.wait_ge(S["coef_lo"], 2)
            forward(PAIRS - 2, 0)
            pe.wait_ge(S["r_norm"], 1)
            for s in range(2):
                mm = pe.transpose(ps_tr[:, s * P:(s + 1) * P], lg[:, s].rearrange("p f c b -> p (f c b)"),
                                  ident[:, :])
            mm.then_inc(S["r_tr"], 1)
            pe.wait_ge(S["coef_in"], 16 * 8)
            pe.wait_ge(S["r_rows"], 16 * 5)
            pe.wait_ge(S["r_rows_pool"], 16 * 3)
            pe.wait_ge(S["a_relu"], 2 * PAIRS)

            ring = (4, 5, 0, 2, 1, 3)

            def filters(i, order):
                free = ((("b_cross", i * 2 - 1),), (("b_p", i * 2),), (("b_cross", i * 2),),
                        (("b_sw", i * 2 + 1),), (("b_sw", i * 2 + 2),), (("b_p", i * 2 + 1),))
                for n in order:
                    for name, count in free[n]:
                        wait_done(pe, S[name], count)
                    pe.matmul(ps_w[n % 3][:, :], coef[:, ring[n], :],
                              RS[:, :, :, ds(i, 1), :].rearrange("r c g b m -> r g c (b m)"), start=True, stop=True)\
                        .then_inc(S["b_w"], 1)

            def branch(i, u, m):
                pe.wait_ge(S["b_u"], i * 2 + 2)
                if not isinstance(i, int) or i >= 3:
                    if m == 0:
                        pe.wait_ge(S["b_tnt"], i - 2)
                    else:
                        pe.wait_ge(S["b_logit"], i - 2)
                wait_done(pe, S["b_vts"], i * 2 - 3 + m)
                for g in range(2):
                    for j in range(2):
                        pe.matmul(ps_v[u][m][:, (2 * g + j) * P:(2 * g + j + 1) * P],
                                  u_c[u][j][:, g * MED + m * P:g * MED + (m + 1) * P], ident[:, :],
                                  start=(g == 0 and j == 0), stop=False, is_transpose=True)
                pe.wait_ge(S["b_y"], i * 2 + 2)
                for e in range(2):
                    for g in range(2):
                        mm = pe.matmul(ps_v[u][m][:, g * PIX:(g + 1) * PIX],
                                       y_c[u][e][:, g * MED + m * P:g * MED + (m + 1) * P], inv[:, e, :],
                                       start=False, stop=(e == 1 and g == 1))
                mm.then_inc(S["b_vt"], 1)

            def project(i, u):
                pe.wait_ge(S["b_vts"], i * 2 + 2)
                wait_done(pe, S["b_t"], i)
                for t in range(4):
                    for m in range(2):
                        mm = pe.matmul(ps_y[:, t * P:(t + 1) * P], vt_c[u][m][:, t * P:(t + 1) * P], wp2[:, m, :],
                                       start=(m == 0), stop=(m == 1))
                mm.then_inc(S["b_w2"], 1)

            def turn_tokens(i, u):
                pe.wait_ge(S["b_norm"], i + 1)
                wait_done(pe, S["b_vts"], min(2 * PAIRS, i * 2 + 4) if isinstance(i, int) else i * 2 + 4)
                for t in range(4):
                    mm = pe.transpose(ps_v[1 - u][0][:, t * P:(t + 1) * P], xn[:, u, t, :], ident[:, :])
                mm.then_inc(S["b_tr"], 1)

            def gating(i, u):
                pe.wait_ge(S["b_tnt"], i + 1)
                for t in range(4):
                    mm = pe.matmul(ps_v[1 - u][1][:, t * P:(t + 1) * P], tnt[u][:, t * P:(t + 1) * P], gate[:, :],
                                   start=True, stop=True)
                mm.then_inc(S["b_gate"], 1)

            def phase_b(i, u):
                lagging = not isinstance(i, int) or 2 <= i < PAIRS - 1
                if not last(i, PAIRS):
                    filters(i + 1, (0, 1, 2))
                if not first(i):
                    project(i - 1, 1 - u)
                if not last(i, PAIRS):
                    filters(i + 1, (3, 4))
                branch(i, u, 0)
                if lagging:
                    turn_tokens(i - 2, u)
                if not last(i, PAIRS):
                    filters(i + 1, (5,))
                branch(i, u, 1)
                if lagging:
                    gating(i - 2, u)
            filters(0, range(6))
            forward(PAIRS - 1, 1)
            pe.wait_ge(S["a_spec"], 2 * PAIRS)
            filter_loop(pe, phase_b)
            project(PAIRS - 1, 1)
            for i in range(PAIRS - 3, PAIRS):
                turn_tokens(i, i % 2)
                gating(i, i % 2)

            pe.wait_ge(S["q_tri"], 3)
            pe.wait_ge(S["q_ready"], 2)
            counts = q_cnt.bitcast(F16)[:, 0:TILES * E].rearrange("p (t e) -> p e t", e=E)
            pe.matmul(ps_tot[:, 0:E * TILES], ones[:, :], counts, start=True, stop=True).then_inc(S["q_count"], 1)
            pe.matmul(ps_rank[:, 0:E * TILES], tri[:, :], counts, start=True, stop=True).then_inc(S["q_count"], 1)

            for g in range(GROUPS):
                pe.wait_ge(S["q_oh_ready"], g + 1)
                for n in range(GCOLS):
                    mm = pe.matmul(ps_idx[:, g * SLOT_TILES:(g + 1) * SLOT_TILES], oh_s[g % 2][:, :, n],
                                   oh_id[g % 2][:, :, n], start=(n == 0), stop=(n == GCOLS - 1))
                mm.then_inc(S["q_oh_used"], 1)

            def transpose_x(j, b):
                pe.wait_ge(S[f"g_x{b}"], (j - b) * (16 // BUFS) + 16)
                wait_done(pe, S["f_xt"], j)
                pe.transpose(p_x[:, 0:P], xg[b], ident[:, :]).then_inc(S["f_tr"], 1)

            def turn(j, u):
                pe.wait_ge(S["f_act"], j + 1)
                wait_done(pe, S["f_hts"], j - 1)
                for c in range(HC):
                    mm = pe.transpose(p_ht[u][:, c * P:(c + 1) * P], hid[u][:, c * P:(c + 1) * P], ident[:, :])
                mm.then_inc(S["f_ht"], 1)

            def down(j, u, e):
                pe.wait_ge(S["f_hts"], j + 1)
                wait_done(pe, S["f_ys"], j)
                for c in range(HC):
                    mm = pe.matmul(p_y[:, 0:DIM], hidt[u][:, c * P:(c + 1) * P], w2s[:, c, ds(e * DIM, DIM)],
                                   start=(c == 0), stop=(c == HC - 1))
                mm.then_inc(S["f_y"], 1)

            def step(j, b):
                u = b % 2
                if not last(j, RUN_TILES):
                    transpose_x(j + 1, (b + 1) % BUFS)
                if b == 0:
                    word = pe.snap(word_reg, min_val=0, max_val=E ** (BUFS + 2) - 1)
                    held[:] = [(word // E ** k) % E for k in range(BUFS + 2)]
                cols = ds(held[b] * HID, HID)
                pe.wait_ge(S["f_xt"], j + 1)
                wait_done(pe, S["f_act"], j - 1)
                for n, (xs, ws) in enumerate(((0, 0), (0, 1), (1, 0))):
                    for psum, w_hl in ((p_h1[u], w1_hl), (p_h3[u], w3_hl)):
                        mm = pe.matmul(psum[:, 0:HID], xgt[u][xs], w_hl[ws][:, cols], start=(n == 0), stop=(n == 2))
                mm.then_inc(S["f_h"], 1)
                if b == 2 and (not isinstance(j, int) or j + BUFS < RUN_TILES):
                    pe.reg_load(word_reg, tile_experts[0:1, ds((j - b) // BUFS + 1, 1)])
                if not first(j):
                    turn(j - 1, 1 - u)
                if not isinstance(j, int) or j >= 2:
                    down(j - 2, u, held[b - 2])
            held = []
            word_reg = pe.alloc_register("tile_experts_word")
            transpose_x(0, 0)
            pe.wait_ge(S["w_hi"], 2)
            pe.wait_ge(S["w_lo"], 2)
            pe.wait_ge(S["w2_in"], 16)
            pe.wait_ge(S["q_tables"], 1)
            pe.reg_load(word_reg, tile_experts[0:1, 0:1])
            tile_loop(pe, step)
            turn(RUN_TILES - 1, (RUN_TILES - 1) % 2)
            for j in range(RUN_TILES - 2, RUN_TILES):
                down(j, j % 2, held[j % BUFS])

        @block.vector
        def _(dve):
            def stats(ph, i, u):
                for t in range(4):
                    op = dve.bn_stats(st6[:, u, t, :], flat(T[:, ds(i * 4 + t, 1), :]))
                op.then_inc(S[ph + "_stats"], 1)
                wait_apart(dve, S[ph + "_stats"], i + 1)
                for t in range(4):
                    op = dve.bn_aggr(mv[:, u, t, :], st6[:, u, t, :])
                op.then_inc(S[ph + "_aggr"], 1)

            def normalise(ph, i, u):
                dve.wait_ge(S[ph + "_rstd"], i + 1)
                for t in range(4):
                    op = dve.tensor_scalar(xn[:, u, t, :], flat(T[:, ds(i * 4 + t, 1), :]), mv[:, u, t, 0:1],
                                           rstd[:, u, t:t + 1], ALU.subtract, ALU.mult)
                op.then_inc(S[ph + "_norm"], 1)

            def star_scale(i):
                for j in range(2):
                    dve.wait_ge(S["a_sq"], i * 2 + j + 1)
                    dve.tensor_scalar(star_at(j, i), sq_x[:, j, :], star_s, star_b, ALU.mult, ALU.add)\
                        .then_inc(S["a_star"], 1)

            def spectrum_copy(i):
                for e in range(2):
                    dve.wait_ge(S["a_dft"], i * 2 + e + 1)
                    dve.tensor_copy(spec_at(0, P, e, i), ps_x[e][:, :]).then_inc(S["a_spec"], 1)

            def phase_a(i, u):
                if isinstance(i, int) and i < 2:
                    for c in ((1,), (2, 3))[i]:
                        dve.wait_ge(S[f"x_in{c}"], 16)
                if not last(i, PAIRS):
                    stats("a", i + 1, 1 - u)
                if first(i):
                    dve.wait_ge(S["consts_in"], CONSTS)
                if not deferred(i):
                    star_scale(i)
                if last(i, PAIRS):
                    star_scale(PAIRS - 2)
                if not last(i, PAIRS):
                    wait_done(dve, S["a_tr"], i)
                    normalise("a", i + 1, 1 - u)
                dve.wait_ge(S["a_relu_s"], i + 1)
                dve.tensor_reduce(rows[:, 1, ds(i, 1), :].rearrange("p o a -> p (o a)"),
                                  s_all[:, ds(i, 1), :, :].rearrange("p o a b -> p (o a) b"), AX.X, ALU.add)\
                    .then_inc(S["a_rows"], 1)
                if not deferred(i):
                    spectrum_copy(i)
            dve.wait_ge(S["x_in0"], 16)
            stats("a", 0, 0)
            normalise("a", 0, 0)
            pair_loop(dve, phase_a)

            dve.wait_ge(S["a_rows"], PAIRS)
            dve.tensor_tensor(rows[:, 0], rows[:, 1], s_all[:, :, :, SIZE - 1], ALU.subtract).then_inc(S["r_cols"], 1)
            dve.tensor_tensor(rows[:, 2], rows[:, 1], s_all[:, :, :, 0], ALU.subtract).then_inc(S["r_cols"], 1)
            dve.wait_ge(S["r_cols"], 2)
            dve.tensor_reduce(tap_sum[:, 1], rows[:], AX.X, ALU.add).then_inc(S["r_full"], 1)
            dve.wait_ge(S["r_full"], 1)
            dve.tensor_tensor(tap_sum[:, 0], tap_sum[:, 1], rows[:, :, :, SIZE - 1], ALU.subtract)\
                .then_inc(S["r_taps"], 1)
            dve.tensor_tensor(tap_sum[:, 2], tap_sum[:, 1], rows[:, :, :, 0], ALU.subtract).then_inc(S["r_taps"], 1)
            dve.wait_ge(S["r_taps"], 2)
            dve.wait_ge(S["a_rsum"], PAIRS)
            dve.wait_ge(S["k_zero"], 2)
            taps = tap_sum[:].rearrange("p y x b -> p (y x) b")
            for g in range(2):
                half, cols = slice(HALF * g, HALF * g + HALF), slice(PAIRS * g, PAIRS * g + PAIRS)
                dve.tensor_copy(tap_k[0:HALF, 0:5, cols], taps[half, 0:TAPS:2, :]).then_inc(S["r_cat"], 1)
                dve.tensor_copy(tap_k[HALF:P, 0:4, cols], taps[half, 1:TAPS:2, :]).then_inc(S["r_cat"], 1)
                dve.tensor_copy(rw_k[half, cols], rsum[half, :]).then_inc(S["r_cat"], 1)
            dve.wait_ge(S["coef_hi"], 2)
            dve.tensor_tensor(coef_hl[:, 1, 0:4 * P], ps_x[0][0:NF, :], coef_hl[:, 0, 0:4 * P].bitcast(F32),
                              ALU.subtract).then_inc(S["coef_lo"], 1)
            dve.tensor_tensor(coef_hl[:, 1, 4 * P:4 * P + PIX], sw_rows[:, :],
                              coef_hl[:, 0, 4 * P:4 * P + PIX].bitcast(F32), ALU.subtract).then_inc(S["coef_lo"], 1)
            dve.wait_ge(S["tab_in"], 16 * 9)
            dve.wait_ge(S["r_mm"], 1)
            for s, banks in ((0, ps_conv), (1, bank[0:2])):
                for h in range(2):
                    dve.scalar_tensor_tensor(
                        out=lg[:, s].rearrange("p f c b -> p (f c) b")[:, 4 * h:4 * h + 4],
                        in0=banks[h][:, :].rearrange("p (k n) -> p k n", k=4)[:, :, 0:BATCH], scalar=1.0 / PIX,
                        in1=route_b[:, 8 * s + 4 * h:8 * s + 4 * h + 4].unsqueeze(2).to_broadcast([P, 4, BATCH]),
                        op0=ALU.mult, op1=ALU.add).then_inc(S["r_log"], 1)
            lg_f = lg[:].rearrange("p s f c b -> p s f (c b)")
            dve.wait_ge(S["r_log"], 4)
            dve.tensor_reduce(lmax[:, :, :], lg_f.rearrange("p s f r -> p s r f"), AX.X, ALU.max)\
                .then_inc(S["r_max"], 1)
            dve.wait_ge(S["r_max"], 1)
            dve.tensor_tensor(lg_f, lg_f, lmax[:, :, :].unsqueeze(2).to_broadcast([P, 2, NF, 32]), ALU.subtract)\
                .then_inc(S["r_sub"], 1)
            dve.wait_ge(S["r_exp"], 1)
            dve.tensor_reduce(lsum[:, :, :], lg_f.rearrange("p s f r -> p s r f"), AX.X, ALU.add)\
                .then_inc(S["r_sum"], 1)
            dve.wait_ge(S["r_sum"], 1)
            dve.reciprocal(lmax[:, :, :], lsum[:, :, :]).then_inc(S["r_rec"], 1)
            dve.wait_ge(S["r_rec"], 1)
            dve.tensor_tensor(lg_f, lg_f, lmax[:, :, :].unsqueeze(2).to_broadcast([P, 2, NF, 32]), ALU.mult)\
                .then_inc(S["r_norm"], 1)
            spectrum_copy(PAIRS - 2)
            dve.wait_ge(S["r_hi"], 1)
            dve.tensor_tensor(r_hl[:, 1, :, :].rearrange("p s m -> p (s m)"), ps_tr[:, 0:2 * P],
                              r_hl[:, 0, :, :].rearrange("p s m -> p (s m)").bitcast(F32), ALU.subtract)\
                .then_inc(S["r_lo"], 1)
            star_scale(PAIRS - 1)

            def filter_products(i, e):
                n_p, n_s = (2, 3) if e == 0 else (4, 5)
                dve.wait_ge(S["b_w"], i * 6 + n_p + 1)
                wait_done(dve, S["b_y"], i * 2 + e - 1)
                dve.tensor_tensor(prod[e], spec_at(0, P, e, i), ps_w[n_p % 3][:, :], ALU.mult)\
                    .then_inc(S["b_p"], 1)
                dve.wait_ge(S["b_w"], i * 6 + n_s + 1)
                dve.tensor_tensor(cross[e][0:64], spec_at(64, P, e, i), ps_w[n_s % 3][0:64, :], ALU.mult)
                dve.tensor_tensor(cross[e][64:P], spec_at(0, 64, e, i), ps_w[n_s % 3][64:P, :], ALU.mult)\
                    .then_inc(S["b_cross"], 1)

            def residual(i, u):
                dve.wait_ge(S["b_w2"], i + 1)
                dve.tensor_tensor(tokens(i), tokens(i), ps_y[:, :].rearrange("p (t d) -> p t d", t=4), ALU.add)\
                    .then_inc(S["b_t"], 1)
                wait_apart(dve, S["b_t"], i + 1)
                stats("b", i, u)

            def normalise_tokens(i, u):
                wait_done(dve, S[f"b_tn{u}"], i * 8 - 8 * u)
                wait_done(dve, S["b_tr"], i - 1)
                normalise("b", i, u)

            def logit_copy(i, u):
                dve.wait_ge(S["b_gate"], i + 1)
                dve.tensor_copy(logits[:, ds(i * 4, 4), :],
                                ps_v[1 - u][1][:, :].rearrange("p (t e) -> p t e", t=4)[:, :, 0:E])\
                    .then_inc(S["b_logit"], 1)

            done = [0]

            def then(op):
                done[0] += 1
                op.then_inc(S["q_dve"], 1)
                dve.wait_ge(S["q_dve"], done[0])

            def by_tile(a):
                return a.rearrange("p (t e) -> p t e", e=E)

            def over_experts(a, n):
                return a.unsqueeze(2).to_broadcast([P, n, E])

            def top_two(t0, t1):
                n = t1 - t0

                def part(a):
                    return by_tile(a)[:, t0:t1]
                source = logits[:, t0:t1, :]
                for k in range(2):
                    then(dve.tensor_reduce(q_m[k][:, t0:t1], source, AX.X, ALU.max))
                    then(dve.tensor_tensor(part(q_eq), source, over_experts(q_m[k][:, t0:t1], n), ALU.is_equal))
                    then(dve.tensor_tensor(part(q_val), part(q_eq), part(q_rev), ALU.mult))
                    then(dve.tensor_reduce(q_c[:, t0:t1], part(q_val), AX.X, ALU.max))
                    then(dve.tensor_tensor(part(q_oh[k]), part(q_rev), over_experts(q_c[:, t0:t1], n), ALU.is_equal))
                    if k == 0:
                        then(dve.scalar_tensor_tensor(out=part(q_l2), in0=part(q_oh[0]), scalar=-3.0e38, in1=source,
                                                      op0=ALU.mult, op1=ALU.add))
                        source = part(q_l2)

            def phase_b(i, u):
                if not last(i, PAIRS):
                    filter_products(i + 1, 0)
                if not first(i):
                    residual(i - 1, 1 - u)
                if not last(i, PAIRS):
                    filter_products(i + 1, 1)
                else:
                    dve.wait_ge(S["q_iota"], 8 + BUFS)
                    dve.wait_ge(S["b_logit"], PAIRS - 3)
                    top_two(0, EARLY)
                if not first(i):
                    normalise_tokens(i - 1, 1 - u)
                if not isinstance(i, int) or 2 <= i < PAIRS - 1:
                    logit_copy(i - 2, u)
            filter_products(0, 0)
            filter_products(0, 1)
            spectrum_copy(PAIRS - 1)
            filter_loop(dve, phase_b)
            residual(PAIRS - 1, 1)
            logit_copy(PAIRS - 3, 1)
            normalise_tokens(PAIRS - 1, 1)
            for i in range(PAIRS - 2, PAIRS):
                logit_copy(i, i % 2)

            dve.memset(q_incl[:, 0:1], 0.0).then_inc(S["q_zero"], 1)
            dve.wait_ge(S["b_logit"], PAIRS)
            top_two(EARLY, TILES)
            dve.tensor_tensor(q_diff, q_m[1], q_m[0], ALU.subtract).then_inc(S["q_ready"], 1)
            dve.tensor_tensor(q_cnt.bitcast(F16)[:, 0:TILES * E], q_oh[0], q_oh[1], ALU.add).then_inc(S["q_ready"], 1)
            dve.wait_ge(S["q_count"], 2)
            dve.wait_ge(S["q_zero"], 1)
            then(dve.tensor_tensor_scan(q_incl[:, 1:], q_one, ps_tot[:, 0:E * TILES], 0.0, ALU.mult, ALU.add))
            starts, ends = q_incl[:, 0:E * TILES:TILES], q_incl[:, TILES::TILES]
            then(dve.scalar_tensor_tensor(out=q_e32[:, :], in0=ends, scalar=float(P - 1), in1=starts,
                                          op0=ALU.add, op1=ALU.subtract))
            then(dve.tensor_scalar(q_e32[:, :], q_e32[:, :], 7, 7, ALU.logical_shift_right, ALU.logical_shift_left))
            then(dve.tensor_copy(q_cpad, q_e32[:, :]))
            then(dve.tensor_tensor_scan(q_pend, q_one[:, 0:E], q_cpad, 0.0, ALU.mult, ALU.add))
            then(dve.tensor_tensor(q_base, q_pend, q_cpad, ALU.subtract))
            then(dve.tensor_tensor(q_base, q_base, starts, ALU.subtract))
            then(dve.tensor_tensor(q_slot, q_incl[:, 1:], ps_rank[:, 0:E * TILES], ALU.add))
            then(dve.tensor_tensor(q_slot.rearrange("p (e t) -> p e t", t=TILES),
                                   q_slot.rearrange("p (e t) -> p e t", t=TILES),
                                   q_base.unsqueeze(2).to_broadcast([P, E, TILES]), ALU.add))
            then(dve.tensor_tensor(q_sel.rearrange("p (k t e) -> p k t e", k=2, e=E),
                                   q_oh_both.rearrange("p (k t e) -> p k t e", k=2, e=E),
                                   q_slot.rearrange("p (e t) -> p t e", t=TILES).unsqueeze(1)
                                   .to_broadcast([P, 2, TILES, E]), ALU.mult))
            then(dve.tensor_reduce(q_pos, q_sel.rearrange("p (n e) -> p n e", e=E), AX.X, ALU.add))
            then(dve.tensor_copy(q_i32[:, :], q_pos))
            dve.tensor_scalar(q_slot_low[:, :], q_i32[:, :], P - 1, None, ALU.bitwise_and)
            then(dve.tensor_scalar(q_slot_high[:, :], q_i32[:, :], 7, None, ALU.logical_shift_right))
            dve.tensor_copy(q_low, q_slot_low[:, :])
            then(dve.tensor_copy(q_high, q_slot_high[:, :]))

            for g in range(GROUPS):
                u, cols = g % 2, slice(g * GCOLS, (g + 1) * GCOLS)
                wait_done(dve, S["q_oh_used"], g - 1)
                dve.tensor_tensor(oh_j[u], tile_row, q_high[:, cols].unsqueeze(1).to_broadcast(
                    [P, SLOT_TILES, GCOLS]), ALU.is_equal).then_inc(S["q_oh_tile"], 1)
                dve.tensor_tensor(oh_s[u], slot_row, q_low[:, cols].unsqueeze(1).to_broadcast(
                    [P, P, GCOLS]), ALU.is_equal)
                dve.wait_ge(S["q_oh_tile"], g + 1)
                dve.tensor_tensor(oh_id[u], oh_j[u], id_row.unsqueeze(1).to_broadcast(
                    [P, SLOT_TILES, GCOLS]), ALU.mult).then_inc(S["q_oh_ready"], 1)
            dve.wait_ge(S["q_exp_done"], 1)
            then(dve.tensor_scalar(q_den, q_exp, 1.0, None, ALU.add))
            then(dve.reciprocal(mix[:, 0, :], q_den))
            then(dve.tensor_tensor(mix[:, 1, :], q_exp, mix[:, 0, :], ALU.mult))
            dve.wait_ge(S["q_oh_used"], GROUPS)
            by_group = ps_idx[:, 0:GROUPS * SLOT_TILES]
            then(dve.scalar_tensor_tensor(out=q_ids, in0=by_group, scalar=0.0, in1=q_offset, op0=ALU.is_gt, op1=ALU.mult))
            then(dve.tensor_tensor(q_ids, q_ids, by_group, ALU.add))
            then(dve.tensor_reduce(q_v, q_ids.rearrange("p (g j) -> p j g", g=GROUPS), AX.X, ALU.add))
            then(dve.tensor_scalar(idx_scatter[:, :], q_v, -1.0, 0.0, ALU.add, ALU.max))
            then(dve.tensor_scalar(idx_gather[:, :], idx_scatter[:, :], NTOK - 1, None, ALU.bitwise_and))

            def gather_rows(j, b):
                dve.tensor_copy(idx_g[b // 4][:, :], idx_gather[:, ds(j, 4)]).then_inc(S["g_idx"], 4)

            def scatter_rows(j, b):
                for k in range(4):
                    wait_done(dve, S[f"y_out{b + k}"], (j - b) * (16 // BUFS))
                dve.tensor_copy(idx_s[b // 4][:, :], idx_scatter[:, ds(j, 4)]).then_inc(S["s_idx"], 4)

            def x_low(j, u):
                dve.wait_ge(S["f_xh"], j + 1)
                wait_done(dve, S["f_h"], j - 1)
                dve.tensor_tensor(xgt[u][1], p_x[:, 0:P], xgt[u][0].bitcast(F32), ALU.subtract).then_inc(S["f_xt"], 1)

            def y_copy(j, b):
                dve.wait_ge(S["f_y"], j + 1)
                wait_done(dve, S[f"y_out{b}"], (j - b) * (16 // BUFS))
                dve.tensor_copy(yo[b], p_y[:, 0:DIM]).then_inc(S["f_ys"], 1)

            def step(j, b):
                u = b % 2
                if not last(j, RUN_TILES):
                    x_low(j + 1, 1 - u)
                if not isinstance(j, int) or j >= 3:
                    y_copy(j - 3, (b - 3) % BUFS)
                if b % 4 == 2 and (not isinstance(j, int) or j + 6 < RUN_TILES):
                    gather_rows(j + 6, (b + 6) % BUFS)
                if b % 4 == 0:
                    scatter_rows(j, b)
                dve.wait_ge(S["f_silu"], j + 1)
                wait_done(dve, S["f_ht"], j - 1)
                dve.tensor_tensor(hid[u], silu[u], p_h3[u][:, 0:HID], ALU.mult).then_inc(S["f_act"], 1)
            gather_rows(0, 0)
            gather_rows(4, 4)
            then(dve.tensor_tensor(q_jcmp.rearrange("p (e j) -> p e j", e=E), q_jtok.rearrange("p (e j) -> p e j", e=E),
                                   q_pend.unsqueeze(2).to_broadcast([P, E, SLOT_TILES]), ALU.is_ge))
            then(dve.tensor_reduce(q_inv, q_jcmp.rearrange("p (e j) -> p j e", e=E), AX.X, ALU.add))
            then(dve.scalar_tensor_tensor(out=q_digit[0:1, :], in0=q_inv[0:1, :], scalar=float(E - 1),
                                          in1=q_power[0:1, :], op0=ALU.min, op1=ALU.mult))
            then(dve.tensor_reduce(q_wordf[0:1, :], q_digit[0:1, :].rearrange("p (n b) -> p n b", b=BUFS),
                                   AX.X, ALU.add))
            words = SLOT_TILES // BUFS
            then(dve.tensor_copy(q_word[0:1, :], q_wordf[0:1, :]))
            dve.tensor_copy(tile_experts[0:1, 0:1], q_word[0:1, 0:1])
            then(dve.tensor_scalar(tile_experts[0:1, 1:words], q_word[0:1, 0:words - 1], 3 * (BUFS - 2), 3 * BUFS,
                                   ALU.logical_shift_right, ALU.logical_shift_left))
            dve.tensor_tensor(tile_experts[0:1, 1:words], tile_experts[0:1, 1:words], q_word[0:1, 1:words],
                              ALU.bitwise_or).then_inc(S["q_tables"], 1)
            then(dve.tensor_scalar(q_inv, q_v, 0.0, None, ALU.is_equal))
            then(dve.tensor_tensor(q_inv, q_inv, q_trash, ALU.mult))
            then(dve.tensor_tensor(q_v, q_v, q_inv, ALU.add))
            then(dve.tensor_scalar(idx_scatter[:, :], q_v, -1.0, None, ALU.add))
            x_low(0, 0)
            tile_loop(dve, step)
            for j in range(RUN_TILES - 3, RUN_TILES):
                y_copy(j, j % BUFS)

            for i in range(PAIRS):
                dve.wait_ge(S[f"c_in{i}"], 32)
                dve.wait_ge(S["c_sum"], i + 1)
                for t in range(4):
                    tile = T[:, 4 * i + t, :]
                    op = dve.scalar_tensor_tensor(out=tile, in0=yb[i][:, t * DIM:(t + 1) * DIM],
                                                  scalar=mix[:, 1, 4 * i + t:4 * i + t + 1], in1=tile,
                                                  op0=ALU.mult, op1=ALU.add)
                op.then_inc(S["c_done"], 1)


def layouts(x, L0_conv_w_pw1, L0_conv_w_pw2, L0_conv_star_scale, L0_conv_star_bias, L0_conv_rw_fc1_w,
            L0_conv_rw_fc1_b, L0_conv_rw_conv_w, L0_conv_rw_conv_b, L0_conv_rw_fc2_w, L0_conv_rw_fc2_b,
            L0_conv_sp_fc1_w, L0_conv_sp_fc1_b, L0_conv_sp_fc2_w, L0_conv_sp_fc2_b, L0_conv_complex_weights,
            L0_conv_spatial_weights, L0_ffn_gate_w, L0_ffn_w1, L0_ffn_w3, L0_ffn_w2):
    c = np.ascontiguousarray
    forward, inverse, sel = fourier_tables()
    cw = L0_conv_complex_weights.reshape(SIZE * FS, NF, 2)
    route_b = np.stack([L0_conv_sp_fc2_b.reshape(NF, 2, P), L0_conv_rw_fc2_b.reshape(NF, 2, P)])
    return {
        "x": c(x.transpose(0, 2, 3, 1).reshape(PAIRS, 4, P, DIM).transpose(0, 2, 1, 3).reshape(NTOK, DIM)),
        "ident": np.eye(P, dtype=np.float32),
        "fwd": c(forward), "inv": c(inverse),
        "sel_a": c(sel[:P].reshape(P, 2, 4 * P)), "sel_b": c(sel[P:].reshape(SIZE * FS - P, 2, 4 * P)),
        "sp1": c(L0_conv_sp_fc1_w.transpose(1, 2, 3, 0).reshape(DIM, TAPS, HALF)),
        "rw1": c(L0_conv_rw_fc1_w[:, :, 0, 0].T),
        "rwc": c(L0_conv_rw_conv_w[:, :, 0, 0].T),
        "route1_b": c(np.tile(np.stack([L0_conv_sp_fc1_b, L0_conv_rw_fc1_b, L0_conv_rw_conv_b], axis=1), (2, 1))),
        "route_b": c(route_b.transpose(3, 0, 1, 2).reshape(P, 16)),
        "sp2_even": c(L0_conv_sp_fc2_w.transpose(1, 2, 3, 0).reshape(HALF, TAPS, NF * MED)[:, 0::2]),
        "sp2_odd": c(L0_conv_sp_fc2_w.transpose(1, 2, 3, 0).reshape(HALF, TAPS, NF * MED)[:, 1::2]),
        "rw2": c(L0_conv_rw_fc2_w[:, :, 0, 0].T),
        "wp1": c(L0_conv_w_pw1.T),
        "wp2": c(L0_conv_w_pw2.T.reshape(2, P, DIM).transpose(1, 0, 2)),
        "star_sb": np.concatenate([L0_conv_star_scale, L0_conv_star_bias]),
        "gate": c(L0_ffn_gate_w.T),
        "cw_a": c(cw[:P]), "cw_b": c(cw[P:]),
        "sw_rows": c(L0_conv_spatial_weights.reshape(PIX, NF).T),
        "w1": c(L0_ffn_w1.transpose(2, 0, 1).reshape(DIM, E * HID)),
        "w3": c(L0_ffn_w3.transpose(2, 0, 1).reshape(DIM, E * HID)),
        "w2": c(L0_ffn_w2.reshape(E, DIM, HC, P).transpose(3, 2, 0, 1).reshape(P, HC, E * DIM)),
    }


def kernel(**inputs):
    import concourse.bacc as bacc
    from concourse.bass_utils import run_bass_kernel_spmd

    arrays = layouts(**{k: np.asarray(a) for k, a in inputs.items()})
    nc = bacc.Bacc("TRN2", target_bir_lowering=False, num_devices=1)
    io = {k: nc.dram_tensor(f"in_{k}", a.shape, mybir.dt.from_np(a.dtype), kind="ExternalInput").ap()
          for k, a in arrays.items()}
    io["out"] = nc.dram_tensor("out", (NTOK, DIM), F32, kind="ExternalOutput").ap()
    metaformer(nc, io)
    r = run_bass_kernel_spmd(nc, [{f"in_{k}": a for k, a in arrays.items()}], core_ids=[0])
    out = r.results[0]["out"].reshape(PAIRS, P, 4, DIM).transpose(0, 2, 1, 3)
    return np.ascontiguousarray(out.reshape(BATCH, SIZE, SIZE, DIM).transpose(0, 3, 1, 2))
```
